# Optimizing a Trainium2 kernel written in Bass

```python
import numpy as np
import jax
import jax.numpy as jnp

def _softmax(x, axis=-1):
    return jax.nn.softmax(x, axis=axis)

def _gelu(x):
    return jax.nn.gelu(x, approximate=True)

def _silu(x):
    return jax.nn.silu(x)

def _sigmoid(x):
    return jax.nn.sigmoid(x)

def _layernorm(x, axis=-1, eps=1e-05):
    m = jnp.mean(x, axis=axis, keepdims=True)
    v = jnp.var(x, axis=axis, keepdims=True)
    return (x - m) / jnp.sqrt(v + eps)

def _scatter_add(tgt, idx, src, axis=0):
    return tgt.at[idx].add(src)

def _segment_sum(src, seg, n):
    return jax.ops.segment_sum(src, seg, n)
kernel_name = 'mk_xattn_seq_d4_seqx_r8_174801'

def setup_inputs(seed: int=0):
    np.random.seed(seed)
    _w = jnp.asarray

    def _rec_inputs():
        import jax
        import jax.numpy as jnp
        _rk = jax.random.key(seed)
        x = -0.0002928 + 1 * jax.random.normal(jax.random.fold_in(_rk, 1), (16, 256, 128), jnp.float32)
        _lenS = 256 - jax.random.randint(jax.random.fold_in(_rk, 7), (16,), 0, max(1, 256 // 4) + 1, jnp.int32)
        _lenS2 = 64 - jax.random.randint(jax.random.fold_in(_rk, 8), (16,), 0, max(1, 64 // 4) + 1, jnp.int32)
        _ctx_1024P = jax.random.normal(jax.random.fold_in(_rk, 11), (16, 16, 128), jnp.float32)
        _ctx_1024c = jax.random.dirichlet(jax.random.fold_in(_rk, 511), 0.3 * jnp.ones((16,), jnp.float32), (16, 64))
        _ctx_1024t = jnp.einsum('bsk,bkd->bsd', _ctx_1024c, _ctx_1024P)
        _ctx_1024t = _ctx_1024t * jax.lax.rsqrt(jnp.mean(jnp.square(_ctx_1024t)) + 1e-12) * 0.953939
        ctx_1024 = -1.39393e-06 + 0.999914 * (_ctx_1024t + 0.3 * jax.random.normal(jax.random.fold_in(_rk, 611), (16, 64, 128), jnp.float32))
        _validS = jnp.arange(256)[None, :] < _lenS[:, None]
        _validS2 = jnp.arange(64)[None, :] < _lenS2[:, None]
        _causal = jnp.tril(jnp.ones((256, 256), dtype=bool))
        mask_Bx1x1xS2_if1 = jnp.where(jnp.ones((16, 1, 1, 64), dtype=bool), 1, 0).astype(jnp.int32)
        return (x, ctx_1024, mask_Bx1x1xS2_if1)
    x, ctx_1024, mask_Bx1x1xS2_if1 = _rec_inputs()

    def _L0_xattn_setup():
        import jax, jax.numpy as jnp
        import numpy as np
        B, Q, KV = (2, 256, 256)
        D_MODEL = 128
        N_HEADS = 16
        D_KV = 64
        EPS = 1e-06
        key = jax.random.key(seed)
        ks = jax.random.split(key, 7)
        s = 0.02
        return {'hidden_states': jax.random.normal(ks[0], (B, Q, D_MODEL), jnp.float32), 'key_value_states': jax.random.normal(ks[1], (B, KV, D_MODEL), jnp.float32), 'wq': jax.random.normal(ks[2], (D_MODEL, N_HEADS * D_KV), jnp.float32) * s, 'wk': jax.random.normal(ks[3], (D_MODEL, N_HEADS * D_KV), jnp.float32) * s, 'wv': jax.random.normal(ks[4], (D_MODEL, N_HEADS * D_KV), jnp.float32) * s, 'wo': jax.random.normal(ks[5], (N_HEADS * D_KV, D_MODEL), jnp.float32) * s, 'norm_w': jnp.ones((D_MODEL,), jnp.float32)}
    _L0_xattn_all = _L0_xattn_setup()
    _L0_xattn_in = {k: v for k, v in _L0_xattn_all.items() if k in ('wq', 'wk', 'wv', 'wo', 'norm_w')}
    del _L0_xattn_all

    def _L1_xattn_setup():
        import jax, jax.numpy as jnp
        import numpy as np
        B, S, D_MODEL, H, D_FF = (2, 256, 128, 16, 512)
        D_HEAD = D_MODEL // H
        LN_EPS = 1e-05

        def _xavier(key, shape):
            fan_out, fan_in = shape
            std = (2.0 / (fan_in + fan_out)) ** 0.5
            return jax.random.normal(key, shape, dtype=jnp.float32) * std

        def _layer_norm(x, g, b):
            mu = jnp.mean(x, axis=-1, keepdims=True)
            var = jnp.mean((x - mu) ** 2, axis=-1, keepdims=True)
            return (x - mu) * jax.lax.rsqrt(var + LN_EPS) * g + b
        key = jax.random.key(seed)
        ks = jax.random.split(key, 8)
        return {'q': jax.random.normal(ks[0], (B, S, D_MODEL), dtype=jnp.float32), 'k': jax.random.normal(ks[1], (B, S, D_MODEL), dtype=jnp.float32), 'Wq': _xavier(ks[2], (D_MODEL, D_MODEL)), 'bq': jnp.zeros((D_MODEL,), jnp.float32), 'Wk': _xavier(ks[3], (D_MODEL, D_MODEL)), 'bk': jnp.zeros((D_MODEL,), jnp.float32), 'Wv': _xavier(ks[4], (D_MODEL, D_MODEL)), 'bv': jnp.zeros((D_MODEL,), jnp.float32), 'W1': _xavier(ks[5], (D_FF, D_MODEL)), 'b1': jnp.zeros((D_FF,), jnp.float32), 'W2': _xavier(ks[6], (D_MODEL, D_FF)), 'b2': jnp.zeros((D_MODEL,), jnp.float32), 'ln_g': jnp.ones((D_MODEL,), jnp.float32), 'ln_b': jnp.zeros((D_MODEL,), jnp.float32), 'use_causal_mask': 1}
    _L1_xattn_all = _L1_xattn_setup()
    _L1_xattn_in = {k: v for k, v in _L1_xattn_all.items() if k in ('Wq', 'bq', 'Wk', 'bk', 'Wv', 'bv', 'W1', 'b1', 'W2', 'b2', 'ln_g', 'ln_b')}
    del _L1_xattn_all

    def _L2_xattn_setup():
        import jax, jax.numpy as jnp
        import numpy as np
        B, S, F = (4, 256, 128)
        key = jax.random.key(seed)
        ks = jax.random.split(key, 9)
        s = 1.0 / np.sqrt(F)
        return {'q': jax.random.normal(ks[0], (B, S, F), jnp.float32), 'k': jax.random.normal(ks[1], (B, S, F), jnp.float32), 'v': jax.random.normal(ks[2], (B, S, F), jnp.float32), 'Wq': jax.random.normal(ks[3], (F, F), jnp.float32) * s, 'bq': jax.random.normal(ks[4], (F,), jnp.float32) * s, 'Wk': jax.random.normal(ks[5], (F, F), jnp.float32) * s, 'bk': jax.random.normal(ks[6], (F,), jnp.float32) * s, 'Wv': jax.random.normal(ks[7], (F, F), jnp.float32) * s, 'bv': jax.random.normal(ks[8], (F,), jnp.float32) * s}
    _L2_xattn_all = _L2_xattn_setup()
    _L2_xattn_in = {k: v for k, v in _L2_xattn_all.items() if k in ('Wq', 'bq', 'Wk', 'bk', 'Wv', 'bv')}
    del _L2_xattn_all

    def _L3_xattn_setup():
        import jax, jax.numpy as jnp
        import numpy as np
        EMBED = 128
        HEADS = 16
        HEAD_DIM = EMBED // HEADS
        FF = 4 * EMBED
        EPS = 1e-05

        def layernorm(x, g, b):
            mu = jnp.mean(x, axis=-1, keepdims=True)
            var = jnp.mean((x - mu) ** 2, axis=-1, keepdims=True)
            return (x - mu) * jax.lax.rsqrt(var + EPS) * g + b
        key = jax.random.key(seed)
        ks = jax.random.split(key, 16)
        B, S = (2, 256)
        f32 = jnp.float32
        inp = {'value': jax.random.normal(ks[0], (B, S, EMBED), f32), 'key': jax.random.normal(ks[1], (B, S, EMBED), f32), 'query': jax.random.normal(ks[2], (B, S, EMBED), f32), 'mask': jnp.ones((B, 1, 1, S), jnp.int32), 'wv': jax.random.normal(ks[3], (HEAD_DIM, HEAD_DIM), f32) * 0.02, 'wk': jax.random.normal(ks[4], (HEAD_DIM, HEAD_DIM), f32) * 0.02, 'wq': jax.random.normal(ks[5], (HEAD_DIM, HEAD_DIM), f32) * 0.02, 'w_out': jax.random.normal(ks[6], (EMBED, EMBED), f32) * 0.02, 'b_out': jnp.zeros((EMBED,), f32), 'g1': jnp.ones((EMBED,), f32), 'beta1': jnp.zeros((EMBED,), f32), 'w_ff1': jax.random.normal(ks[7], (EMBED, FF), f32) * 0.02, 'b_ff1': jnp.zeros((FF,), f32), 'w_ff2': jax.random.normal(ks[8], (FF, EMBED), f32) * 0.02, 'b_ff2': jnp.zeros((EMBED,), f32), 'g2': jnp.ones((EMBED,), f32), 'beta2': jnp.zeros((EMBED,), f32)}
        return inp
    _L3_xattn_all = _L3_xattn_setup()
    _L3_xattn_in = {k: v for k, v in _L3_xattn_all.items() if k in ('wv', 'wk', 'wq', 'w_out', 'b_out', 'g1', 'beta1', 'w_ff1', 'b_ff1', 'w_ff2', 'b_ff2', 'g2', 'beta2')}
    del _L3_xattn_all
    return {'x': x, 'ctx_1024': ctx_1024, 'mask_Bx1x1xS2_if1': mask_Bx1x1xS2_if1, 'L0_xattn_wq': _L0_xattn_in['wq'], 'L0_xattn_wk': _L0_xattn_in['wk'], 'L0_xattn_wv': _L0_xattn_in['wv'], 'L0_xattn_wo': _L0_xattn_in['wo'], 'L0_xattn_norm_w': _L0_xattn_in['norm_w'], 'L1_xattn_Wq': _L1_xattn_in['Wq'], 'L1_xattn_bq': _L1_xattn_in['bq'], 'L1_xattn_Wk': _L1_xattn_in['Wk'], 'L1_xattn_bk': _L1_xattn_in['bk'], 'L1_xattn_Wv': _L1_xattn_in['Wv'], 'L1_xattn_bv': _L1_xattn_in['bv'], 'L1_xattn_W1': _L1_xattn_in['W1'], 'L1_xattn_b1': _L1_xattn_in['b1'], 'L1_xattn_W2': _L1_xattn_in['W2'], 'L1_xattn_b2': _L1_xattn_in['b2'], 'L1_xattn_ln_g': _L1_xattn_in['ln_g'], 'L1_xattn_ln_b': _L1_xattn_in['ln_b'], 'L2_xattn_Wq': _L2_xattn_in['Wq'], 'L2_xattn_bq': _L2_xattn_in['bq'], 'L2_xattn_Wk': _L2_xattn_in['Wk'], 'L2_xattn_bk': _L2_xattn_in['bk'], 'L2_xattn_Wv': _L2_xattn_in['Wv'], 'L2_xattn_bv': _L2_xattn_in['bv'], 'L3_xattn_wv': _L3_xattn_in['wv'], 'L3_xattn_wk': _L3_xattn_in['wk'], 'L3_xattn_wq': _L3_xattn_in['wq'], 'L3_xattn_w_out': _L3_xattn_in['w_out'], 'L3_xattn_b_out': _L3_xattn_in['b_out'], 'L3_xattn_g1': _L3_xattn_in['g1'], 'L3_xattn_beta1': _L3_xattn_in['beta1'], 'L3_xattn_w_ff1': _L3_xattn_in['w_ff1'], 'L3_xattn_b_ff1': _L3_xattn_in['b_ff1'], 'L3_xattn_w_ff2': _L3_xattn_in['w_ff2'], 'L3_xattn_b_ff2': _L3_xattn_in['b_ff2'], 'L3_xattn_g2': _L3_xattn_in['g2'], 'L3_xattn_beta2': _L3_xattn_in['beta2']}

def reference(x, ctx_1024, mask_Bx1x1xS2_if1, L0_xattn_wq, L0_xattn_wk, L0_xattn_wv, L0_xattn_wo, L0_xattn_norm_w, L1_xattn_Wq, L1_xattn_bq, L1_xattn_Wk, L1_xattn_bk, L1_xattn_Wv, L1_xattn_bv, L1_xattn_W1, L1_xattn_b1, L1_xattn_W2, L1_xattn_b2, L1_xattn_ln_g, L1_xattn_ln_b, L2_xattn_Wq, L2_xattn_bq, L2_xattn_Wk, L2_xattn_bk, L2_xattn_Wv, L2_xattn_bv, L3_xattn_wv, L3_xattn_wk, L3_xattn_wq, L3_xattn_w_out, L3_xattn_b_out, L3_xattn_g1, L3_xattn_beta1, L3_xattn_w_ff1, L3_xattn_b_ff1, L3_xattn_w_ff2, L3_xattn_b_ff2, L3_xattn_g2, L3_xattn_beta2):
    import jax
    import jax.numpy as jnp

    def _L0_xattn_ref(hidden_states, key_value_states, wq, wk, wv, wo, norm_w):
        import jax, jax.numpy as jnp
        import numpy as np
        B, Q, KV = (2, 256, 256)
        D_MODEL = 128
        N_HEADS = 16
        D_KV = 64
        EPS = 1e-06
        var = jnp.mean(jnp.square(hidden_states), axis=-1, keepdims=True)
        normed = hidden_states * jax.lax.rsqrt(var + EPS) * norm_w
        b, q_len, _ = hidden_states.shape
        kv_len = key_value_states.shape[1]

        def split_heads(x):
            return x.reshape(b, -1, N_HEADS, D_KV).transpose(0, 2, 1, 3)
        q = split_heads(normed @ wq)
        k = split_heads(key_value_states @ wk)
        v = split_heads(key_value_states @ wv)
        scores = jnp.einsum('bhqd,bhkd->bhqk', q, k)
        attn = jax.nn.softmax(scores.astype(jnp.float32), axis=-1).astype(scores.dtype)
        ctx = jnp.einsum('bhqk,bhkd->bhqd', attn, v)
        ctx = ctx.transpose(0, 2, 1, 3).reshape(b, q_len, N_HEADS * D_KV)
        attn_out = ctx @ wo
        return hidden_states + attn_out

    def _L1_xattn_ref(q, k, Wq, bq, Wk, bk, Wv, bv, W1, b1, W2, b2, ln_g, ln_b, use_causal_mask):
        import jax, jax.numpy as jnp
        import numpy as np
        B, S, D_MODEL, H, D_FF = (2, 256, 128, 16, 512)
        D_HEAD = D_MODEL // H
        LN_EPS = 1e-05

        def _xavier(key, shape):
            fan_out, fan_in = shape
            std = (2.0 / (fan_in + fan_out)) ** 0.5
            return jax.random.normal(key, shape, dtype=jnp.float32) * std

        def _layer_norm(x, g, b):
            mu = jnp.mean(x, axis=-1, keepdims=True)
            var = jnp.mean((x - mu) ** 2, axis=-1, keepdims=True)
            return (x - mu) * jax.lax.rsqrt(var + LN_EPS) * g + b
        Bq, Sq, _ = q.shape
        Sk = k.shape[1]
        Q = q @ Wq.T + bq
        K = k @ Wk.T + bk
        V = k @ Wv.T + bv
        Q_ = Q.reshape(Bq, Sq, H, D_HEAD).transpose(0, 2, 1, 3)
        K_ = K.reshape(Bq, Sk, H, D_HEAD).transpose(0, 2, 1, 3)
        V_ = V.reshape(Bq, Sk, H, D_HEAD).transpose(0, 2, 1, 3)
        scores = jnp.einsum('bhqd,bhkd->bhqk', Q_, K_) / D_HEAD ** 0.5
        if use_causal_mask:
            causal = jnp.tril(jnp.ones((Sq, Sk), dtype=bool))
            scores = jnp.where(causal, scores, jnp.float32(-1000000000.0))
        sim = jax.nn.softmax(scores, axis=-1)
        att = jnp.einsum('bhqk,bhkd->bhqd', sim, V_)
        att_h = att.transpose(0, 2, 1, 3).reshape(Bq, Sq, D_MODEL)
        att_h = att_h + q
        att_h = _layer_norm(att_h, ln_g, ln_b)
        ff = jax.nn.gelu(att_h @ W1.T + b1, approximate=False) @ W2.T + b2
        return ff + att_h

    def _L2_xattn_ref(q, k, v, Wq, bq, Wk, bk, Wv, bv):
        import jax, jax.numpy as jnp
        import numpy as np
        B, S, F = (4, 256, 128)
        qp = jnp.einsum('bsf,gf->bsg', q, Wq) + bq
        kp = jnp.einsum('bsf,gf->bsg', k, Wk) + bk
        vp = jnp.einsum('bsf,gf->bsg', v, Wv) + bv
        attn = jax.nn.softmax(jnp.einsum('bqf,bkf->bqk', qp, kp), axis=-1)
        return jnp.einsum('bqk,bkf->bqf', attn, vp) + q

    def _L3_xattn_ref(value, key, query, mask, wv, wk, wq, w_out, b_out, g1, beta1, w_ff1, b_ff1, w_ff2, b_ff2, g2, beta2):
        import jax, jax.numpy as jnp
        import numpy as np
        EMBED = 128
        HEADS = 16
        HEAD_DIM = EMBED // HEADS
        FF = 4 * EMBED
        EPS = 1e-05

        def layernorm(x, g, b):
            mu = jnp.mean(x, axis=-1, keepdims=True)
            var = jnp.mean((x - mu) ** 2, axis=-1, keepdims=True)
            return (x - mu) * jax.lax.rsqrt(var + EPS) * g + b
        B, S, E = query.shape
        v = value.reshape(B, -1, HEADS, HEAD_DIM) @ wv
        k = key.reshape(B, -1, HEADS, HEAD_DIM) @ wk
        q = query.reshape(B, -1, HEADS, HEAD_DIM) @ wq
        scores = jnp.einsum('bqhd,bkhd->bhqk', q, k)
        scores = jnp.where(mask == 0, jnp.float32(-1e+20), scores)
        attn = jax.nn.softmax(scores / jnp.sqrt(jnp.float32(EMBED)), axis=-1)
        out = jnp.einsum('bhqk,bkhd->bqhd', attn, v).reshape(B, S, E)
        attention = out @ w_out + b_out
        x = layernorm(attention + query, g1, beta1)
        ff = jax.nn.relu(x @ w_ff1 + b_ff1) @ w_ff2 + b_ff2
        return layernorm(ff + x, g2, beta2)
    x = _L0_xattn_ref(x, ctx_1024, L0_xattn_wq, L0_xattn_wk, L0_xattn_wv, L0_xattn_wo, L0_xattn_norm_w)
    x = _L1_xattn_ref(x, ctx_1024, L1_xattn_Wq, L1_xattn_bq, L1_xattn_Wk, L1_xattn_bk, L1_xattn_Wv, L1_xattn_bv, L1_xattn_W1, L1_xattn_b1, L1_xattn_W2, L1_xattn_b2, L1_xattn_ln_g, L1_xattn_ln_b, 1)
    x = _L2_xattn_ref(x, ctx_1024, ctx_1024, L2_xattn_Wq, L2_xattn_bq, L2_xattn_Wk, L2_xattn_bk, L2_xattn_Wv, L2_xattn_bv)
    x = _L3_xattn_ref(ctx_1024, ctx_1024, x, mask_Bx1x1xS2_if1, L3_xattn_wv, L3_xattn_wk, L3_xattn_wq, L3_xattn_w_out, L3_xattn_b_out, L3_xattn_g1, L3_xattn_beta1, L3_xattn_w_ff1, L3_xattn_b_ff1, L3_xattn_w_ff2, L3_xattn_b_ff2, L3_xattn_g2, L3_xattn_beta2)
    return x

_drawn_inputs = setup_inputs


def setup_inputs(seed=0):
    import zlib

    import numpy as np

    out = dict(_drawn_inputs(seed))
    spreads = {'L0_xattn_norm_w': (1.0, 0.6),
     'L1_xattn_bq': (0.0, 0.1),
     'L1_xattn_bk': (0.0, 2.0),
     'L1_xattn_bv': (0.0, 0.1),
     'L1_xattn_b1': (0.0, 0.1),
     'L1_xattn_b2': (0.0, 0.1),
     'L1_xattn_ln_g': (1.0, 0.2),
     'L1_xattn_ln_b': (0.0, 0.1),
     'L3_xattn_b_out': (0.0, 0.1),
     'L3_xattn_g1': (1.0, 0.2),
     'L3_xattn_beta1': (0.0, 0.1),
     'L3_xattn_b_ff1': (0.0, 0.271),
     'L3_xattn_b_ff2': (0.0, 0.1),
     'L3_xattn_g2': (1.0, 0.2),
     'L3_xattn_beta2': (0.0, 0.1)}
    factors = {'L0_xattn_wq': 2.717,
     'L2_xattn_bk': 64.0,
     'L3_xattn_wv': 8.0,
     'L3_xattn_wk': 37.474,
     'L3_xattn_wq': 35.162,
     'L3_xattn_w_out': 8.0}
    for name, (base, spread) in spreads.items():
        noise = np.random.default_rng([zlib.crc32(name.encode()), seed]).standard_normal(out[name].shape)
        drawn = base * np.exp(spread * noise) if base else spread * noise
        out[name] = jnp.asarray(drawn.astype(out[name].dtype))
    for name, factor in factors.items():
        out[name] = (out[name] * factor).astype(out[name].dtype)
    return out
```

```python
import concourse.bass as bass
from concourse import mybir
from contextlib import ExitStack

BATCH, QL, D = 16, 256, 128
KL = 64
HEADS = 16
DKV = 64
DH = D // HEADS
FF = 512
P = 128
TILES = QL // P
G = 2
TURNS = BATCH // G
PAIRS = HEADS // 2
CHUNKS_FF = FF // P
STACKS = 4
RMS_EPS, LN_EPS = 1e-6, 1e-5
CAUSAL_FILL, MASK_FILL = -1e9, -1e20
SCALE1 = DH ** -0.5
SCALE3 = D ** -0.5

BANKS_BIG, BIG = 3, 1024
BANKS_SMALL, SMALL = 2, 512

ROWS = ["bq1", "bk1", "bv1", "b2_1", "ln_g", "ln_b", "bv2", "b_out", "g1", "beta1", "b_ff2", "g2", "beta2"]
COLS = ["norm_w", "bk2", "bq2", "b1_0", "b1_1", "b1_2", "b1_3", "bff1_0", "bff1_1", "bff1_2", "bff1_3"]

PROLOGUE = [
    ("rows0", 0, 0, "big"), ("rows1", 0, 0, "big"), ("cols", 0, 0, "small"), ("l3_small_t", 0, 0, "small"),
    ("wkT", 0, 0, "big"), ("wqT", 0, 0, "big"), ("l3_b", 0, 0, "small"), ("l3_rep", 0, 0, "small"),
    ("wvT", 0, 0, "big"), ("wqk", 0, 0, "big"), ("wqk", 0, 1, "big"), ("l3_full", 0, 0, "small"),
    ("wvo", 0, 0, "big"), ("wvo", 0, 1, "big"), ("l1_wT", 0, 0, "big"), ("l12_w", 0, 0, "big"),
]


def turn_bursts():
    b = [("ctxT", 0, 0, "small"), ("fold_k", 0, 0, "big"), ("fold_k", 0, 1, "big"),
         ("ctx_k", 0, 0, "small"), ("ctx_v", 0, 0, "small"),
         ("xnT", 0, 0, "small"), ("xnT", 1, 0, "small"),
         ("fold_v", 0, 0, "big"), ("fold_v", 1, 0, "big"), ("stack_k", 0, 0, "big")]
    b += [("s0", 0, 0, "big"), ("s0", 0, 1, "big"), ("s0", 1, 0, "big"),
          ("max0", 0, 0, "small"), ("sub0", 0, 0, "more s0"), ("sub0", 0, 1, "more s0"),
          ("s0", 1, 1, "big"),
          ("max0", 1, 0, "small"), ("sub0", 1, 0, "more s0"), ("sub0", 1, 1, "more s0")]
    for g in range(G):
        b += [("p0T", g, 0, "big"), ("p0T", g, 1, "big"), ("o0", g, 0, "small")]
    b += [(n, g, 0, r) for n, r in (("x1T", "small"), ("q1", "small"), ("q1T", "big")) for g in range(G)]
    for l in "13":
        if l == "3":
            b += [(n, g, 0, "big" if n == "o2" else "small") for n in ("x2T", "s2", "p2T", "o2") for g in range(G)]
            b += [("q3T", g, 0, "big") for g in range(G)]
        b += [("s" + l, g, t, "big") for g in range(G) for t in range(TILES)]
        b += [("max" + l, g, 0, "small") for g in range(G)]
        b += [("st" + l, 0, 0, "big"), ("st" + l, 0, 1, "big"), ("st" + l, 1, 0, "big"),
              ("pv" + l, 0, 0, "small"), ("st" + l, 1, 1, "big"), ("pv" + l, 1, 0, "small")]
        b += [("at" + l, g, 0, "small") for g in range(G)]
        if l == "3":
            b += [(n, g, 0, "small") for n in ("a3T", "w3") for g in range(G)]
        b += [("y%sT" % l, g, 0, "small") for g in range(G)]
        b += [("h" + l, g, 0, "big") for g in range(G)]
        b += [("f" + l, g, 0, "small") for g in range(G)]
    return b


class Burst:

    def __init__(self, region, writes, drains):
        self.region, self.writes, self.drains = region, writes, drains
        self.per_turn = (0, 0)

    def is_written(self, i=0):
        return i * self.per_turn[0] + self.writes

    def is_free(self, i=0):
        return i * self.per_turn[1] + self.drains

    def is_drained(self, i=0):
        return self.is_free(i) + 1


def place(order, writes, drains):
    at, first, used = {}, (dict(writes), dict(drains)), {"big": 0, "small": 0}
    for name, g, part, ring in order:
        if ring.startswith("more"):
            region = at[(ring.split()[1], g, part)].region
            before = at[(ring.split()[1], g, part)].drains
        else:
            count = BANKS_BIG if ring == "big" else BANKS_SMALL
            region = (ring, used[ring] % count)
            used[ring] += 1
            before = drains[region]
            drains[region] += 1
        writes[region] += 1
        at[(name, g, part)] = Burst(region, writes[region], before)
    for b in at.values():
        b.per_turn = (writes[b.region] - first[0][b.region], drains[b.region] - first[1][b.region])
    return at


def build(nc, I, out):
    f32, f32r, bf16, i32 = mybir.dt.float32, mybir.dt.float32r, mybir.dt.bfloat16, mybir.dt.int32
    ACT, ALU, AX = mybir.ActivationFunctionType, mybir.AluOpType, mybir.AxisListType
    ctx = ExitStack()
    with ctx:
        def sb(name, shape, dt=f32):
            return ctx.enter_context(nc.sbuf_tensor(name, shape, dt))

        def sem(name):
            return ctx.enter_context(nc.semaphore(name))

        regions = [("big", n) for n in range(BANKS_BIG)] + [("small", n) for n in range(BANKS_SMALL)]
        psum = {r: ctx.enter_context(nc.psum_tensor("ps_%s%d" % r, [P, BIG if r[0] == "big" else SMALL], f32))
                for r in regions}
        written = {r: sem("written_%s%d" % r) for r in regions}
        drained = {r: sem("drained_%s%d" % r) for r in regions}
        writes, drains = {r: 0 for r in regions}, {r: 0 for r in regions}
        pro = place(PROLOGUE, writes, drains)
        body = place(turn_bursts(), writes, drains)

        early = sb("early", [P, 7 * HEADS * DKV])
        wq0, wk0, wv0 = (early[:, n * HEADS * DKV:(n + 1) * HEADS * DKV] for n in range(3))
        wo0, wkT, wqT, wvT = (early[:, n * HEADS * DKV:(n + 1) * HEADS * DKV].rearrange("p (c n) -> p c n", n=D)
                              for n in range(3, 7))
        wq1, wk1, wv1, w2_1 = sb("wq1", [P, D]), sb("wk1", [P, D]), sb("wv1", [P, D]), sb("w2_1", [P, FF])
        w1_1 = sb("w1_1", [P, CHUNKS_FF, D])
        wq2, wk2, wv2 = (sb(n, [P, D]) for n in ("wq2", "wk2", "wv2"))
        w8 = sb("w8", [DH, 3, DH])
        w_out, w_ff1, w_ff2 = sb("w_out", [P, D]), sb("w_ff1", [P, FF]), sb("w_ff2", [P, CHUNKS_FF, D])
        wqk = sb("wqk", [P, HEADS, D])
        wvo = sb("wvo", [P, 2, PAIRS, D])
        l1_wT = sb("l1_wT", [P, 3, D])
        w1T = sb("w1T", [P, CHUNKS_FF, P])
        w2T = sb("w2T", [P, CHUNKS_FF, D])
        wv2T, wqk2 = sb("wv2T", [P, D]), sb("wqk2", [P, D])
        c2 = sb("c2", [P, 3])
        w8T = sb("w8T", [DH, 3, DH])
        b8 = sb("b8", [DH, DH])
        rep8 = sb("rep8", [DH, 2, D])
        l3_full = sb("l3_full", [P, 2, D])
        bc = sb("bc", [P, len(ROWS), D])
        cols = sb("cols", [P, len(COLS)])

        def row(name):
            return bc[:, ROWS.index(name), :]

        def col(name):
            n = COLS.index(name)
            return cols[:, n:n + 1]

        ident = sb("ident", [P, P])
        ident_bf = sb("ident_bf", [P, P], bf16)
        ones_row = sb("ones_row", [1, P])
        rep_id = sb("rep_id", [DH, HEADS, DH])
        head_of = sb("head_of", [P, HEADS])
        stack_head = sb("stack_head", [P, STACKS])
        stack_head3 = sb("stack_head3", [P, STACKS])
        spread = sb("spread", [2 * HEADS, HEADS, KL], f32r)
        causal = sb("causal", [KL, 2, KL], bf16)
        half_power = sb("half_power", [P, 2])

        x_in = sb("x_in", [P, G, TILES, D])
        c_in = sb("c_in", [P, D])
        m_in = sb("m_in", [P, 1], i32)
        m01, pen = sb("m01", [P, 1]), sb("pen", [P, 1])
        ctxT = sb("ctxT", [P, G * KL])
        fold_k = sb("fold_k", [P, G, HEADS, KL])
        fold_v = sb("fold_v", [P, G, PAIRS, D])
        k1f, k3f = sb("k1f", [P, D]), sb("k3f", [P, D])
        k_rows = sb("k_rows", [P, 2, STACKS, 4, 32])
        k_stack = sb("k_stack", [P, 2, STACKS, G * KL])
        spread_f = k_stack[0:2 * HEADS, :, :, :].rearrange("p b s k -> p (b s k)").rearrange("p (h k) -> p h k", k=KL)
        k_blocks = sb("k_blocks", [P, 2, G, STACKS, 4, KL], f32r)
        v_blocks = sb("v_blocks", [P, 2, G, PAIRS, 32])
        fold2 = sb("fold2", [P, G * KL])
        s2_row = sb("s2_row", [1, G * KL])
        v2 = sb("v2", [P, G, D])
        ss, ms, rs = sb("ss", [P, G, 2]), sb("ms", [P, G, 2]), sb("rs", [P, G, 2])
        xn = sb("xn", [P, G, TILES, D])
        xT = sb("xT", [P, G, QL])
        nmax = sb("nmax", [P, G, TILES, HEADS])
        nmax_hl = sb("nmax_hl", [P, G, TILES, 2, HEADS])
        nmaxT = sb("nmaxT", [2 * HEADS, G, QL], f32r)
        prob = early[:, 0:4096].rearrange("p (g t n) -> p g t n", g=G, t=TILES)
        probT = sb("probT", [P, G, PAIRS, QL])
        rows = probT[0:1, :, :, :].rearrange("p g c q -> p (g c q)")[:, 0:(len(ROWS) + len(COLS)) * D].rearrange("p (r n) -> p r n", n=D)
        sums, rsum = sb("sums", [P, G, TILES, HEADS]), sb("rsum", [P, G, TILES, HEADS])
        x1, x2, x3 = (sb(n, [P, G, TILES, D]) for n in ("x1", "x2", "x3"))
        qf = sb("qf", [P, G, TILES, D])
        q_rows = early[:, 4096:6144].rearrange("p (g t s a r) -> p g t s a r", g=G, t=TILES, s=STACKS, a=4)
        q_rows3 = sb("q_rows3", [P, G, TILES, STACKS, 4, 32])
        q_stack = sb("q_stack", [P, G, STACKS, QL], f32r)
        attT = sb("attT", [P, G, 2, QL])
        att = sb("att", [P, G, TILES, D])
        pre = sb("pre", [P, G, TILES, D])
        stats, mv = sb("stats", [P, G, TILES, 6]), sb("mv", [P, G, TILES, 2])
        y = sb("y", [P, G, TILES, D])
        yb = sb("yb", [P, G, TILES, D])
        hT = sb("hT", [P, G, CHUNKS_FF, QL])
        nmax2, sums2, rsum2 = sb("nmax2", [P, G, TILES]), sb("sums2", [P, G, TILES]), sb("rsum2", [P, G, TILES])
        prob2 = sb("prob2", [P, G, TILES, KL])
        prob2T = sb("prob2T", [P, G, P])
        y_out = sb("y_out", [P, G, TILES, D])

        weights_in = sem("weights_in")
        x_loaded, c_loaded = sem("x_loaded"), sem("c_loaded")
        stored = sem("stored")
        pool_consts = sem("pool_consts")
        vec_consts = sem("vec_consts")
        wq_scaled = sem("wq_scaled")
        mask_read = sem("mask_read")
        ctx_read = sem("ctx_read")
        k_rows_ready = sem("k_rows_ready")
        k_stack_ready = sem("k_stack_ready")
        k_blocks_ready = sem("k_blocks_ready")
        squares = sem("squares")
        ms_ready, rs_ready = sem("ms_ready"), sem("rs_ready")
        xn_ready = sem("xn_ready")
        nmax_ready = {l: sem("nmax_ready" + l) for l in "013"}
        exp_done = {l: sem("exp_done" + l) for l in "02"}
        rsum_ready = sem("rsum_ready")
        norm_vec, norm_pool = sem("norm_vec"), sem("norm_pool")
        x1_ready, x2_ready, x3_ready = sem("x1_ready"), sem("x2_ready"), sem("x3_ready")
        q_rows_ready = {l: sem("q_rows_ready" + l) for l in "13"}
        nmax2_ready = sem("nmax2_ready")
        att_ready = sem("att_ready")
        var_ready = {l: sem("var_ready" + l) for l in ("1", "3", "4")}
        rstd_ready = {l: sem("rstd_ready" + l) for l in ("1", "3", "4")}
        y_ready = {l: sem("y_ready" + l) for l in "13"}
        out_ready = sem("out_ready")
        stats_written = sem("stats_written")
        step = sem("step")
        setup_step = sem("setup_step")

        block = ctx.enter_context(nc.Block())

        N_WEIGHTS = 18 + len(ROWS) + 5

        @block.sync
        def _(sp):
            def load_context(i):
                sp.dma_start(c_in[:, :], I["ctx_1024"].rearrange("(i g) k d -> i (g k) d", g=G)[i, :, :]).then_inc(c_loaded, 16)
                sp.dma_start(m_in[:, :], I["mask_Bx1x1xS2_if1"].rearrange("(i g) a b k -> i (g k) (a b)", g=G)[i, :, :]).then_inc(c_loaded, 16)

            def load_x(i):
                sp.dma_start(x_in[:, :, :, :], I["x"].rearrange("(i g) (t p) d -> i p g t d", g=G, p=P)[i, :, :, :, :]).then_inc(x_loaded, 16)

            def store(i):
                for g in range(G):
                    sp.wait_ge(out_ready, i * G + g + 1)
                    sp.dma_start(out.rearrange("(i g) (t p) d -> i g p t d", g=G, p=P)[i, g, :, :, :],
                                 y_out[:, g, :, :]).then_inc(stored, 16)

            sp.sem_inc(stored, 16)
            n = [0]

            def weight(dst, src):
                sp.dma_start(dst, src).then_inc(weights_in, 16)
                n[0] += 1

            biases = {"bq1": "L1_xattn_bq", "bk1": "L1_xattn_bk", "bv1": "L1_xattn_bv", "b2_1": "L1_xattn_b2",
                      "ln_g": "L1_xattn_ln_g", "ln_b": "L1_xattn_ln_b", "bv2": "L2_xattn_bv", "b_out": "L3_xattn_b_out",
                      "g1": "L3_xattn_g1", "beta1": "L3_xattn_beta1", "b_ff2": "L3_xattn_b_ff2",
                      "g2": "L3_xattn_g2", "beta2": "L3_xattn_beta2"}
            for r, name in enumerate(ROWS):
                weight(rows[0:1, r, :], I[biases[name]].rearrange("(a n) -> a n", a=1))
            first = len(ROWS)
            for r, name in ((0, "L0_xattn_norm_w"), (1, "L2_xattn_bk"), (2, "L2_xattn_bq")):
                weight(rows[0:1, first + r, :], I[name].rearrange("(a n) -> a n", a=1))
            weight(rows[0:1, first + 3:first + 7, :], I["L1_xattn_b1"].rearrange("(a c n) -> a c n", a=1, n=D))
            weight(rows[0:1, first + 7:first + 11, :], I["L3_xattn_b_ff1"].rearrange("(a c n) -> a c n", a=1, n=D))
            for k, name in enumerate(("L3_xattn_wk", "L3_xattn_wq", "L3_xattn_wv")):
                weight(w8[:, k, :], I[name])
            weight(wk0, I["L0_xattn_wk"])
            weight(wq0, I["L0_xattn_wq"])
            load_context(0)
            load_x(0)
            weight(wv0, I["L0_xattn_wv"])
            weight(wo0, I["L0_xattn_wo"].rearrange("(c p) n -> p c n", p=P))
            for dst, name in ((wq1, "L1_xattn_Wq"), (wk1, "L1_xattn_Wk"), (wv1, "L1_xattn_Wv"), (w2_1, "L1_xattn_W2"),
                              (wq2, "L2_xattn_Wq"), (wk2, "L2_xattn_Wk"), (wv2, "L2_xattn_Wv"),
                              (w_out, "L3_xattn_w_out"), (w_ff1, "L3_xattn_w_ff1")):
                weight(dst[:, :], I[name])
            weight(w1_1[:, :, :], I["L1_xattn_W1"].rearrange("(c p) n -> p c n", p=P))
            weight(w_ff2[:, :, :], I["L3_xattn_w_ff2"].rearrange("(c p) n -> p c n", p=P))
            assert n[0] == N_WEIGHTS, n[0]

            def refill(i):
                sp.wait_ge(ctx_read, i + 1)
                sp.wait_ge(mask_read, i + 1)
                load_context(i + 1)
                sp.wait_ge(x1_ready, (i + 1) * G)
                load_x(i + 1)

            with sp.Fori(0, TURNS - 1) as i:
                refill(i)
                store(i)
            store(TURNS - 1)
            sp.wait_ge(stored, 16 * BATCH + 16)

        @block.gpsimd
        def _(pool):
            for t in (ident, ident_bf):
                pool.memset(t[:, :], 0.0)
            pool.memset(spread_f, 0.0)
            for t in (rep_id, causal):
                pool.memset(t[:, :, :], 0.0)
            pool.memset(half_power[:, :], -0.5)
            pool.memset(v_blocks[:, :, :, :, :].rearrange("p a b c d -> p (a b c d)"), 0.0)
            pool.memset(k_rows[:, :, :, :, :].rearrange("p a b c d -> p (a b c d)"), 0.0)
            pool.memset(q_rows3[:, :, :, :, :, :].rearrange("p a b c d e -> p (a b c d e)"), 0.0)
            pool.memset(ones_row[:, :], 1.0).then_inc(pool_consts, 1)
            pool.wait_ge(pool_consts, 1)
            for t in (ident, ident_bf):
                pool.affine_select(out=t[:, :], in_=t[:, :], compare_op=ALU.not_equal, fill=1.0, base=0,
                                   pattern=[[-1, P]], channel_multiplier=1)
            pool.affine_select(out=rep_id[:, :, :], in_=rep_id[:, :, :], compare_op=ALU.not_equal, fill=1.0, base=0,
                               pattern=[[0, HEADS], [-1, DH]], channel_multiplier=1)
            pool.affine_select(out=causal[:, :, :], in_=causal[:, :, :], compare_op=ALU.is_ge, fill=CAUSAL_FILL, base=0,
                               pattern=[[0, 2], [-1, KL]], channel_multiplier=1)
            pool.affine_select(out=spread_f, in_=spread_f, compare_op=ALU.not_equal, fill=1.0, base=0,
                               pattern=[[-1, HEADS], [0, KL]], channel_multiplier=1).then_inc(pool_consts, 1)
            pool.wait_ge(pool_consts, 2)
            pool.affine_select(out=spread_f, in_=spread_f, compare_op=ALU.not_equal, fill=1.0,
                               base=-HEADS, pattern=[[-1, HEADS], [0, KL]], channel_multiplier=1)
            pool.memset(q_rows3[:, :, :, :, 3, 0:2].rearrange("p g t s d -> p (g t s) d"), 1.0).then_inc(pool_consts, 1)

            with pool.Fori(0, TURNS) as i:
                for g in range(G):
                    pool.wait_ge(ms_ready, i * G + g + 1)
                    pool.tensor_tensor(out=rs[:, g, :], in0=ms[:, g, :], in1=half_power[:, :], op=ALU.pow).then_inc(rs_ready, 1)
                pool.wait_ge(k_stack_ready, i + 1)
                pool.wait_ge(vec_consts, 2)
                for b, heads_of in ((0, stack_head), (1, stack_head3)):
                    for g in range(G):
                        for s in range(STACKS):
                            last = pool.tensor_tensor(
                                out=k_blocks[:, b, g, s, :, :],
                                in0=k_stack[:, b, s, g * KL:(g + 1) * KL].unsqueeze(1).broadcast_to([P, 4, KL]),
                                in1=heads_of[:, :].unsqueeze(2).broadcast_to([P, 4, KL]), op=ALU.mult)
                        last.then_inc(k_blocks_ready, 1)
                for g in range(G):
                    pool.wait_ge(rsum_ready, (i * G + g) * TILES + 2)
                    pool.tensor_tensor(out=prob[:, g, 1, :].rearrange("p (h k) -> p h k", k=KL),
                                       in0=prob[:, g, 1, :].rearrange("p (h k) -> p h k", k=KL),
                                       in1=rsum[:, g, 1, :].unsqueeze(2).broadcast_to([P, HEADS, KL]),
                                       op=ALU.mult).then_inc(norm_pool, 1)
                for l in ("1", "3", "4"):
                    for g in range(G):
                        pool.wait_ge(var_ready[l], i * G + g + 1)
                        pool.tensor_tensor(out=rs[:, g, :], in0=ms[:, g, :], in1=half_power[:, :],
                                           op=ALU.pow).then_inc(rstd_ready[l], 1)

        @block.scalar
        def _(act):
            for name, part, dst in (("wkT", 0, wkT), ("wvT", 0, wvT),
                                    ("wqk", 0, wqk[:, 0:8, :].rearrange("p (c a) n -> p a c n", a=2)),
                                    ("wqk", 1, wqk[:, 8:16, :].rearrange("p (c a) n -> p a c n", a=2)),
                                    ("wvo", 0, wvo[:, 0, :, :]), ("wvo", 1, wvo[:, 1, :, :])):
                b = pro[(name, 0, part)]
                act.wait_ge(written[b.region], b.is_written())
                src = psum[b.region][:, :].rearrange("p (c n) -> p c n", n=P)
                if name == "wqk":
                    src = psum[b.region][:, :].rearrange("p (a c n) -> p a c n", a=2, n=P)
                act.activation(dst, src, ACT.Copy).then_inc(drained[b.region], 1)

            def drain(key, i, dst, src):
                b = body[key]
                act.wait_ge(written[b.region], b.is_written(i))
                act.activation(dst, src(psum[b.region]), ACT.Copy).then_inc(drained[b.region], 1)

            def exps_to_probT(l, scale, g, half, i):
                b = body[("st" + l, g, half)]
                act.wait_ge(written[b.region], b.is_written(i))
                act.activation(probT[:, g, 4 * half:4 * half + 4, :],
                               psum[b.region][:, :].rearrange("p (c q) -> p c q", q=QL), ACT.Exp,
                               scale=scale).then_inc(drained[b.region], 1)

            with act.Fori(0, TURNS) as i:
                act.wait_ge(x_loaded, 16 * (i + 1))
                for g in range(G):
                    for t in range(TILES):
                        last = act.activation(xn[:, g, t, :], x_in[:, g, t, :], ACT.Square, accum_out=ss[:, g, t:t + 1])
                    last.then_inc(squares, 1)
                for half in range(2):
                    drain(("fold_k", 0, half), i, fold_k[:, :, 8 * half:8 * half + 8, :],
                          lambda ps: ps[:, :].rearrange("p (h g k) -> p g h k", g=G, k=KL))
                for g in range(G):
                    drain(("fold_v", g, 0), i, fold_v[:, g, :, :], lambda ps: ps[:, :].rearrange("p (c n) -> p c n", n=D))
                b = body[("stack_k", 0, 0)]
                act.wait_ge(written[b.region], b.is_written(i))
                act.activation(k_stack[:, :, :, :], psum[b.region][:, :].rearrange("p (b s k) -> p b s k", b=2, s=STACKS),
                               ACT.Copy).then_inc(drained[b.region], 1)
                act.wait_ge(drained[b.region], b.is_drained(i))
                act.sem_inc(k_stack_ready, 1)
                for g in range(G):
                    for t in range(TILES):
                        b = body[("sub0", g, t)]
                        act.wait_ge(written[b.region], b.is_written(i))
                        act.activation(prob[:, g, t, :], psum[b.region][:, :], ACT.Exp).then_inc(drained[b.region], 1)
                for g in range(G):
                    for t in range(TILES):
                        drain(("p0T", g, t), i, probT[:, g, :, t * P:(t + 1) * P],
                              lambda ps: ps[:, :].rearrange("p (c q) -> p c q", q=P))
                for l, scale in (("1", SCALE1), ("3", SCALE3)):
                    if l == "3":
                        for g in range(G):
                            act.wait_ge(nmax2_ready, i * G + g + 1)
                            b = body[("s2", g, 0)]
                            for t in range(TILES):
                                last = act.activation(prob2[:, g, t, :], psum[b.region][:, t * KL:(t + 1) * KL], ACT.Exp,
                                                      bias=nmax2[:, g, t:t + 1], accum_out=sums2[:, g, t:t + 1])
                            last.then_inc(drained[b.region], 1)
                        for g in range(G):
                            drain(("p2T", g, 0), i, prob2T[:, g, :], lambda ps: ps[:, 0:P])
                    for g in range(G):
                        drain(("q%sT" % l, g, 0), i, q_stack[:, g, :, :], lambda ps: ps[:, :].rearrange("p (s q) -> p s q", q=QL))
                    for g, half in ((0, 0), (0, 1), (1, 0)):
                        exps_to_probT(l, scale, g, half, i)
                    exps_to_probT(l, scale, 1, 1, i)
                    for g in range(G):
                        drain(("pv" + l, g, 0), i, attT[:, g, :, :], lambda ps: ps[:, :].rearrange("p (a q) -> p a q", q=QL))
                    for g in range(G):
                        b = body[("h" + l, g, 0)]
                        act.wait_ge(written[b.region], b.is_written(i))
                        for c in range(CHUNKS_FF):
                            last = act.activation(hT[:, g, c, :], psum[b.region][:, c * QL:(c + 1) * QL],
                                                  ACT.Gelu if l == "1" else ACT.Relu,
                                                  bias=col(("b1_%d" if l == "1" else "bff1_%d") % c))
                        last.then_inc(drained[b.region], 1)

        @block.vector
        def _(dve):
            made = [0]

            def setup(ins):
                made[0] += 1
                ins.then_inc(setup_step, 1)
                dve.wait_ge(setup_step, made[0])

            def take(key, dst, src):
                b = pro[key]
                dve.wait_ge(written[b.region], b.is_written())
                dve.tensor_copy(dst, src(psum[b.region])).then_inc(drained[b.region], 1)

            dve.wait_ge(pool_consts, 3)
            setup(dve.tensor_copy(spread[:, :, :], spread_f))
            for half in range(2):
                dve.memset(v_blocks[half * KL:(half + 1) * KL, :, :, :, 16 + half:17 + half], 1.0)
            setup(dve.reduce_sum(head_of[:, :], ident[:, :].rearrange("p (h r) -> p h r", r=DH), axis=AX.X))
            setup(dve.reduce_sum(stack_head[:, :], head_of[:, :].rearrange("p (a h) -> p h a", h=4), axis=AX.X))
            setup(dve.tensor_copy(stack_head3[:, :], stack_head[:, :]))
            dve.memset(stack_head3[96:128, :], 1.0).then_inc(vec_consts, 1)
            ps_rows = len(ROWS) * D
            take(("rows0", 0, 0), bc[:, 0:8, :], lambda ps: ps[:, :].rearrange("p (r n) -> p r n", n=D))
            take(("rows1", 0, 0), bc[:, 8:len(ROWS), :], lambda ps: ps[:, 0:ps_rows - BIG].rearrange("p (r n) -> p r n", n=D))
            take(("cols", 0, 0), cols[:, :], lambda ps: ps[:, 0:len(COLS)])
            b = pro[("cols", 0, 0)]
            dve.wait_ge(drained[b.region], b.is_drained())
            dve.tensor_scalar(wq0, wq0, col("norm_w"), None, ALU.mult).then_inc(wq_scaled, 1)
            take(("l3_small_t", 0, 0), w8T[:, :, :], lambda ps: ps[0:DH, 0:3 * DH].rearrange("p (a n) -> p a n", n=DH))
            take(("wqT", 0, 0), wqT, lambda ps: ps[:, :].rearrange("p (c n) -> p c n", n=P))
            take(("l3_b", 0, 0), b8[:, :], lambda ps: ps[0:DH, 0:DH])
            take(("l3_rep", 0, 0), rep8[:, :, :], lambda ps: ps[0:DH, 0:2 * D].rearrange("p (a n) -> p a n", n=D))
            b = pro[("l3_full", 0, 0)]
            dve.wait_ge(written[b.region], b.is_written())
            for a in range(2):
                last = dve.tensor_tensor(out=l3_full[:, a, :].rearrange("p (h d) -> p h d", d=DH),
                                         in0=psum[b.region][:, a * D:(a + 1) * D].rearrange("p (h d) -> p h d", d=DH),
                                         in1=head_of[:, :].unsqueeze(2).broadcast_to([P, HEADS, DH]), op=ALU.mult)
            last.then_inc(drained[b.region], 1)
            b = pro[("l1_wT", 0, 0)]
            dve.wait_ge(written[b.region], b.is_written())
            dve.tensor_copy(l1_wT[:, :, :], psum[b.region][:, 0:3 * P].rearrange("p (a n) -> p a n", n=P))
            dve.tensor_copy(w1T[:, :, :], psum[b.region][:, 3 * P:7 * P].rearrange("p (a n) -> p a n", n=P)).then_inc(drained[b.region], 1)
            b = pro[("l12_w", 0, 0)]
            dve.wait_ge(written[b.region], b.is_written())
            dve.tensor_copy(w2T[:, :, :], psum[b.region][:, 0:FF].rearrange("p (a n) -> p a n", n=P))
            dve.tensor_copy(wv2T[:, :], psum[b.region][:, FF:FF + D])
            dve.tensor_copy(wqk2[:, :], psum[b.region][:, FF + D:FF + 2 * D])
            dve.tensor_copy(c2[:, 0:2], psum[b.region][:, FF + 2 * D:FF + 2 * D + 2])
            dve.tensor_copy(c2[0:1, 2:3], psum[b.region][0:1, FF + 2 * D + 2:FF + 2 * D + 3]).then_inc(drained[b.region], 1)
            dve.wait_ge(drained[b.region], b.is_drained())
            dve.sem_inc(vec_consts, 1)

            count = [0]
            STEPS = 56

            with dve.Fori(0, TURNS) as i:
                def link(ins):
                    count[0] += 1
                    ins.then_inc(step, 1)
                    dve.wait_ge(step, i * STEPS + count[0])

                def written_wait(key):
                    b = body[key]
                    dve.wait_ge(written[b.region], b.is_written(i))
                    return psum[b.region], drained[b.region], b

                def drain(key, dst, src):
                    ps, free, _ = written_wait(key)
                    dve.tensor_copy(dst, src(ps)).then_inc(free, 1)

                def split(hi_dst, lo_dst, src_hi, src_lo, hi_for_lo):
                    link(dve.tensor_copy(hi_dst.bitcast(f32r), src_hi))
                    return dve.tensor_tensor(out=lo_dst.bitcast(f32r), in0=src_lo, in1=hi_for_lo, op=ALU.subtract)

                def max_split(l, g):
                    link(dve.tensor_copy(nmax_hl[:, g, :, 0, :].bitcast(f32r), nmax[:, g, :, :]))
                    dve.tensor_tensor(out=nmax_hl[:, g, :, 1, :].bitcast(f32r), in0=nmax[:, g, :, :],
                                      in1=nmax_hl[:, g, :, 0, :], op=ALU.subtract).then_inc(nmax_ready[l], 1)

                def tile_max(key, l, g, t):
                    ps, free, _ = written_wait(key)
                    ins = dve.tensor_reduce(out=nmax[:, g, t, :], in_=ps[:, :].rearrange("p (h k) -> p h k", k=KL),
                                            op=ALU.max, axis=AX.X, negate=True)
                    return ins, free

                def drain_maxT(l, g):
                    drain(("max" + l, g, 0), nmaxT[:, g, :], lambda ps: ps[0:2 * HEADS, 0:QL])

                def layer_norm(src, l, g, gamma, beta, dst, done):
                    for t in range(TILES):
                        last = dve.bn_stats(stats[:, g, t, :], src[:, g, t, :])
                    link(last)
                    dve.sem_inc(stats_written, 1)
                    for t in range(TILES):
                        last = dve.bn_aggr(mv[:, g, t, :], stats[:, g, t, :])
                    link(last)
                    dve.tensor_scalar(ms[:, g, :], mv[:, g, :, 1], LN_EPS, None, ALU.add).then_inc(var_ready[l], 1)
                    dve.wait_ge(rstd_ready[l], i * G + g + 1)
                    for t in range(TILES):
                        last = dve.tensor_scalar(dst[:, g, t, :], src[:, g, t, :], mv[:, g, t, 0:1], rs[:, g, t:t + 1],
                                                 ALU.subtract, ALU.mult)
                    link(last)
                    link(dve.tensor_tensor(out=dst[:, g, :, :], in0=dst[:, g, :, :],
                                           in1=row(gamma).unsqueeze(1).broadcast_to([P, TILES, D]), op=ALU.mult))
                    dve.tensor_tensor(out=dst[:, g, :, :], in0=dst[:, g, :, :],
                                      in1=row(beta).unsqueeze(1).broadcast_to([P, TILES, D]), op=ALU.add).then_inc(done, 1)

                dve.wait_ge(c_loaded, 32 * (i + 1))
                dve.tensor_scalar(m01[:, :], m_in[:, :], 0.0, None, ALU.not_equal)
                ins = dve.tensor_scalar(pen[:, :], m_in[:, :], 0.0, MASK_FILL, ALU.is_equal, ALU.mult)
                link(ins)
                dve.sem_inc(mask_read, 1)
                drain(("ctxT", 0, 0), ctxT[:, :], lambda ps: ps[:, 0:P])
                for g in range(G):
                    dve.wait_ge(squares, i * G + g + 1)
                    dve.tensor_scalar(ms[:, g, :], ss[:, g, :], 1.0 / D, RMS_EPS, ALU.mult, ALU.add).then_inc(ms_ready, 1)
                ps, free, b = written_wait(("ctx_k", 0, 0))
                dve.tensor_tensor(out=k1f[:, :], in0=ps[:, 0:D], in1=row("bk1"), op=ALU.add)
                dve.tensor_scalar(k3f[:, :], ps[:, D:2 * D], m01[:, 0:1], None, ALU.mult)
                dve.tensor_scalar(fold2[:, :], ps[:, 2 * D:3 * D], c2[:, 0:1], None, ALU.add)
                dve.tensor_scalar(s2_row[:, :], ps[0:1, 3 * D:4 * D], c2[0:1, 2:3], None, ALU.add).then_inc(free, 1)
                dve.wait_ge(free, b.is_drained(i))
                for n, kf in ((0, k1f), (1, k3f)):
                    kv = kf[:, :].rearrange("p (s r) -> p s r", r=32)
                    for part in (0, 2):
                        last = dve.tensor_copy(k_rows[:, n, :, part, :].bitcast(f32r), kv)
                last = dve.tensor_copy(k_rows[:, 1, :, 3, 0:1].bitcast(f32r), pen[:, :].unsqueeze(1).broadcast_to([P, STACKS, 1]))
                link(last)
                for part in (1, 3):
                    dve.tensor_tensor(out=k_rows[:, 0, :, part, :].bitcast(f32r), in0=k1f[:, :].rearrange("p (s r) -> p s r", r=32),
                                      in1=k_rows[:, 0, :, 0, :], op=ALU.subtract)
                dve.tensor_tensor(out=k_rows[:, 1, :, 3, 1:2].bitcast(f32r), in0=pen[:, :].unsqueeze(1).broadcast_to([P, STACKS, 1]),
                                  in1=k_rows[:, 1, :, 3, 0:1], op=ALU.subtract)
                dve.tensor_tensor(out=k_rows[:, 1, :, 1, :].bitcast(f32r), in0=k3f[:, :].rearrange("p (s r) -> p s r", r=32),
                                  in1=k_rows[:, 1, :, 0, :], op=ALU.subtract).then_inc(k_rows_ready, 1)
                ps, free, b = written_wait(("ctx_v", 0, 0))
                for half in range(2):
                    rows_of = slice(half * KL, (half + 1) * KL)
                    cols_of = slice(half * DH, (half + 1) * DH)
                    for g in range(G):
                        dve.tensor_tensor(out=v_blocks[rows_of, 0, g, :, cols_of],
                                          in0=ps[rows_of, g * KL:(g + 1) * KL].rearrange("p (c d) -> p c d", d=DH),
                                          in1=row("bv1")[rows_of, :].rearrange("p (c a d) -> p c a d", a=2, d=DH)[:, :, half, :],
                                          op=ALU.add)
                        dve.tensor_copy(v_blocks[rows_of, 1, g, :, cols_of],
                                        ps[rows_of, P + g * KL:P + (g + 1) * KL].rearrange("p (c d) -> p c d", d=DH))
                dve.tensor_tensor(out=v2[:, :, :], in0=ps[:, 2 * P:4 * P].rearrange("p (g n) -> p g n", n=D),
                                  in1=row("bv2").unsqueeze(1).broadcast_to([P, G, D]), op=ALU.add).then_inc(free, 1)
                for g in range(G):
                    dve.wait_ge(rs_ready, i * G + g + 1)
                    for t in range(TILES):
                        last = dve.tensor_scalar(xn[:, g, t, :], x_in[:, g, t, :], rs[:, g, t:t + 1], None, ALU.mult)
                    last.then_inc(xn_ready, 1)
                for g in range(G):
                    drain(("xnT", g, 0), xT[:, g, :], lambda ps: ps[:, 0:QL])
                for g in range(G):
                    if g == 0:
                        ins, _ = tile_max(("s0", 0, 0), "0", 0, 0)
                        ins, _ = tile_max(("s0", 0, 1), "0", 0, 1)
                        link(ins)
                        max_split("0", 0)
                        tile_max(("s0", 1, 0), "0", 1, 0)
                        drain_maxT("0", 0)
                    else:
                        ins, _ = tile_max(("s0", 1, 1), "0", 1, 1)
                        link(ins)
                        max_split("0", 1)
                        drain_maxT("0", 1)
                for g in range(G):
                    for t in range(TILES):
                        b = body[("s0", g, t)]
                        dve.wait_ge(drained[b.region], b.is_drained(i))
                        pv = prob[:, g, t, :].rearrange("p (h k) -> p h k", k=KL)
                        link(dve.reduce_sum(sums[:, g, t, :], pv, axis=AX.X))
                        ins = dve.reciprocal(rsum[:, g, t, :], sums[:, g, t, :])
                        ins.then_inc(rsum_ready, 1)
                        if t == 0:
                            dve.wait_ge(rsum_ready, (i * G + g) * TILES + 1)
                            dve.tensor_tensor(out=pv, in0=pv, in1=rsum[:, g, t, :].unsqueeze(2).broadcast_to([P, HEADS, KL]),
                                              op=ALU.mult).then_inc(norm_vec, 1)
                for g in range(G):
                    ps, free, b = written_wait(("o0", g, 0))
                    dve.tensor_tensor(out=x1[:, g, :, :], in0=ps[:, 0:QL].rearrange("p (t n) -> p t n", n=D),
                                      in1=x_in[:, g, :, :], op=ALU.add).then_inc(free, 1)
                    dve.wait_ge(free, b.is_drained(i))
                    dve.sem_inc(x1_ready, 1)
                for g in range(G):
                    drain(("x1T", g, 0), xT[:, g, :], lambda ps: ps[:, 0:QL])
                for g in range(G):
                    ps, free, b = written_wait(("q1", g, 0))
                    dve.tensor_tensor(out=qf[:, g, :, :], in0=ps[:, 0:QL].rearrange("p (t n) -> p t n", n=D),
                                      in1=row("bq1").unsqueeze(1).broadcast_to([P, TILES, D]), op=ALU.add).then_inc(free, 1)
                    dve.wait_ge(free, b.is_drained(i))
                    qv = qf[:, g, :, :].rearrange("p t (s r) -> p (t s) r", r=32)
                    dst = q_rows[:, g, :, :, :, :].rearrange("p t s a r -> p (t s) a r")
                    link(dve.tensor_copy(dst[:, :, 0:2, :].bitcast(f32r), qv.unsqueeze(2).broadcast_to([P, 8, 2, 32])))
                    dve.tensor_tensor(out=dst[:, :, 2:4, :].bitcast(f32r), in0=qv.unsqueeze(2).broadcast_to([P, 8, 2, 32]),
                                      in1=dst[:, :, 0:2, :], op=ALU.subtract).then_inc(q_rows_ready["1"], 1)
                for l in "13":
                    n = 0 if l == "1" else 1
                    if l == "3":
                        for g in range(G):
                            drain(("x2T", g, 0), xT[:, g, :], lambda ps: ps[:, 0:QL])
                        for g in range(G):
                            ps, _, b = written_wait(("s2", g, 0))
                            dve.tensor_reduce(out=nmax2[:, g, :], in_=ps[:, 0:TILES * KL].rearrange("p (t k) -> p t k", k=KL),
                                              op=ALU.max, axis=AX.X, negate=True).then_inc(nmax2_ready, 1)
                        for g in range(G):
                            b = body[("s2", g, 0)]
                            dve.wait_ge(drained[b.region], b.is_drained(i))
                            link(dve.reciprocal(rsum2[:, g, :], sums2[:, g, :]))
                        for g in range(G):
                            ps, free, b = written_wait(("o2", g, 0))
                            for t in range(TILES):
                                last = dve.scalar_tensor_tensor(out=x3[:, g, t, :], in0=ps[:, t * 512:t * 512 + D],
                                                                scalar=rsum2[:, g, t:t + 1], in1=x2[:, g, t, :],
                                                                op0=ALU.mult, op1=ALU.add)
                            last.then_inc(free, 1)
                            dve.wait_ge(free, b.is_drained(i))
                            dve.sem_inc(x3_ready, 1)
                            xv = x3[:, g, :, :].rearrange("p t (s r) -> p (t s) r", r=32)
                            dst = q_rows3[:, g, :, :, :, :].rearrange("p t s a r -> p (t s) a r")
                            link(dve.tensor_copy(dst[:, :, 0:2, :].bitcast(f32r), xv.unsqueeze(2).broadcast_to([P, 8, 2, 32])))
                            dve.tensor_tensor(out=dst[:, :, 2, :].bitcast(f32r), in0=xv,
                                              in1=dst[:, :, 0, :], op=ALU.subtract).then_inc(q_rows_ready["3"], 1)
                    for g in range(G):
                        for t in range(TILES):
                            ins, free = tile_max(("s" + l, g, t), l, g, t)
                            ins.then_inc(free, 1)
                        b = body[("s" + l, g, 1)]
                        dve.wait_ge(drained[b.region], b.is_drained(i))
                        max_split(l, g)
                    for g in range(G):
                        drain_maxT(l, g)
                    for g in range(G):
                        ps, free, b = written_wait(("at" + l, g, 0))
                        pv = ps[:, :].rearrange("p (n m) -> p n m", m=32)
                        link(dve.reciprocal(rsum[:, g, :, :].rearrange("p t (c a) -> p (t c) a", a=2), pv[:, :, 16:18]))
                        dve.tensor_tensor(out=att[:, g, :, :].rearrange("p t (c a d) -> p (t c) a d", a=2, d=DH),
                                          in0=pv[:, :, 0:16].rearrange("p n (a d) -> p n a d", d=DH),
                                          in1=rsum[:, g, :, :].rearrange("p t (c a) -> p (t c) a", a=2).unsqueeze(3).broadcast_to([P, 16, 2, DH]),
                                          op=ALU.mult).then_inc(free, 1)
                        dve.wait_ge(free, b.is_drained(i))
                        if l == "1":
                            link(dve.tensor_tensor(out=pre[:, g, :, :], in0=att[:, g, :, :], in1=x1[:, g, :, :], op=ALU.add))
                            layer_norm(pre, "1", g, "ln_g", "ln_b", y, y_ready["1"])
                        else:
                            dve.sem_inc(att_ready, 1)
                    if l == "3":
                        for g in range(G):
                            drain(("a3T", g, 0), xT[:, g, :], lambda ps: ps[:, 0:QL])
                        for g in range(G):
                            link(dve.tensor_tensor(out=yb[:, g, :, :], in0=x3[:, g, :, :],
                                                   in1=row("b_out").unsqueeze(1).broadcast_to([P, TILES, D]), op=ALU.add))
                            ps, free, b = written_wait(("w3", g, 0))
                            dve.tensor_tensor(out=pre[:, g, :, :], in0=ps[:, 0:QL].rearrange("p (t n) -> p t n", n=D),
                                              in1=yb[:, g, :, :], op=ALU.add).then_inc(free, 1)
                            dve.wait_ge(free, b.is_drained(i))
                            layer_norm(pre, "3", g, "g1", "beta1", y, y_ready["3"])
                    for g in range(G):
                        drain(("y%sT" % l, g, 0), xT[:, g, :], lambda ps: ps[:, 0:QL])
                    for g in range(G):
                        dve.wait_ge(y_ready[l], i * G + g + 1)
                        link(dve.tensor_tensor(out=yb[:, g, :, :], in0=y[:, g, :, :],
                                               in1=row("b2_1" if l == "1" else "b_ff2").unsqueeze(1).broadcast_to([P, TILES, D]),
                                               op=ALU.add))
                    for g in range(G):
                        ps, free, b = written_wait(("f" + l, g, 0))
                        dst = x2 if l == "1" else pre
                        dve.tensor_tensor(out=dst[:, g, :, :], in0=ps[:, 0:QL].rearrange("p (t n) -> p t n", n=D),
                                          in1=yb[:, g, :, :], op=ALU.add).then_inc(free, 1)
                        dve.wait_ge(free, b.is_drained(i))
                        if l == "1":
                            dve.sem_inc(x2_ready, 1)
                        else:
                            dve.wait_ge(stored, 16 * G * i + 16)
                            layer_norm(pre, "4", g, "g2", "beta2", y_out, out_ready)
            assert count[0] == STEPS, count[0]

        @block.tensor
        def _(pe):
            mm = nc.tensor.matmul

            def open_pro(key):
                b = pro[key]
                if b.drains:
                    pe.wait_ge(drained[b.region], b.is_free())
                return psum[b.region], written[b.region]

            def pro_ready(key):
                b = pro[key]
                pe.wait_ge(drained[b.region], b.is_drained())

            pe.wait_ge(pool_consts, 3)
            pe.wait_ge(weights_in, 16 * N_WEIGHTS)
            for key, n0, n1 in ((("rows0", 0, 0), 0, 8), (("rows1", 0, 0), 8, len(ROWS))):
                ps, full = open_pro(key)
                for c in range(n0, n1, 4):
                    e = min(c + 4, n1)
                    last = mm(ps[:, (c - n0) * D:(e - n0) * D], ones_row[0:1, :], rows[0:1, c:e, :], start=True, stop=True)
                last.then_inc(full, 1)
            ps, full = open_pro(("cols", 0, 0))
            for c in range(len(COLS)):
                last = mm(ps[:, c:c + 1], rows[0:1, len(ROWS) + c, :], ones_row[0:1, 0:1], start=True, stop=True)
            last.then_inc(full, 1)
            ps, full = open_pro(("l3_small_t", 0, 0))
            for a in range(3):
                last = mm(ps[0:DH, a * DH:(a + 1) * DH], w8[:, a, :], ident[0:DH, 0:DH], start=True, stop=True)
            last.then_inc(full, 1)

            def transposes(key, src):
                ps, full = open_pro(key)
                for c, s in enumerate(src):
                    last = nc.tensor.transpose(ps[:, c * P:(c + 1) * P], s, ident[:, :])
                last.then_inc(full, 1)

            transposes(("wkT", 0, 0), [wk0[:, c * P:(c + 1) * P] for c in range(PAIRS)])
            pe.wait_ge(wq_scaled, 1)
            transposes(("wqT", 0, 0), [wq0[:, c * P:(c + 1) * P] for c in range(PAIRS)])
            pro_ready(("l3_small_t", 0, 0))
            ps, full = open_pro(("l3_b", 0, 0))
            mm(ps[0:DH, 0:DH], w8T[:, 1, :], w8T[:, 0, :], start=True, stop=True).then_inc(full, 1)
            pro_ready(("l3_b", 0, 0))
            ps, full = open_pro(("l3_rep", 0, 0))
            mm(ps[0:DH, 0:D], b8[:, :], rep_id[:, :, :], start=True, stop=True)
            mm(ps[0:DH, D:2 * D], w8T[:, 2, :], rep_id[:, :, :], start=True, stop=True).then_inc(full, 1)
            transposes(("wvT", 0, 0), [wv0[:, c * P:(c + 1) * P] for c in range(PAIRS)])
            pro_ready(("wkT", 0, 0))
            pro_ready(("wqT", 0, 0))
            for part in range(2):
                ps, full = open_pro(("wqk", 0, part))
                for n in range(8):
                    h = 8 * part + n
                    r = slice((h % 2) * DKV, (h % 2 + 1) * DKV)
                    at = (h % 2) * 4 + n // 2
                    last = mm(ps[:, at * P:(at + 1) * P], wkT[r, h // 2, :], wqT[r, h // 2, :], start=True, stop=True)
                last.then_inc(full, 1)
            pro_ready(("l3_rep", 0, 0))
            ps, full = open_pro(("l3_full", 0, 0))
            mm(ps[:, 0:2 * D], rep_id[:, :, :].rearrange("p h d -> p (h d)"), rep8[:, :, :], start=True, stop=True).then_inc(full, 1)
            pro_ready(("wvT", 0, 0))
            for part in range(2):
                ps, full = open_pro(("wvo", 0, part))
                r = slice(part * DKV, (part + 1) * DKV)
                for c in range(PAIRS):
                    last = mm(ps[:, c * D:(c + 1) * D], wvT[r, c, :], wo0[r, c, :], start=True, stop=True)
                last.then_inc(full, 1)
            transposes(("l1_wT", 0, 0), [wq1[:, :], wk1[:, :], wv1[:, :]] + [w1_1[:, c, :] for c in range(CHUNKS_FF)])
            ps, full = open_pro(("l12_w", 0, 0))
            for c in range(CHUNKS_FF):
                nc.tensor.transpose(ps[:, c * P:(c + 1) * P], w2_1[:, c * P:(c + 1) * P], ident[:, :])
            nc.tensor.transpose(ps[:, FF:FF + D], wv2[:, :], ident[:, :])
            mm(ps[:, FF + D:FF + 2 * D], wk2[:, :], wq2[:, :], start=True, stop=True)
            mm(ps[:, FF + 2 * D:FF + 2 * D + 1], wq2[:, :], col("bk2"), start=True, stop=True)
            mm(ps[:, FF + 2 * D + 1:FF + 2 * D + 2], wk2[:, :], col("bq2"), start=True, stop=True)
            mm(ps[0:1, FF + 2 * D + 2:FF + 2 * D + 3], col("bq2"), col("bk2"), start=True, stop=True).then_inc(full, 1)
            pe.wait_ge(vec_consts, 2)
            pro_ready(("wvo", 0, 1))

            with pe.Fori(0, TURNS) as i:
                def open_(key):
                    b = body[key]
                    pe.wait_ge(drained[b.region], b.is_free(i))
                    return psum[b.region], written[b.region]

                def ready(key):
                    b = body[key]
                    pe.wait_ge(drained[b.region], b.is_drained(i))

                def transpose_tiles(key, src, g):
                    ps, full = open_(key)
                    for t in range(TILES):
                        last = nc.tensor.transpose(ps[:, t * P:(t + 1) * P], src[:, g, t, :], ident[:, :])
                    last.then_inc(full, 1)

                def transpose_maxima(l, g):
                    pe.wait_ge(nmax_ready[l], i * G + g + 1)
                    ps, full = open_(("max" + l, g, 0))
                    for t in range(TILES):
                        last = nc.tensor.transpose(ps[0:2 * HEADS, t * P:(t + 1) * P],
                                                   nmax_hl[:, g, t, :, :].rearrange("p a h -> p (a h)"), ident[:, :])
                    last.then_inc(full, 1)

                pe.wait_ge(c_loaded, 32 * (i + 1))
                ps, full = open_(("ctxT", 0, 0))
                nc.tensor.transpose(ps[:, 0:P], c_in[:, :], ident[:, :]).then_inc(full, 1)
                ready(("ctxT", 0, 0))
                for half in range(2):
                    ps, full = open_(("fold_k", 0, half))
                    for n in range(8):
                        last = mm(ps[:, n * P:(n + 1) * P], wqk[:, 8 * half + n, :], ctxT[:, :], start=True, stop=True)
                    last.then_inc(full, 1)
                ps, full = open_(("ctx_k", 0, 0))
                mm(ps[:, 0:D], ctxT[:, :], l1_wT[:, 1, :], start=True, stop=True)
                mm(ps[:, D:2 * D], ctxT[:, :], l3_full[:, 0, :], start=True, stop=True)
                mm(ps[:, 2 * D:3 * D], wqk2[:, :], ctxT[:, :], start=True, stop=True)
                mm(ps[0:1, 3 * D:4 * D], c2[:, 1:2], ctxT[:, :], start=True, stop=True).then_inc(full, 1)
                ps, full = open_(("ctx_v", 0, 0))
                for g in range(G):
                    for half in range(2):
                        for n, w in ((0, l1_wT[:, 2, :]), (1, l3_full[:, 1, :])):
                            mm(ps[half * KL:(half + 1) * KL, n * P + g * KL:n * P + (g + 1) * KL], ctxT[:, g * KL:(g + 1) * KL],
                               w.rearrange("p (c a d) -> p c a d", a=2, d=DH)[:, :, half, :], start=True, stop=True)
                for g in range(G):
                    for half in range(2):
                        last = mm(ps[half * KL:(half + 1) * KL, 2 * P + g * D:2 * P + (g + 1) * D], ctxT[:, g * KL:(g + 1) * KL],
                                  wv2T[:, :], start=True, stop=True)
                last.then_inc(full, 1)
                for g in range(G):
                    pe.wait_ge(xn_ready, i * G + g + 1)
                    transpose_tiles(("xnT", g, 0), xn, g)
                for g in range(G):
                    ps, full = open_(("fold_v", g, 0))
                    for c in range(0, PAIRS, 4):
                        for half in range(2):
                            last = mm(ps[half * KL:(half + 1) * KL, c * D:(c + 4) * D], ctxT[:, g * KL:(g + 1) * KL],
                                      wvo[:, half, c:c + 4, :], start=True, stop=True)
                    last.then_inc(full, 1)
                pe.wait_ge(k_rows_ready, i + 1)
                ps, full = open_(("stack_k", 0, 0))
                for n in range(2):
                    for s in range(STACKS):
                        last = nc.tensor.transpose(ps[:, (n * STACKS + s) * P:(n * STACKS + s + 1) * P],
                                                   k_rows[:, n, s, :, :].rearrange("p a r -> p (a r)"), ident[:, :])
                last.then_inc(full, 1)
                pe.sem_inc(ctx_read, 1)

                def scores0(g, t):
                    ps, full = open_(("s0", g, t))
                    for c in range(0, HEADS, 8):
                        last = mm(ps[:, c * KL:(c + 8) * KL], xT[:, g, t * P:(t + 1) * P], fold_k[:, g, c:c + 8, :],
                                  start=True, stop=True)
                    last.then_inc(full, 1)

                def less_max0(g, t):
                    b = body[("sub0", g, t)]
                    for c in range(0, HEADS, 8):
                        last = mm(psum[b.region][:, c * KL:(c + 8) * KL], nmaxT[:, g, t * P:(t + 1) * P], spread[:, c:c + 8, :],
                                  start=False, stop=True, skip_group_check=True)
                    last.then_inc(written[b.region], 1)

                ready(("fold_k", 0, 1))
                ready(("xnT", 0, 0))
                scores0(0, 0)
                scores0(0, 1)
                ready(("xnT", 1, 0))
                scores0(1, 0)
                transpose_maxima("0", 0)
                ready(("max0", 0, 0))
                less_max0(0, 0)
                less_max0(0, 1)
                scores0(1, 1)
                transpose_maxima("0", 1)
                ready(("max0", 1, 0))
                less_max0(1, 0)
                less_max0(1, 1)
                for g in range(G):
                    for t in range(TILES):
                        if t == 0:
                            pe.wait_ge(norm_vec, i * G + g + 1)
                        else:
                            pe.wait_ge(norm_pool, i * G + g + 1)
                        ps, full = open_(("p0T", g, t))
                        for c in range(PAIRS):
                            last = nc.tensor.transpose(ps[:, c * P:(c + 1) * P], prob[:, g, t, c * P:(c + 1) * P], ident[:, :])
                        last.then_inc(full, 1)
                    ready(("p0T", g, 1))
                    ready(("fold_v", g, 0))
                    ps, full = open_(("o0", g, 0))
                    for t in range(TILES):
                        for c in range(PAIRS):
                            last = mm(ps[:, t * D:(t + 1) * D], probT[:, g, c, t * P:(t + 1) * P], fold_v[:, g, c, :],
                                      start=(c == 0), stop=(c == PAIRS - 1))
                    last.then_inc(full, 1)
                for g in range(G):
                    pe.wait_ge(x1_ready, i * G + g + 1)
                    transpose_tiles(("x1T", g, 0), x1, g)
                for g in range(G):
                    ready(("x1T", g, 0))
                    ps, full = open_(("q1", g, 0))
                    for t in range(TILES):
                        last = mm(ps[:, t * D:(t + 1) * D], xT[:, g, t * P:(t + 1) * P], l1_wT[:, 0, :], start=True, stop=True)
                    last.then_inc(full, 1)

                def stack_queries(l, rows_):
                    for g in range(G):
                        pe.wait_ge(q_rows_ready[l], i * G + g + 1)
                        ps, full = open_(("q%sT" % l, g, 0))
                        for s in range(STACKS):
                            for t in range(TILES):
                                last = nc.tensor.transpose(ps[:, s * QL + t * P:s * QL + (t + 1) * P],
                                                           rows_[:, g, t, s, :, :].rearrange("p a r -> p (a r)"), ident[:, :])
                        last.then_inc(full, 1)

                def small_heads(l):
                    n = 0 if l == "1" else 1
                    masked = l == "1"
                    for g in range(G):
                        ready(("q%sT" % l, g, 0))
                        pe.wait_ge(k_blocks_ready, i * 2 * G + n * G + g + 1)
                        for t in range(TILES):
                            ps, full = open_(("s" + l, g, t))
                            for bank in range(2):
                                fill = masked and t == 0
                                if fill:
                                    mm(ps[:, bank * 512:(bank + 1) * 512], ident_bf[0:KL, :],
                                       causal[:, 0, :].unsqueeze(1).broadcast_to([KL, 8, KL]), start=True, stop=False,
                                       skip_group_check=True)
                                for s in (2 * bank, 2 * bank + 1):
                                    last = mm(ps[:, s * QL:(s + 1) * QL], q_stack[:, g, s, t * P:(t + 1) * P],
                                              k_blocks[:, n, g, s, :, :], start=(s % 2 == 0 and not fill), stop=True,
                                              skip_group_check=True)
                            last.then_inc(full, 1)
                    for g in range(G):
                        transpose_maxima(l, g)

                    def scoresT(g, half):
                        ps, full = open_(("st" + l, g, half))
                        for c in range(4):
                            pair = 4 * half + c
                            s, a = pair // 2, pair % 2
                            o = ps[:, c * QL:(c + 1) * QL]
                            mm(o, k_blocks[:, n, g, s, 2 * a:2 * a + 2, :], q_stack[:, g, s, :], start=(c % 2 == 0), stop=False,
                               skip_group_check=True)
                            if masked:
                                mm(ps[:, c * QL:c * QL + KL], causal[:, :, :], ident_bf[0:KL, 0:KL], start=False, stop=False,
                                   skip_group_check=True)
                            last = mm(o, spread[:, 2 * pair:2 * pair + 2, :], nmaxT[:, g, :], start=False, stop=True,
                                      skip_group_check=True)
                        last.then_inc(full, 1)

                    def values(g):
                        ready(("st" + l, g, 1))
                        ps, full = open_(("pv" + l, g, 0))
                        for half in range(2):
                            for c in range(4):
                                last = mm(ps[32 * c:32 * c + 32, half * QL:(half + 1) * QL], v_blocks[:, n, g, 4 * half + c, :],
                                          probT[:, g, 4 * half + c, :], start=True, stop=True)
                        last.then_inc(full, 1)

                    ready(("max" + l, 0, 0))
                    scoresT(0, 0)
                    scoresT(0, 1)
                    ready(("max" + l, 1, 0))
                    scoresT(1, 0)
                    values(0)
                    scoresT(1, 1)
                    values(1)
                    for g in range(G):
                        ready(("pv" + l, g, 0))
                        ps, full = open_(("at" + l, g, 0))
                        for t in range(TILES):
                            for half in range(2):
                                last = nc.tensor.transpose(ps[:, (t * 2 + half) * P:(t * 2 + half + 1) * P],
                                                           attT[:, g, half, t * P:(t + 1) * P], ident[:, :])
                        last.then_inc(full, 1)

                def feed_forward(l, up, down):
                    for g in range(G):
                        pe.wait_ge(y_ready[l], i * G + g + 1)
                        transpose_tiles(("y%sT" % l, g, 0), y, g)
                    for g in range(G):
                        ready(("y%sT" % l, g, 0))
                        ps, full = open_(("h" + l, g, 0))
                        for c in range(CHUNKS_FF):
                            last = mm(ps[:, c * QL:(c + 1) * QL], up(c), xT[:, g, :], start=True, stop=True)
                        last.then_inc(full, 1)
                    for g in range(G):
                        ready(("h" + l, g, 0))
                        ps, full = open_(("f" + l, g, 0))
                        for t in range(TILES):
                            for c in range(CHUNKS_FF):
                                last = mm(ps[:, t * D:(t + 1) * D], hT[:, g, c, t * P:(t + 1) * P], down[:, c, :],
                                          start=(c == 0), stop=(c == CHUNKS_FF - 1))
                        last.then_inc(full, 1)

                stack_queries("1", q_rows)
                small_heads("1")
                feed_forward("1", lambda c: w1T[:, c, :], w2T)
                for g in range(G):
                    pe.wait_ge(x2_ready, i * G + g + 1)
                    transpose_tiles(("x2T", g, 0), x2, g)
                for g in range(G):
                    ready(("x2T", g, 0))
                    ps, full = open_(("s2", g, 0))
                    for t in range(TILES):
                        o = ps[:, t * KL:(t + 1) * KL]
                        mm(o, xT[:, g, t * P:(t + 1) * P], fold2[:, g * KL:(g + 1) * KL], start=True, stop=False)
                        last = mm(o, ones_row[0:1, :], s2_row[0:1, g * KL:(g + 1) * KL], start=False, stop=True)
                    last.then_inc(full, 1)
                for g in range(G):
                    ready(("s2", g, 0))
                    ps, full = open_(("p2T", g, 0))
                    nc.tensor.transpose(ps[:, 0:P], prob2[:, g, :, :].rearrange("p t k -> p (t k)"), ident[:, :]).then_inc(full, 1)
                for g in range(G):
                    ready(("p2T", g, 0))
                    ps, full = open_(("o2", g, 0))
                    for t in range(TILES):
                        last = mm(ps[:, t * 512:t * 512 + D], prob2T[t * KL:(t + 1) * KL, g, :], v2[t * KL:(t + 1) * KL, g, :],
                                  start=True, stop=True)
                    last.then_inc(full, 1)
                stack_queries("3", q_rows3)
                small_heads("3")
                for g in range(G):
                    pe.wait_ge(att_ready, i * G + g + 1)
                    transpose_tiles(("a3T", g, 0), att, g)
                for g in range(G):
                    ready(("a3T", g, 0))
                    ps, full = open_(("w3", g, 0))
                    for t in range(TILES):
                        last = mm(ps[:, t * D:(t + 1) * D], xT[:, g, t * P:(t + 1) * P], w_out[:, :], start=True, stop=True)
                    last.then_inc(full, 1)
                feed_forward("3", lambda c: w_ff1[:, c * P:(c + 1) * P], w_ff2)


INPUTS = ["x", "ctx_1024", "mask_Bx1x1xS2_if1",
          "L0_xattn_wq", "L0_xattn_wk", "L0_xattn_wv", "L0_xattn_wo", "L0_xattn_norm_w",
          "L1_xattn_Wq", "L1_xattn_bq", "L1_xattn_Wk", "L1_xattn_bk", "L1_xattn_Wv", "L1_xattn_bv",
          "L1_xattn_W1", "L1_xattn_b1", "L1_xattn_W2", "L1_xattn_b2", "L1_xattn_ln_g", "L1_xattn_ln_b",
          "L2_xattn_Wq", "L2_xattn_bq", "L2_xattn_Wk", "L2_xattn_bk", "L2_xattn_Wv", "L2_xattn_bv",
          "L3_xattn_wv", "L3_xattn_wk", "L3_xattn_wq", "L3_xattn_w_out", "L3_xattn_b_out", "L3_xattn_g1",
          "L3_xattn_beta1", "L3_xattn_w_ff1", "L3_xattn_b_ff1", "L3_xattn_w_ff2", "L3_xattn_b_ff2",
          "L3_xattn_g2", "L3_xattn_beta2"]


def kernel(**inputs):
    import numpy as np
    import concourse.bacc as bacc
    from concourse.bass_utils import run_bass_kernel_spmd

    nc = bacc.Bacc("TRN2", target_bir_lowering=False, num_devices=1)
    arrays = {name: np.ascontiguousarray(inputs[name]) for name in INPUTS}
    aps = {name: nc.dram_tensor(name, a.shape, mybir.dt.from_np(a.dtype), kind="ExternalInput").ap()
           for name, a in arrays.items()}
    out = nc.dram_tensor("out", (BATCH, QL, D), mybir.dt.float32, kind="ExternalOutput").ap()
    build(nc, aps, out)
    r = run_bass_kernel_spmd(nc, [arrays], core_ids=[0])
    return r.results[0]["out"]
```

```python
import concourse.bass as bass
from concourse import mybir
from contextlib import ExitStack

BATCH, QL, D = 16, 256, 128
KL = 64
HEADS = 16
DKV = 64
DH = D // HEADS
FF = 512
P = 128
TILES = QL // P
G = 2
TURNS = BATCH // G
PAIRS = HEADS // 2
CHUNKS_FF = FF // P
STACKS = 4
RMS_EPS, LN_EPS = 1e-6, 1e-5
CAUSAL_FILL, MASK_FILL = -1e9, -1e20
SCALE1 = DH ** -0.5
SCALE3 = D ** -0.5

BANKS_BIG, BIG = 3, 1024
BANKS_SMALL, SMALL = 2, 512

ROWS = ["bq1", "bk1", "bv1", "b2_1", "ln_g", "ln_b", "bv2", "b_out", "g1", "beta1", "b_ff2", "g2", "beta2"]
COLS = ["norm_w", "bk2", "bq2", "ln_gc", "ln_bc", "g1c", "beta1c"] + \
    ["b1_c%d" % c for c in range(CHUNKS_FF)] + ["bff1_c%d" % c for c in range(CHUNKS_FF)]
ROW_INPUT = {"bq1": "L1_xattn_bq", "bk1": "L1_xattn_bk", "bv1": "L1_xattn_bv", "b2_1": "L1_xattn_b2",
             "ln_g": "L1_xattn_ln_g", "ln_b": "L1_xattn_ln_b", "bv2": "L2_xattn_bv", "b_out": "L3_xattn_b_out",
             "g1": "L3_xattn_g1", "beta1": "L3_xattn_beta1", "b_ff2": "L3_xattn_b_ff2",
             "g2": "L3_xattn_g2", "beta2": "L3_xattn_beta2"}
COL_INPUT = {"norm_w": "L0_xattn_norm_w", "bk2": "L2_xattn_bk", "bq2": "L2_xattn_bq", "ln_gc": "L1_xattn_ln_g",
             "ln_bc": "L1_xattn_ln_b", "g1c": "L3_xattn_g1", "beta1c": "L3_xattn_beta1",
             "b1": "L1_xattn_b1", "bff1": "L3_xattn_b_ff1"}
VEC_STEPS, POOL_STEPS = 32, 3

PROLOGUE = [
    ("wkT", 0, 0, "big"), ("wqT", 0, 0, "big"), ("wvT", 0, 0, "big"), ("wqk", 0, 0, "big"), ("wqk", 0, 1, "big"),
    ("l3_small_t", 0, 0, "small"), ("wvo", 0, 0, "big"), ("wvo", 0, 1, "big"), ("l3_b", 0, 0, "small"),
    ("l1_wT", 0, 0, "big"), ("l3_rep", 0, 0, "small"), ("l12_w", 0, 0, "big"), ("l3_full", 0, 0, "small"),
]

SEQS, TS = range(G), range(TILES)


def each(name, ring):
    return {"%s_%d" % (name, g): [(name, g, 0, ring)] for g in SEQS}


def each_tiles(name, ring):
    return {"%s_%d" % (name, g): [(name, g, t, ring) for t in TS] for g in SEQS}


def halves(name, ring):
    return {"%s_%d%d" % (name, g, h): [(name, g, h, ring)] for g in SEQS for h in range(2)}


FRONT = {
    "ctxT": [("ctxT", 0, 0, "small")], "fold_k_0": [("fold_k", 0, 0, "big")], "fold_k_1": [("fold_k", 0, 1, "big")],
    "ctx1": [("ctx_k1", 0, 0, "small"), ("ctx_v1", 0, 0, "small")],
    **each("xnT", "small"), **each("fold_v", "big"), "stack_k1": [("stack_k1", 0, 0, "small")],
    **each_tiles("s0", "big"), **each("max0", "small"), **each_tiles("sub0", "more s0"), **each_tiles("p0T", "big"),
    **each("o0", "small"), **each("x1T", "small"), **each("q1", "small"), **each("q1T", "big"), **each_tiles("s1", "big"),
    **each("max1", "small"), **halves("st1", "big"), **each("pv1", "small"), **each("at1", "small"),
    "ctx3": [("ctx_k3", 0, 0, "small"), ("ctx_v3", 0, 0, "small")], "stack_k3": [("stack_k3", 0, 0, "small")],
}
BACK = {
    **each("y1T", "small"), **each("h1", "big"), **each("f1", "small"), **each("x2T", "small"), **each("s2", "small"),
    **each("p2T", "small"), **each("o2", "big"), **each("q3T", "big"), **each_tiles("s3", "big"), **each("max3", "small"),
    **halves("st3", "big"), **each("pv3", "small"), **each("at3", "small"), **each("a3T", "small"), **each("w3", "small"),
    **each("y3T", "small"), **each("h3", "big"), **each("f3", "small"),
}
FRONT_OTHERS = {"mask", "squares", "key_blocks1", "key_blocks3", "xn", "sums0_0", "sums0_1", "stats1", "norm1"}
BACK_OTHERS = {"stats3", "norm3", "stats4", "norm4", "x3_bias", "rsum2"}
ORDER = {
    "tensor": ("ctxT fold_k_0 fold_k_1 y1T_0 fold_v_1 y1T_1 h1_0 ctx1 h1_1 xnT_0 f1_0 xnT_1 s0_0 f1_1 max0_0 x2T_0 sub0_0 "
               "x2T_1 s2_0 fold_v_0 p2T_0 s0_1 s2_1 o2_0 max0_1 sub0_1 p2T_1 stack_k1 p0T_0 o2_1 q3T_0 o0_0 q3T_1 s3_0 p0T_1 "
               "s3_1 max3_0 x1T_0 o0_1 max3_1 st3_00 st3_01 q1_0 x1T_1 st3_10 st3_11 pv3_0 q1_1 q1T_0 at3_0 pv3_1 s1_0 q1T_1 "
               "a3T_0 at3_1 s1_1 max1_0 a3T_1 ctx3 max1_1 w3_1 w3_0 st1_00 st1_01 st1_10 st1_11 stack_k3 pv1_0 pv1_1 y3T_0 "
               "at1_0 y3T_1 at1_1 h3_0 h3_1 f3_0 f3_1"),
    "vector": ("y1T_0 squares mask y1T_1 xn ctx1 xnT_0 f1_0 xnT_1 s0_0 f1_1 max0_0 x2T_0 x2T_1 s2_0 sums0_0 s0_1 s2_1 max0_1 "
               "rsum2 o2_0 sums0_1 o2_1 s3_0 o0_0 max3_0 s3_1 o0_1 x1T_0 max3_1 q1_0 x1T_1 q1_1 at3_0 s1_0 a3T_0 at3_1 s1_1 "
               "max1_0 a3T_1 ctx3 max1_1 w3_0 w3_1 stats3 norm3 y3T_0 at1_0 y3T_1 at1_1 stats1 norm1 f3_0 f3_1 stats4 norm4"),
    "scalar": ("ctxT fold_k_0 squares fold_k_1 fold_v_1 h1_0 h1_1 sub0_0 s2_0 fold_v_0 p2T_0 s2_1 sub0_1 p2T_1 stack_k1 "
               "p0T_0 q3T_0 q3T_1 p0T_1 st3_00 st3_01 st3_10 st3_11 pv3_0 q1T_0 pv3_1 q1T_1 st1_00 st1_01 st1_10 st1_11 "
               "stack_k3 pv1_0 pv1_1 h3_0 h3_1"),
    "gpsimd": ("xn sums0_0 sums0_1 key_blocks1 x3_bias stats3 key_blocks3 norm3 stats1 norm1 stats4 norm4"),
}
ROOMY = {"at1_1", "at3_0", "at3_1", "ctx3", "ctxT", "max1_0", "o0_1", "pv1_1", "pv3_1", "stack_k3", "w3_0", "xnT_0", "xnT_1", "y3T_0", "y3T_1"}


def orders(engine):
    both = ORDER[engine].split()
    front, back = set(FRONT) | FRONT_OTHERS, set(BACK) | BACK_OTHERS
    assert all((s in front) != (s in back) for s in both) and len(set(both)) == len(both)
    return [s for s in both if s in front], both, [s for s in both if s in back]


def bursts(stages):
    return [(name, g, part, "big" if s in ROOMY and ring == "small" else ring)
            for s in stages for name, g, part, ring in (FRONT[s] if s in FRONT else BACK[s])]


class Burst:

    def __init__(self, region, writes, drains):
        self.region, self.writes, self.drains = region, writes, drains
        self.per_turn = (0, 0)

    def is_written(self, j=0):
        return j * self.per_turn[0] + self.writes

    def is_free(self, j=0):
        return j * self.per_turn[1] + self.drains

    def is_drained(self, j=0):
        return self.is_free(j) + 1


def place(order, writes, drains, turns=1):
    at, first, used = {}, (dict(writes), dict(drains)), {"big": 0, "small": 0}
    for name, g, part, ring in order:
        if ring.startswith("more"):
            region = at[(ring.split()[1], g, part)].region
            before = at[(ring.split()[1], g, part)].drains
        else:
            count = BANKS_BIG if ring == "big" else BANKS_SMALL
            region = (ring, used[ring] % count)
            used[ring] += 1
            before = drains[region]
            drains[region] += 1
        writes[region] += 1
        at[(name, g, part)] = Burst(region, writes[region], before)
    for b in at.values():
        b.per_turn = (writes[b.region] - first[0][b.region], drains[b.region] - first[1][b.region])
    for r in writes:
        writes[r] += (turns - 1) * (writes[r] - first[0][r])
        drains[r] += (turns - 1) * (drains[r] - first[1][r])
    return at


def build(nc, I, out):
    f32, f32r, bf16, i32 = mybir.dt.float32, mybir.dt.float32r, mybir.dt.bfloat16, mybir.dt.int32
    ACT, ALU, AX = mybir.ActivationFunctionType, mybir.AluOpType, mybir.AxisListType
    ctx = ExitStack()
    with ctx:
        def sb(name, shape, dt=f32):
            return ctx.enter_context(nc.sbuf_tensor(name, shape, dt))

        def sem(name):
            return ctx.enter_context(nc.semaphore(name))

        regions = [("big", n) for n in range(BANKS_BIG)] + [("small", n) for n in range(BANKS_SMALL)]
        psum = {r: ctx.enter_context(nc.psum_tensor("ps_%s%d" % r, [P, BIG if r[0] == "big" else SMALL], f32))
                for r in regions}
        written = {r: sem("written_%s%d" % r) for r in regions}
        drained = {r: sem("drained_%s%d" % r) for r in regions}
        writes, drains = {r: 0 for r in regions}, {r: 0 for r in regions}
        pro = place(PROLOGUE, writes, drains)
        head = place(bursts(orders("tensor")[0]), writes, drains)
        body = place(bursts(orders("tensor")[1]), writes, drains, TURNS - 1)
        tail = place(bursts(orders("tensor")[2]), writes, drains)

        def sections(eng, name, stages_of):
            in_front, both, in_back = orders(name)
            stages = stages_of(head, 0, 0, None)
            for s in in_front:
                stages[s]()
            with eng.Fori(0, TURNS - 1) as j:
                stages = stages_of(body, j, j + 1, j)
                for s in both:
                    stages[s]()
            stages = stages_of(tail, 0, None, TURNS - 1)
            for s in in_back:
                stages[s]()

        def of_each(name, stage):
            return {"%s_%d" % (name, g): (lambda g=g: stage(g)) for g in SEQS}

        early = sb("early", [P, 7 * HEADS * DKV])
        wq0, wk0, wv0 = (early[:, n * HEADS * DKV:(n + 1) * HEADS * DKV] for n in range(3))
        wo0, wkT, wqT, wvT = (early[:, n * HEADS * DKV:(n + 1) * HEADS * DKV].rearrange("p (c n) -> p c n", n=D)
                              for n in range(3, 7))
        probT = {l: sb("probT" + l, [P, G, PAIRS, QL]) for l in "13"}
        early2 = probT["3"][:, 1, :, :].rearrange("p c q -> p (c q)")
        hT = probT["3"][:, 0, :, :].rearrange("p (g c) q -> p g c q", g=G)
        wq1, wk1, wv1, wq2, wk2, wv2 = (early2[:, n * D:(n + 1) * D] for n in range(6))
        w2_1 = early2[:, 6 * D:6 * D + FF]
        w1_1 = early2[:, 10 * D:14 * D].rearrange("p (c n) -> p c n", n=D)
        w8 = sb("w8", [DH, 3, DH])
        w_out, w_ff1, w_ff2 = sb("w_out", [P, D]), sb("w_ff1", [P, FF]), sb("w_ff2", [P, CHUNKS_FF, D])
        wqk = sb("wqk", [P, HEADS, D])
        wvo = sb("wvo", [P, 2, PAIRS, D])
        l1_wT = sb("l1_wT", [P, 3, D])
        w1T = sb("w1T", [P, CHUNKS_FF, P])
        w2T = sb("w2T", [P, CHUNKS_FF, D])
        wv2T, wqk2 = sb("wv2T", [P, D]), sb("wqk2", [P, D])
        c2 = sb("c2", [P, 3])
        w8T = sb("w8T", [DH, 3, DH])
        b8 = sb("b8", [DH, DH])
        rep8 = sb("rep8", [DH, 2, D])
        l3_full = sb("l3_full", [P, 2, D])
        bc = sb("bc", [P, len(ROWS), D])
        cols = sb("cols", [P, len(COLS)])

        def row(name):
            return bc[:, ROWS.index(name), :]

        def col(name):
            n = COLS.index(name)
            return cols[:, n:n + 1]

        def per_tile(r):
            return r.unsqueeze(1).broadcast_to([P, G * TILES, D])

        ident = sb("ident", [P, P])
        ident_bf = sb("ident_bf", [P, P], bf16)
        ones_row = sb("ones_row", [1, P])
        rep_id = sb("rep_id", [DH, HEADS, DH])
        head_of = sb("head_of", [P, HEADS])
        stack_head = sb("stack_head", [P, STACKS])
        stack_head3 = sb("stack_head3", [P, STACKS])
        spread = sb("spread", [2 * HEADS, HEADS, KL], f32r)
        causal = sb("causal", [KL, 2, KL], bf16)
        half_power = sb("half_power", [P, G * TILES])

        x_in = sb("x_in", [P, G, TILES, D])
        c_in = sb("c_in", [P, D])
        m_in = sb("m_in", [P, 1], i32)
        m01, pen = sb("m01", [P, 1]), sb("pen", [P, 1])
        ctxT = sb("ctxT", [P, G * KL])
        fold_k = sb("fold_k", [P, G, HEADS, KL])
        fold_v = sb("fold_v", [P, G, PAIRS, D])
        fold2 = sb("fold2", [P, G * KL])
        s2_row = sb("s2_row", [1, G * KL])
        v2 = sb("v2", [P, G, D])
        kf = {l: sb("kf" + l, [P, D]) for l in "13"}
        k_rows = {l: sb("k_rows" + l, [P, STACKS, 4, 32]) for l in "13"}
        k_stack = sb("k_stack", [P, STACKS, G * KL])
        k_blocks = {l: sb("k_blocks" + l, [P, G, STACKS, 4, KL], f32r) for l in "13"}
        v_blocks = {l: sb("v_blocks" + l, [P, G, PAIRS, 32]) for l in "13"}
        xT = {l: sb("xT" + l, [P, G, QL]) for l in "13"}
        xn = sb("xn", [P, G, TILES, D])
        ss, ms, rs = sb("ss", [P, G * TILES]), sb("ms", [P, G * TILES]), sb("rs", [P, G * TILES])
        nmax = {l: sb("nmax" + l, [P, G, TILES, HEADS]) for l in "13"}
        nmax_hl = {l: sb("nmax_hl" + l, [P, G, TILES, 2, HEADS]) for l in "13"}
        nmaxT = {l: sb("nmaxT" + l, [2 * HEADS, G, QL], f32r) for l in "13"}
        prob = early[:, 0:4096].rearrange("p (g t n) -> p g t n", g=G, t=TILES)
        spread_f = probT["3"][0:2 * HEADS, 0, 0:4, :].rearrange("p c q -> p (c q)").rearrange("p (h k) -> p h k", k=KL)
        sums = sb("sums", [P, G, TILES, HEADS])
        rsum = {l: sb("rsum" + l, [P, G, TILES, HEADS]) for l in "013"}
        x1, x2 = (sb(n, [P, G, TILES, D]) for n in ("x1", "x2"))
        x3 = x2
        q_rows = {"1": early[:, 4096:6144].rearrange("p (g t s a r) -> p g t s a r", g=G, t=TILES, s=STACKS, a=4),
                  "3": sb("q_rows3", [P, G, TILES, STACKS, 4, 32])}
        q_stack = {l: sb("q_stack" + l, [P, G, STACKS, QL], f32r) for l in "13"}
        attT = early[:, 6144:7168].rearrange("p (g a q) -> p g a q", g=G, a=2)
        pre = {l: sb("pre" + l, [P, G, TILES, D]) for l in "134"}
        qf, att = pre["1"], pre
        stats, mv = ({l: sb(n + l, [P, G * TILES, w]) for l in "134"} for n, w in (("stats", 6), ("mv", 2)))
        var, rstd = ({l: sb(n + l, [P, G * TILES]) for l in "134"} for n in ("var", "rstd"))
        z = {l: pre[l][:, :, :, :].rearrange("p g t n -> p (g t) n") for l in "134"}
        y_bias = {l: sb("y_bias" + l, [P, G * TILES, D]) for l in "13"}
        x3_bias = xn[:, :, :, :].rearrange("p g t n -> p (g t) n")
        nmax2, sums2, rsum2 = sb("nmax2", [P, G, TILES]), sb("sums2", [P, G, TILES]), sb("rsum2", [P, G, TILES])
        prob2 = sb("prob2", [P, G, TILES, KL])
        prob2T = sb("prob2T", [P, G, P])
        y_out = sb("y_out", [P, G * TILES, D])

        keys_in, values_in, weights_in = sem("keys_in"), sem("values_in"), sem("weights_in")
        x_loaded, c_loaded = sem("x_loaded"), sem("c_loaded")
        stored = sem("stored")
        pool_consts = sem("pool_consts")
        vec_consts = sem("vec_consts")
        wq_scaled = sem("wq_scaled")
        mask_read, ctx_read = sem("mask_read"), sem("ctx_read")
        k_rows_ready = {l: sem("k_rows_ready" + l) for l in "13"}
        k_blocks_ready = {l: sem("k_blocks_ready" + l) for l in "13"}
        squares = sem("squares")
        ms_ready, rs_ready = sem("ms_ready"), sem("rs_ready")
        xn_ready = sem("xn_ready")
        nmax_ready = {l: sem("nmax_ready" + l) for l in "013"}
        rsum_ready = sem("rsum_ready")
        norm_vec, norm_pool = sem("norm_vec"), sem("norm_pool")
        x1_ready, x2_ready, x3_ready = sem("x1_ready"), sem("x2_ready"), sem("x3_ready")
        x3_bias_ready = sem("x3_bias_ready")
        q_rows_ready = {l: sem("q_rows_ready" + l) for l in "13"}
        nmax2_ready = sem("nmax2_ready")
        att_ready = sem("att_ready")
        var_ready, rstd_ready, z_ready = ({l: sem(n + l) for l in "134"} for n in ("var_ready", "rstd_ready", "z_ready"))
        y_bias_ready = {l: sem("y_bias_ready" + l) for l in "13"}
        out_ready = sem("out_ready")
        stats_written = sem("stats_written")
        step = sem("step")
        pool_step = sem("pool_step")
        setup_step = sem("setup_step")

        block = ctx.enter_context(nc.Block())

        N_WEIGHTS = len(ROWS) + 8 + 3 + 11

        @block.sync
        def _(sp):
            def load_context(i):
                sp.dma_start(c_in[:, :], I["ctx_1024"].rearrange("(i g) k d -> i (g k) d", g=G)[i, :, :]).then_inc(c_loaded, 16)
                sp.dma_start(m_in[:, :], I["mask_Bx1x1xS2_if1"].rearrange("(i g) a b k -> i (g k) (a b)", g=G)[i, :, :]).then_inc(c_loaded, 16)

            def load_x(i):
                sp.dma_start(x_in[:, :, :, :], I["x"].rearrange("(i g) (t p) d -> i p g t d", g=G, p=P)[i, :, :, :, :]).then_inc(x_loaded, 16)

            def store(i):
                sp.wait_ge(out_ready, i + 1)
                sp.dma_start(out.rearrange("(i g) (t p) d -> i p (g t) d", g=G, p=P)[i, :, :, :], y_out[:, :, :]).then_inc(stored, 16)

            sp.sem_inc(stored, 16)
            n = [0]

            def weight(dst, src):
                sp.dma_start(dst, src, allow_slow_non_contiguous=True).then_inc(weights_in, 16)
                n[0] += 1

            sp.dma_start(wk0, I["L0_xattn_wk"]).then_inc(keys_in, 16)
            sp.dma_start(wq0, I["L0_xattn_wq"]).then_inc(keys_in, 16)
            sp.dma_start(col("norm_w"), I[COL_INPUT["norm_w"]].rearrange("(n a) -> n a", a=1)).then_inc(keys_in, 16)
            sp.dma_start(wv0, I["L0_xattn_wv"]).then_inc(values_in, 16)
            sp.dma_start(wo0, I["L0_xattn_wo"].rearrange("(c p) n -> p c n", p=P)).then_inc(values_in, 16)
            load_context(0)
            load_x(0)
            for dst, name in ((wq1, "L1_xattn_Wq"), (wk1, "L1_xattn_Wk"), (wv1, "L1_xattn_Wv"), (w2_1, "L1_xattn_W2"),
                              (wq2, "L2_xattn_Wq"), (wk2, "L2_xattn_Wk"), (wv2, "L2_xattn_Wv")):
                weight(dst, I[name])
            weight(w1_1, I["L1_xattn_W1"].rearrange("(c p) n -> p c n", p=P))
            for k, name in enumerate(("L3_xattn_wk", "L3_xattn_wq", "L3_xattn_wv")):
                weight(w8[:, k, :], I[name])
            for r, name in enumerate(ROWS):
                weight(row(name), I[ROW_INPUT[name]].rearrange("(a n) -> a n", a=1).broadcast_to([P, D]))
            for c, name in enumerate(COLS[1:], 1):
                if name.endswith("_c0"):
                    weight(cols[:, c:c + CHUNKS_FF], I[COL_INPUT[name[:-3]]].rearrange("(c n) -> n c", n=P))
                elif "_c" not in name:
                    weight(cols[:, c:c + 1], I[COL_INPUT[name]].rearrange("(n a) -> n a", a=1))
            for dst, name in ((w_out[:, :], "L3_xattn_w_out"), (w_ff1[:, :], "L3_xattn_w_ff1")):
                weight(dst, I[name])
            weight(w_ff2[:, :, :], I["L3_xattn_w_ff2"].rearrange("(c p) n -> p c n", p=P))
            assert n[0] == N_WEIGHTS, n[0]

            def load_after(j):
                sp.wait_ge(ctx_read, j + 1)
                sp.wait_ge(mask_read, j + 1)
                load_context(j + 1)
                sp.wait_ge(x1_ready, (j + 1) * G)
                load_x(j + 1)

            load_after(0)
            with sp.Fori(0, TURNS - 2) as j:
                load_after(j + 1)
                store(j)
            store(TURNS - 2)
            store(TURNS - 1)
            sp.wait_ge(stored, 16 * TURNS + 16)

        @block.gpsimd
        def _(pool):
            pool.memset(ident[:, :], 0.0).then_inc(pool_consts, 1)
            pool.wait_ge(pool_consts, 1)
            pool.affine_select(out=ident[:, :], in_=ident[:, :], compare_op=ALU.not_equal, fill=1.0, base=0,
                               pattern=[[-1, P]], channel_multiplier=1).then_inc(pool_consts, 1)
            pool.memset(ident_bf[:, :], 0.0)
            pool.memset(spread_f, 0.0)
            for t in (rep_id, causal):
                pool.memset(t[:, :, :], 0.0)
            pool.memset(half_power[:, :], -0.5)
            for l in "13":
                pool.memset(v_blocks[l][:, :, :, :].rearrange("p b c d -> p (b c d)"), 0.0)
                pool.memset(k_rows[l][:, :, :, :].rearrange("p b c d -> p (b c d)"), 0.0)
            pool.memset(q_rows["3"][:, :, :, :, :, :].rearrange("p a b c d e -> p (a b c d e)"), 0.0)
            pool.memset(ones_row[:, :], 1.0).then_inc(pool_consts, 1)
            pool.wait_ge(pool_consts, 3)
            pool.affine_select(out=ident_bf[:, :], in_=ident_bf[:, :], compare_op=ALU.not_equal, fill=1.0, base=0,
                               pattern=[[-1, P]], channel_multiplier=1)
            pool.affine_select(out=rep_id[:, :, :], in_=rep_id[:, :, :], compare_op=ALU.not_equal, fill=1.0, base=0,
                               pattern=[[0, HEADS], [-1, DH]], channel_multiplier=1)
            pool.affine_select(out=causal[:, :, :], in_=causal[:, :, :], compare_op=ALU.is_ge, fill=CAUSAL_FILL, base=0,
                               pattern=[[0, 2], [-1, KL]], channel_multiplier=1)
            pool.affine_select(out=spread_f, in_=spread_f, compare_op=ALU.not_equal, fill=1.0, base=0,
                               pattern=[[-1, HEADS], [0, KL]], channel_multiplier=1).then_inc(pool_consts, 1)
            pool.wait_ge(pool_consts, 4)
            pool.affine_select(out=spread_f, in_=spread_f, compare_op=ALU.not_equal, fill=1.0,
                               base=-HEADS, pattern=[[-1, HEADS], [0, KL]], channel_multiplier=1)
            pool.memset(q_rows["3"][:, :, :, :, 3, 0:2].rearrange("p g t s d -> p (g t s) d"), 1.0).then_inc(pool_consts, 1)
            pool.wait_ge(vec_consts, 2)

            taken = [0]

            def stages(at, j, front, back):
                if front is None or back is None:
                    base = [taken[0]]
                else:
                    base = [taken[0]]
                    taken[0] += POOL_STEPS * (TURNS - 1)
                own = [0]

                def link(ins):
                    own[0] += 1
                    ins.then_inc(pool_step, 1)
                    if front is None or back is None:
                        taken[0] += 1
                        pool.wait_ge(pool_step, taken[0])
                    else:
                        pool.wait_ge(pool_step, base[0] + j * POOL_STEPS + own[0])

                def key_blocks(l, i):
                    b = at[("stack_k" + l, 0, 0)]
                    heads_of = stack_head if l == "1" else stack_head3
                    pool.wait_ge(drained[b.region], b.is_drained(j))
                    for g in SEQS:
                        for s in range(STACKS):
                            last = pool.tensor_tensor(
                                out=k_blocks[l][:, g, s, :, :],
                                in0=k_stack[:, s, g * KL:(g + 1) * KL].unsqueeze(1).broadcast_to([P, 4, KL]),
                                in1=heads_of[:, :].unsqueeze(2).broadcast_to([P, 4, KL]), op=ALU.mult)
                        last.then_inc(k_blocks_ready[l], 1)

                def input_norm():
                    pool.wait_ge(ms_ready, front + 1)
                    pool.tensor_tensor(out=rs[:, :], in0=ms[:, :], in1=half_power[:, :], op=ALU.pow).then_inc(rs_ready, 1)

                def normalise(g):
                    pool.wait_ge(rsum_ready, (front * G + g) * TILES + 2)
                    pool.tensor_tensor(out=prob[:, g, 1, :].rearrange("p (h k) -> p h k", k=KL),
                                       in0=prob[:, g, 1, :].rearrange("p (h k) -> p h k", k=KL),
                                       in1=rsum["0"][:, g, 1, :].unsqueeze(2).broadcast_to([P, HEADS, KL]),
                                       op=ALU.mult).then_inc(norm_pool, 1)

                def power(l, i):
                    pool.wait_ge(var_ready[l], i + 1)
                    pool.tensor_tensor(out=rstd[l][:, :], in0=var[l][:, :], in1=half_power[:, :],
                                       op=ALU.pow).then_inc(rstd_ready[l], 1)

                def gain(l, i, gamma, beta, dst, done):
                    pool.wait_ge(z_ready[l], i + 1)
                    src = z[l]
                    if l == "4":
                        pool.wait_ge(stored, 16 * i + 16)
                    link(pool.tensor_tensor(out=dst, in0=src, in1=per_tile(row(gamma)), op=ALU.mult))
                    pool.tensor_tensor(out=dst, in0=dst, in1=per_tile(row(beta)), op=ALU.add).then_inc(done, 1)

                def x3_and_bias():
                    pool.wait_ge(x3_ready, (back + 1) * G)
                    pool.tensor_tensor(out=x3_bias[:, :, :], in0=x3[:, :, :, :].rearrange("p g t n -> p (g t) n"),
                                       in1=per_tile(row("b_out")), op=ALU.add).then_inc(x3_bias_ready, 1)

                return {"xn": input_norm, "key_blocks3": lambda: key_blocks("3", front), "key_blocks1": lambda: key_blocks("1", front),
                        **of_each("sums0", normalise), "x3_bias": x3_and_bias,
                        "stats1": lambda: power("1", front), "stats3": lambda: power("3", back), "stats4": lambda: power("4", back),
                        "norm1": lambda: gain("1", front, "ln_g", "ln_b", y_bias["1"][:, :, :], y_bias_ready["1"]),
                        "norm3": lambda: gain("3", back, "g1", "beta1", y_bias["3"][:, :, :], y_bias_ready["3"]),
                        "norm4": lambda: gain("4", back, "g2", "beta2", y_out[:, :, :], out_ready)}

            sections(pool, "gpsimd", stages)

        @block.scalar
        def _(act):
            for name, part, dst in (("wkT", 0, wkT), ("wvT", 0, wvT),
                                    ("wqk", 0, wqk[:, 0:8, :].rearrange("p (c a) n -> p a c n", a=2)),
                                    ("wqk", 1, wqk[:, 8:16, :].rearrange("p (c a) n -> p a c n", a=2)),
                                    ("wvo", 0, wvo[:, 0, :, :]), ("wvo", 1, wvo[:, 1, :, :])):
                b = pro[(name, 0, part)]
                act.wait_ge(written[b.region], b.is_written())
                src = psum[b.region][:, :].rearrange("p (c n) -> p c n", n=P)
                if name == "wqk":
                    src = psum[b.region][:, :].rearrange("p (a c n) -> p a c n", a=2, n=P)
                act.activation(dst, src, ACT.Copy).then_inc(drained[b.region], 1)

            def stages(at, j, front, back):
                def drain(key, dst, src):
                    b = at[key]
                    act.wait_ge(written[b.region], b.is_written(j))
                    act.activation(dst, src(psum[b.region]), ACT.Copy).then_inc(drained[b.region], 1)

                def input_squares():
                    act.wait_ge(x_loaded, 16 * (front + 1))
                    for n in range(G * TILES):
                        last = act.activation(xn[:, n // TILES, n % TILES, :], x_in[:, n // TILES, n % TILES, :], ACT.Square,
                                              accum_out=ss[:, n:n + 1])
                    last.then_inc(squares, 1)

                def keys0(half):
                    drain(("fold_k", 0, half), fold_k[:, :, 8 * half:8 * half + 8, :],
                          lambda ps: ps[:, :].rearrange("p (h g k) -> p g h k", g=G, k=KL))

                def stack(l):
                    if l == "3":
                        act.wait_ge(k_blocks_ready["1"], (front + 1) * G)
                    elif back is not None:
                        act.wait_ge(k_blocks_ready["3"], (back + 1) * G)
                    drain(("stack_k" + l, 0, 0), k_stack[:, :, :], lambda ps: ps[:, 0:SMALL].rearrange("p (s k) -> p s k", s=STACKS))

                def values0(g):
                    drain(("fold_v", g, 0), fold_v[:, g, :, :], lambda ps: ps[:, :].rearrange("p (c n) -> p c n", n=D))

                def exps0(g):
                    for t in TS:
                        b = at[("sub0", g, t)]
                        act.wait_ge(written[b.region], b.is_written(j))
                        act.activation(prob[:, g, t, :], psum[b.region][:, :], ACT.Exp).then_inc(drained[b.region], 1)

                def probabilities_T(g):
                    for t in TS:
                        drain(("p0T", g, t), probT["1"][:, g, :, t * P:(t + 1) * P], lambda ps: ps[:, :].rearrange("p (c q) -> p c q", q=P))

                def queries(l, g):
                    drain(("q%sT" % l, g, 0), q_stack[l][:, g, :, :], lambda ps: ps[:, :].rearrange("p (s q) -> p s q", q=QL))

                def exps_T(l, scale, g, half):
                    b = at[("st" + l, g, half)]
                    act.wait_ge(written[b.region], b.is_written(j))
                    act.activation(probT[l][:, g, 4 * half:4 * half + 4, :],
                                   psum[b.region][:, :].rearrange("p (c q) -> p c q", q=QL), ACT.Exp,
                                   scale=scale).then_inc(drained[b.region], 1)

                def outputs_T(l, g):
                    drain(("pv" + l, g, 0), attT[:, g, :, :], lambda ps: ps[:, 0:SMALL].rearrange("p (a q) -> p a q", q=QL))

                def hidden(l, g):
                    b = at[("h" + l, g, 0)]
                    act.wait_ge(written[b.region], b.is_written(j))
                    for c in range(CHUNKS_FF):
                        last = act.activation(hT[:, g, c, :], psum[b.region][:, c * QL:(c + 1) * QL],
                                              ACT.Gelu if l == "1" else ACT.Relu,
                                              bias=col(("b1_c%d" if l == "1" else "bff1_c%d") % c))
                    last.then_inc(drained[b.region], 1)

                def exps2(g):
                    act.wait_ge(nmax2_ready, back * G + g + 1)
                    b = at[("s2", g, 0)]
                    for t in TS:
                        last = act.activation(prob2[:, g, t, :], psum[b.region][:, t * KL:(t + 1) * KL], ACT.Exp,
                                              bias=nmax2[:, g, t:t + 1], accum_out=sums2[:, g, t:t + 1])
                    last.then_inc(drained[b.region], 1)

                def prob2_T(g):
                    drain(("p2T", g, 0), prob2T[:, g, :], lambda ps: ps[:, 0:P])

                named = {"ctxT": lambda: drain(("ctxT", 0, 0), ctxT[:, :], lambda ps: ps[:, 0:P]), "squares": input_squares, "fold_k_0": lambda: keys0(0), "fold_k_1": lambda: keys0(1),
                         **of_each("fold_v", values0), "stack_k1": lambda: stack("1"), "stack_k3": lambda: stack("3"),
                         **of_each("sub0", exps0), **of_each("p0T", probabilities_T), **of_each("s2", exps2), **of_each("p2T", prob2_T)}
                for l, scale in (("1", SCALE1), ("3", SCALE3)):
                    named.update(of_each("q%sT" % l, lambda g, l=l: queries(l, g)))
                    named.update(of_each("pv" + l, lambda g, l=l: outputs_T(l, g)))
                    named.update(of_each("h" + l, lambda g, l=l: hidden(l, g)))
                    for half in range(2):
                        for g in SEQS:
                            named["st%s_%d%d" % (l, g, half)] = lambda l=l, s=scale, g=g, half=half: exps_T(l, s, g, half)
                return named

            sections(act, "scalar", stages)

        @block.vector
        def _(dve):
            made = [0]

            def setup(ins):
                made[0] += 1
                ins.then_inc(setup_step, 1)
                dve.wait_ge(setup_step, made[0])

            def take(key, dst, src):
                b = pro[key]
                dve.wait_ge(written[b.region], b.is_written())
                dve.tensor_copy(dst, src(psum[b.region])).then_inc(drained[b.region], 1)

            dve.wait_ge(keys_in, 3 * 16)
            dve.tensor_scalar(wq0, wq0, col("norm_w"), None, ALU.mult).then_inc(wq_scaled, 1)
            dve.wait_ge(pool_consts, 5)
            setup(dve.tensor_copy(spread[:, :, :], spread_f))
            for half in range(2):
                for l in "13":
                    dve.memset(v_blocks[l][half * KL:(half + 1) * KL, :, :, 16 + half:17 + half], 1.0)
            setup(dve.reduce_sum(head_of[:, :], ident[:, :].rearrange("p (h r) -> p h r", r=DH), axis=AX.X))
            setup(dve.reduce_sum(stack_head[:, :], head_of[:, :].rearrange("p (a h) -> p h a", h=4), axis=AX.X))
            setup(dve.tensor_copy(stack_head3[:, :], stack_head[:, :]))
            dve.memset(stack_head3[96:128, :], 1.0).then_inc(vec_consts, 1)
            take(("wqT", 0, 0), wqT, lambda ps: ps[:, :].rearrange("p (c n) -> p c n", n=P))
            take(("l3_small_t", 0, 0), w8T[:, :, :], lambda ps: ps[0:DH, 0:3 * DH].rearrange("p (a n) -> p a n", n=DH))
            take(("l3_b", 0, 0), b8[:, :], lambda ps: ps[0:DH, 0:DH])
            b = pro[("l1_wT", 0, 0)]
            dve.wait_ge(written[b.region], b.is_written())
            dve.tensor_copy(l1_wT[:, :, :], psum[b.region][:, 0:3 * P].rearrange("p (a n) -> p a n", n=P))
            dve.tensor_copy(w1T[:, :, :], psum[b.region][:, 3 * P:7 * P].rearrange("p (a n) -> p a n", n=P)).then_inc(drained[b.region], 1)
            take(("l3_rep", 0, 0), rep8[:, :, :], lambda ps: ps[0:DH, 0:2 * D].rearrange("p (a n) -> p a n", n=D))
            b = pro[("l12_w", 0, 0)]
            dve.wait_ge(written[b.region], b.is_written())
            dve.tensor_copy(w2T[:, :, :], psum[b.region][:, 0:FF].rearrange("p (a n) -> p a n", n=P))
            dve.tensor_copy(wv2T[:, :], psum[b.region][:, FF:FF + D])
            dve.tensor_copy(wqk2[:, :], psum[b.region][:, FF + D:FF + 2 * D])
            dve.tensor_copy(c2[:, 0:2], psum[b.region][:, FF + 2 * D:FF + 2 * D + 2])
            dve.tensor_copy(c2[0:1, 2:3], psum[b.region][0:1, FF + 2 * D + 2:FF + 2 * D + 3]).then_inc(drained[b.region], 1)
            b = pro[("l3_full", 0, 0)]
            dve.wait_ge(written[b.region], b.is_written())
            for a in range(2):
                last = dve.tensor_tensor(out=l3_full[:, a, :].rearrange("p (h d) -> p h d", d=DH),
                                         in0=psum[b.region][:, a * D:(a + 1) * D].rearrange("p (h d) -> p h d", d=DH),
                                         in1=head_of[:, :].unsqueeze(2).broadcast_to([P, HEADS, DH]), op=ALU.mult)
            last.then_inc(drained[b.region], 1)
            dve.wait_ge(drained[b.region], b.is_drained())
            dve.wait_ge(weights_in, 16 * N_WEIGHTS)
            dve.tensor_tensor(out=row("ln_b"), in0=row("ln_b"), in1=row("b2_1"), op=ALU.add)
            setup(dve.tensor_tensor(out=row("beta1"), in0=row("beta1"), in1=row("b_ff2"), op=ALU.add))
            dve.sem_inc(vec_consts, 1)

            taken = [0]

            def stages(at, j, front, back):
                looped = front is not None and back is not None
                base, own = taken[0], [0]
                if looped:
                    taken[0] += VEC_STEPS * (TURNS - 1)
                vec_counts.append(own)

                def link(ins):
                    own[0] += 1
                    ins.then_inc(step, 1)
                    if looped:
                        dve.wait_ge(step, base + j * VEC_STEPS + own[0])
                    else:
                        taken[0] += 1
                        dve.wait_ge(step, taken[0])

                def opened(key):
                    b = at[key]
                    dve.wait_ge(written[b.region], b.is_written(j))
                    return psum[b.region], drained[b.region], b

                def drain(key, dst, src):
                    ps, free, _ = opened(key)
                    dve.tensor_copy(dst, src(ps)).then_inc(free, 1)

                def drain_T(name, dst):
                    return of_each(name, lambda g: drain((name, g, 0), dst[:, g, :], lambda ps: ps[:, 0:QL]))

                def tiles_of(ps):
                    return ps[:, 0:QL].rearrange("p (t n) -> p t n", n=D)

                def key_rows(l):
                    kv = kf[l][:, :].rearrange("p (s r) -> p s r", r=32)
                    for part in (0, 2):
                        last = dve.tensor_copy(k_rows[l][:, :, part, :].bitcast(f32r), kv)
                    if l == "3":
                        last = dve.tensor_copy(k_rows[l][:, :, 3, 0:1].bitcast(f32r), pen[:, :].unsqueeze(1).broadcast_to([P, STACKS, 1]))
                    link(last)
                    for part in ((1, 3) if l == "1" else (1,)):
                        last = dve.tensor_tensor(out=k_rows[l][:, :, part, :].bitcast(f32r), in0=kv,
                                                 in1=k_rows[l][:, :, 0, :], op=ALU.subtract)
                    if l == "3":
                        last = dve.tensor_tensor(out=k_rows[l][:, :, 3, 1:2].bitcast(f32r), in0=pen[:, :].unsqueeze(1).broadcast_to([P, STACKS, 1]),
                                                 in1=k_rows[l][:, :, 3, 0:1], op=ALU.subtract)
                    last.then_inc(k_rows_ready[l], 1)

                def value_blocks(l, ps):
                    for half in range(2):
                        rows_of, cols_of = slice(half * KL, (half + 1) * KL), slice(half * DH, (half + 1) * DH)
                        dst = v_blocks[l][rows_of, :, :, cols_of]
                        src = ps[rows_of, 0:P].rearrange("p (g c d) -> p g c d", g=G, d=DH)
                        if l == "1":
                            for g in SEQS:
                                last = dve.tensor_tensor(out=dst[:, g, :, :], in0=src[:, g, :, :],
                                                         in1=row("bv1")[rows_of, :].rearrange("p (c a d) -> p c a d", a=2, d=DH)[:, :, half, :],
                                                         op=ALU.add)
                        else:
                            last = dve.tensor_copy(dst, src)
                    return last

                def context3():
                    ps, free, b = opened(("ctx_k3", 0, 0))
                    dve.tensor_scalar(kf["3"][:, :], ps[:, 0:D], m01[:, 0:1], None, ALU.mult)
                    dve.tensor_scalar(fold2[:, :], ps[:, D:2 * D], c2[:, 0:1], None, ALU.add)
                    dve.tensor_scalar(s2_row[:, :], ps[0:1, 2 * D:3 * D], c2[0:1, 2:3], None, ALU.add).then_inc(free, 1)
                    dve.wait_ge(free, b.is_drained(j))
                    key_rows("3")
                    ps, free, b = opened(("ctx_v3", 0, 0))
                    value_blocks("3", ps)
                    dve.tensor_tensor(out=v2[:, :, :], in0=ps[:, P:P + G * D].rearrange("p (g n) -> p g n", n=D),
                                      in1=row("bv2").unsqueeze(1).broadcast_to([P, G, D]), op=ALU.add).then_inc(free, 1)

                def mask():
                    if back is not None:
                        dve.wait_ge(k_rows_ready["3"], back + 1)
                    dve.wait_ge(c_loaded, 32 * (front + 1))
                    dve.tensor_scalar(m01[:, :], m_in[:, :], 0.0, None, ALU.not_equal)
                    link(dve.tensor_scalar(pen[:, :], m_in[:, :], 0.0, MASK_FILL, ALU.is_equal, ALU.mult))
                    dve.sem_inc(mask_read, 1)

                def mean_squares():
                    dve.wait_ge(squares, front + 1)
                    dve.tensor_scalar(ms[:, :], ss[:, :], 1.0 / D, RMS_EPS, ALU.mult, ALU.add).then_inc(ms_ready, 1)

                def context1():
                    ps, free, b = opened(("ctx_k1", 0, 0))
                    dve.tensor_tensor(out=kf["1"][:, :], in0=ps[:, 0:D], in1=row("bk1"), op=ALU.add).then_inc(free, 1)
                    dve.wait_ge(free, b.is_drained(j))
                    key_rows("1")
                    ps, free, b = opened(("ctx_v1", 0, 0))
                    value_blocks("1", ps).then_inc(free, 1)

                def input_over_rms():
                    dve.wait_ge(rs_ready, front + 1)
                    for g in SEQS:
                        for t in TS:
                            last = dve.tensor_scalar(xn[:, g, t, :], x_in[:, g, t, :], rs[:, g * TILES + t:g * TILES + t + 1], None, ALU.mult)
                        last.then_inc(xn_ready, 1)

                def tile_max(key, l, g, t):
                    ps, free, _ = opened(key)
                    return dve.tensor_reduce(out=nmax[l][:, g, t, :], in_=ps[:, :].rearrange("p (h k) -> p h k", k=KL),
                                             op=ALU.max, axis=AX.X, negate=True), free

                def max_split(l, buf, g):
                    link(dve.tensor_copy(nmax_hl[buf][:, g, :, 0, :].bitcast(f32r), nmax[buf][:, g, :, :]))
                    dve.tensor_tensor(out=nmax_hl[buf][:, g, :, 1, :].bitcast(f32r), in0=nmax[buf][:, g, :, :],
                                      in1=nmax_hl[buf][:, g, :, 0, :], op=ALU.subtract).then_inc(nmax_ready[l], 1)

                def maxima0(g):
                    tile_max(("s0", g, 0), "1", g, 0)
                    link(tile_max(("s0", g, 1), "1", g, 1)[0])
                    max_split("0", "1", g)

                def maxima(l, g):
                    for t in TS:
                        ins, free = tile_max(("s" + l, g, t), l, g, t)
                        ins.then_inc(free, 1)
                    b = at[("s" + l, g, 1)]
                    dve.wait_ge(drained[b.region], b.is_drained(j))
                    max_split(l, l, g)

                def drain_maxT(l, buf, g):
                    drain(("max" + l, g, 0), nmaxT[buf][:, g, :], lambda ps: ps[0:2 * HEADS, 0:QL])

                def sums0(g):
                    for t in TS:
                        b = at[("s0", g, t)]
                        dve.wait_ge(drained[b.region], b.is_drained(j))
                        pv = prob[:, g, t, :].rearrange("p (h k) -> p h k", k=KL)
                        link(dve.reduce_sum(sums[:, g, t, :], pv, axis=AX.X))
                        dve.reciprocal(rsum["0"][:, g, t, :], sums[:, g, t, :]).then_inc(rsum_ready, 1)
                    dve.tensor_tensor(out=prob[:, g, 0, :].rearrange("p (h k) -> p h k", k=KL),
                                      in0=prob[:, g, 0, :].rearrange("p (h k) -> p h k", k=KL),
                                      in1=rsum["0"][:, g, 0, :].unsqueeze(2).broadcast_to([P, HEADS, KL]),
                                      op=ALU.mult).then_inc(norm_vec, 1)

                def output0(g):
                    ps, free, b = opened(("o0", g, 0))
                    dve.tensor_tensor(out=x1[:, g, :, :], in0=tiles_of(ps), in1=x_in[:, g, :, :], op=ALU.add).then_inc(free, 1)
                    dve.wait_ge(free, b.is_drained(j))
                    dve.sem_inc(x1_ready, 1)

                def query_rows(l, src, g):
                    qv = src[:, g, :, :].rearrange("p t (s r) -> p (t s) r", r=32)
                    dst = q_rows[l][:, g, :, :, :, :].rearrange("p t s a r -> p (t s) a r")
                    lo = 4 if l == "1" else 3
                    link(dve.tensor_copy(dst[:, :, 0:2, :].bitcast(f32r), qv.unsqueeze(2).broadcast_to([P, 8, 2, 32])))
                    dve.tensor_tensor(out=dst[:, :, 2:lo, :].bitcast(f32r), in0=qv.unsqueeze(2).broadcast_to([P, 8, lo - 2, 32]),
                                      in1=dst[:, :, 0:lo - 2, :], op=ALU.subtract).then_inc(q_rows_ready[l], 1)

                def queries1(g):
                    ps, free, b = opened(("q1", g, 0))
                    dve.tensor_tensor(out=qf[:, g, :, :], in0=tiles_of(ps),
                                      in1=row("bq1").unsqueeze(1).broadcast_to([P, TILES, D]), op=ALU.add).then_inc(free, 1)
                    dve.wait_ge(free, b.is_drained(j))
                    query_rows("1", qf, g)

                def statistics(l):
                    for n in range(G * TILES):
                        last = dve.bn_stats(stats[l][:, n, :], pre[l][:, n // TILES, n % TILES, :])
                    link(last)
                    dve.sem_inc(stats_written, 1)
                    for n in range(G * TILES):
                        last = dve.bn_aggr(mv[l][:, n, :], stats[l][:, n, :])
                    link(last)
                    dve.tensor_scalar(var[l][:, :], mv[l][:, :, 1], LN_EPS, None, ALU.add).then_inc(var_ready[l], 1)

                def norm(l, i):
                    dve.wait_ge(rstd_ready[l], i + 1)
                    for n in range(G * TILES):
                        src = pre[l][:, n // TILES, n % TILES, :]
                        last = dve.tensor_scalar(src, src, mv[l][:, n, 0:1], rstd[l][:, n:n + 1],
                                                 ALU.subtract, ALU.mult)
                    last.then_inc(z_ready[l], 1)

                def attention(l, g):
                    ps, free, b = opened(("at" + l, g, 0))
                    pv = ps[:, 0:SMALL].rearrange("p (n m) -> p n m", m=32)
                    link(dve.reciprocal(rsum[l][:, g, :, :].rearrange("p t (c a) -> p (t c) a", a=2), pv[:, :, 16:18]))
                    dve.tensor_tensor(out=att[l][:, g, :, :].rearrange("p t (c a d) -> p (t c) a d", a=2, d=DH),
                                      in0=pv[:, :, 0:16].rearrange("p n (a d) -> p n a d", d=DH),
                                      in1=rsum[l][:, g, :, :].rearrange("p t (c a) -> p (t c) a", a=2).unsqueeze(3).broadcast_to([P, 16, 2, DH]),
                                      op=ALU.mult).then_inc(free, 1)
                    dve.wait_ge(free, b.is_drained(j))
                    if l == "3":
                        dve.sem_inc(att_ready, 1)
                    else:
                        link(dve.tensor_tensor(out=pre[l][:, g, :, :], in0=att[l][:, g, :, :], in1=x1[:, g, :, :], op=ALU.add))

                def drain_yT(l, gamma, beta, g):
                    ps, free, b = opened(("y%sT" % l, g, 0))
                    dve.tensor_scalar(xT["3"][:, g, :], ps[:, 0:QL], col(gamma), col(beta), ALU.mult, ALU.add).then_inc(free, 1)

                def feed_forward_out(l, g):
                    dve.wait_ge(y_bias_ready[l], back + 1)
                    ps, free, b = opened(("f" + l, g, 0))
                    dst = x2 if l == "1" else pre["4"]
                    dve.tensor_tensor(out=dst[:, g, :, :], in0=tiles_of(ps), in1=y_bias[l][:, g * TILES:(g + 1) * TILES, :],
                                      op=ALU.add).then_inc(free, 1)
                    dve.wait_ge(free, b.is_drained(j))
                    if l == "1":
                        dve.sem_inc(x2_ready, 1)

                def maxima2(g):
                    ps, _, b = opened(("s2", g, 0))
                    dve.tensor_reduce(out=nmax2[:, g, :], in_=ps[:, 0:TILES * KL].rearrange("p (t k) -> p t k", k=KL),
                                      op=ALU.max, axis=AX.X, negate=True).then_inc(nmax2_ready, 1)

                def inverse_sums2():
                    for g in SEQS:
                        b = at[("s2", g, 0)]
                        dve.wait_ge(drained[b.region], b.is_drained(j))
                        last = dve.reciprocal(rsum2[:, g, :], sums2[:, g, :])
                    link(last)

                def output2(g):
                    ps, free, b = opened(("o2", g, 0))
                    for t in TS:
                        last = dve.scalar_tensor_tensor(out=x3[:, g, t, :], in0=ps[:, t * 512:t * 512 + D],
                                                        scalar=rsum2[:, g, t:t + 1], in1=x2[:, g, t, :],
                                                        op0=ALU.mult, op1=ALU.add)
                    last.then_inc(free, 1)
                    dve.wait_ge(free, b.is_drained(j))
                    dve.sem_inc(x3_ready, 1)
                    query_rows("3", x3, g)

                def out3(g):
                    dve.wait_ge(x3_bias_ready, back + 1)
                    ps, free, b = opened(("w3", g, 0))
                    dve.tensor_tensor(out=pre["3"][:, g, :, :], in0=tiles_of(ps), in1=x3_bias[:, g * TILES:(g + 1) * TILES, :],
                                      op=ALU.add).then_inc(free, 1)
                    dve.wait_ge(free, b.is_drained(j))

                named = {"ctx3": context3, "mask": mask, "squares": mean_squares, "ctx1": context1, "xn": input_over_rms,
                         **drain_T("xnT", xT["1"]), **drain_T("x1T", xT["1"]), **drain_T("x2T", xT["3"]), **drain_T("a3T", xT["3"]),
                         **of_each("y1T", lambda g: drain_yT("1", "ln_gc", "ln_bc", g)),
                         **of_each("y3T", lambda g: drain_yT("3", "g1c", "beta1c", g)),
                         **of_each("s0", maxima0), **of_each("max0", lambda g: drain_maxT("0", "1", g)), **of_each("sums0", sums0),
                         **of_each("o0", output0), **of_each("q1", queries1), **of_each("s2", maxima2), "rsum2": inverse_sums2,
                         **of_each("o2", output2), **of_each("w3", out3),
                         "norm1": lambda: norm("1", front), "norm3": lambda: norm("3", back), "norm4": lambda: norm("4", back),
                         "stats1": lambda: statistics("1"), "stats3": lambda: statistics("3"), "stats4": lambda: statistics("4")}
                for l in "13":
                    named.update(of_each("s" + l, lambda g, l=l: maxima(l, g)))
                    named.update(of_each("max" + l, lambda g, l=l: drain_maxT(l, l, g)))
                    named.update(of_each("at" + l, lambda g, l=l: attention(l, g)))
                    named.update(of_each("f" + l, lambda g, l=l: feed_forward_out(l, g)))
                return named

            vec_counts = []
            sections(dve, "vector", stages)
            assert vec_counts[1][0] == VEC_STEPS, vec_counts

        @block.tensor
        def _(pe):
            mm = nc.tensor.matmul

            def open_pro(key):
                b = pro[key]
                if b.drains:
                    pe.wait_ge(drained[b.region], b.is_free())
                return psum[b.region], written[b.region]

            def pro_ready(key):
                b = pro[key]
                pe.wait_ge(drained[b.region], b.is_drained())

            pe.wait_ge(pool_consts, 2)
            pe.wait_ge(keys_in, 3 * 16)
            def transposes(key, src):
                ps, full = open_pro(key)
                for c, s in enumerate(src):
                    last = nc.tensor.transpose(ps[:, c * P:(c + 1) * P], s, ident[:, :])
                last.then_inc(full, 1)

            transposes(("wkT", 0, 0), [wk0[:, c * P:(c + 1) * P] for c in range(PAIRS)])
            pe.wait_ge(wq_scaled, 1)
            transposes(("wqT", 0, 0), [wq0[:, c * P:(c + 1) * P] for c in range(PAIRS)])
            pe.wait_ge(values_in, 2 * 16)
            transposes(("wvT", 0, 0), [wv0[:, c * P:(c + 1) * P] for c in range(PAIRS)])
            pro_ready(("wkT", 0, 0))
            pro_ready(("wqT", 0, 0))
            for part in range(2):
                ps, full = open_pro(("wqk", 0, part))
                for n in range(8):
                    h = 8 * part + n
                    r = slice((h % 2) * DKV, (h % 2 + 1) * DKV)
                    at = (h % 2) * 4 + n // 2
                    last = mm(ps[:, at * P:(at + 1) * P], wkT[r, h // 2, :], wqT[r, h // 2, :], start=True, stop=True)
                last.then_inc(full, 1)
            pro_ready(("wvT", 0, 0))
            for part in range(2):
                ps, full = open_pro(("wvo", 0, part))
                r = slice(part * DKV, (part + 1) * DKV)
                for c in range(PAIRS):
                    last = mm(ps[:, c * D:(c + 1) * D], wvT[r, c, :], wo0[r, c, :], start=True, stop=True)
                last.then_inc(full, 1)
            pe.wait_ge(pool_consts, 5)
            pe.wait_ge(weights_in, 16 * N_WEIGHTS)
            ps, full = open_pro(("l3_small_t", 0, 0))
            for a in range(3):
                last = mm(ps[0:DH, a * DH:(a + 1) * DH], w8[:, a, :], ident[0:DH, 0:DH], start=True, stop=True)
            last.then_inc(full, 1)
            pro_ready(("l3_small_t", 0, 0))
            ps, full = open_pro(("l3_b", 0, 0))
            mm(ps[0:DH, 0:DH], w8T[:, 1, :], w8T[:, 0, :], start=True, stop=True).then_inc(full, 1)
            transposes(("l1_wT", 0, 0), [wq1, wk1, wv1] + [w1_1[:, c, :] for c in range(CHUNKS_FF)])
            pro_ready(("l3_b", 0, 0))
            ps, full = open_pro(("l3_rep", 0, 0))
            mm(ps[0:DH, 0:D], b8[:, :], rep_id[:, :, :], start=True, stop=True)
            mm(ps[0:DH, D:2 * D], w8T[:, 2, :], rep_id[:, :, :], start=True, stop=True).then_inc(full, 1)
            ps, full = open_pro(("l12_w", 0, 0))
            for c in range(CHUNKS_FF):
                nc.tensor.transpose(ps[:, c * P:(c + 1) * P], w2_1[:, c * P:(c + 1) * P], ident[:, :])
            nc.tensor.transpose(ps[:, FF:FF + D], wv2, ident[:, :])
            mm(ps[:, FF + D:FF + 2 * D], wk2, wq2, start=True, stop=True)
            mm(ps[:, FF + 2 * D:FF + 2 * D + 1], wq2, col("bk2"), start=True, stop=True)
            mm(ps[:, FF + 2 * D + 1:FF + 2 * D + 2], wk2, col("bq2"), start=True, stop=True)
            mm(ps[0:1, FF + 2 * D + 2:FF + 2 * D + 3], col("bq2"), col("bk2"), start=True, stop=True).then_inc(full, 1)
            pro_ready(("l3_rep", 0, 0))
            ps, full = open_pro(("l3_full", 0, 0))
            mm(ps[:, 0:2 * D], rep_id[:, :, :].rearrange("p h d -> p (h d)"), rep8[:, :, :], start=True, stop=True).then_inc(full, 1)
            pe.wait_ge(vec_consts, 2)
            pro_ready(("wvo", 0, 1))

            def stages(at, j, front, back):
                def open_(key):
                    b = at[key]
                    pe.wait_ge(drained[b.region], b.is_free(j))
                    return psum[b.region], written[b.region]

                def ready(key):
                    b = at[key]
                    pe.wait_ge(drained[b.region], b.is_drained(j))

                def transpose_tiles(key, src):
                    ps, full = open_(key)
                    for t in TS:
                        last = nc.tensor.transpose(ps[:, t * P:(t + 1) * P], src(t), ident[:, :])
                    last.then_inc(full, 1)

                def tiles_times(name, after, lhs, rhs, g):
                    ready((after, g, 0))
                    ps, full = open_((name, g, 0))
                    for t in TS:
                        last = mm(ps[:, t * D:(t + 1) * D], lhs[:, g, t * P:(t + 1) * P], rhs, start=True, stop=True)
                    last.then_inc(full, 1)

                def values_of_context(l, w, ps):
                    for g in SEQS:
                        for half in range(2):
                            last = mm(ps[half * KL:(half + 1) * KL, g * KL:(g + 1) * KL], ctxT[:, g * KL:(g + 1) * KL],
                                      w.rearrange("p (c a d) -> p c a d", a=2, d=DH)[:, :, half, :], start=True, stop=True)
                    return last

                def stack_keys(l, i):
                    pe.wait_ge(k_rows_ready[l], i + 1)
                    ps, full = open_(("stack_k" + l, 0, 0))
                    for s in range(STACKS):
                        last = nc.tensor.transpose(ps[:, s * P:(s + 1) * P], k_rows[l][:, s, :, :].rearrange("p a r -> p (a r)"), ident[:, :])
                    last.then_inc(full, 1)

                def context3():
                    ps, full = open_(("ctx_k3", 0, 0))
                    mm(ps[:, 0:D], ctxT[:, :], l3_full[:, 0, :], start=True, stop=True)
                    mm(ps[:, D:2 * D], wqk2[:, :], ctxT[:, :], start=True, stop=True)
                    mm(ps[0:1, 2 * D:3 * D], c2[:, 1:2], ctxT[:, :], start=True, stop=True).then_inc(full, 1)
                    ps, full = open_(("ctx_v3", 0, 0))
                    values_of_context("3", l3_full[:, 1, :], ps)
                    for g in SEQS:
                        for half in range(2):
                            last = mm(ps[half * KL:(half + 1) * KL, P + g * D:P + (g + 1) * D], ctxT[:, g * KL:(g + 1) * KL],
                                      wv2T[:, :], start=True, stop=True)
                    last.then_inc(full, 1)

                def context_T():
                    pe.wait_ge(c_loaded, 32 * (front + 1))
                    b = at[("ctxT", 0, 0)]
                    ps, full = open_(("ctxT", 0, 0))
                    nc.tensor.transpose(ps[:, 0:P], c_in[:, :], ident[:, :]).then_inc(full, 1)
                    pe.wait_ge(full, b.is_written(j))
                    pe.sem_inc(ctx_read, 1)
                    ready(("ctxT", 0, 0))

                def keys0(half):
                    ps, full = open_(("fold_k", 0, half))
                    for n in range(8):
                        last = mm(ps[:, n * P:(n + 1) * P], wqk[:, 8 * half + n, :], ctxT[:, :], start=True, stop=True)
                    last.then_inc(full, 1)

                def context1():
                    ps, full = open_(("ctx_k1", 0, 0))
                    mm(ps[:, 0:D], ctxT[:, :], l1_wT[:, 1, :], start=True, stop=True).then_inc(full, 1)
                    ps, full = open_(("ctx_v1", 0, 0))
                    values_of_context("1", l1_wT[:, 2, :], ps).then_inc(full, 1)

                def values0(g):
                    ps, full = open_(("fold_v", g, 0))
                    for c in range(0, PAIRS, 4):
                        for half in range(2):
                            last = mm(ps[half * KL:(half + 1) * KL, c * D:(c + 4) * D], ctxT[:, g * KL:(g + 1) * KL],
                                      wvo[:, half, c:c + 4, :], start=True, stop=True)
                    last.then_inc(full, 1)

                def transpose_maxima(l, buf, g, i):
                    pe.wait_ge(nmax_ready[l], i * G + g + 1)
                    ps, full = open_(("max" + l, g, 0))
                    for t in TS:
                        last = nc.tensor.transpose(ps[0:2 * HEADS, t * P:(t + 1) * P],
                                                   nmax_hl[buf][:, g, t, :, :].rearrange("p a h -> p (a h)"), ident[:, :])
                    last.then_inc(full, 1)

                def scores0(g):
                    ready(("fold_k", 0, 1))
                    ready(("xnT", g, 0))
                    for t in TS:
                        ps, full = open_(("s0", g, t))
                        for c in range(0, HEADS, 8):
                            last = mm(ps[:, c * KL:(c + 8) * KL], xT["1"][:, g, t * P:(t + 1) * P], fold_k[:, g, c:c + 8, :],
                                      start=True, stop=True)
                        last.then_inc(full, 1)

                def less_max0(g):
                    ready(("max0", g, 0))
                    for t in TS:
                        b = at[("sub0", g, t)]
                        for c in range(0, HEADS, 8):
                            last = mm(psum[b.region][:, c * KL:(c + 8) * KL], nmaxT["1"][:, g, t * P:(t + 1) * P], spread[:, c:c + 8, :],
                                      start=False, stop=True, skip_group_check=True)
                        last.then_inc(written[b.region], 1)

                def probabilities_T(g):
                    for t in TS:
                        if t == 0:
                            pe.wait_ge(norm_vec, front * G + g + 1)
                        else:
                            pe.wait_ge(norm_pool, front * G + g + 1)
                        ps, full = open_(("p0T", g, t))
                        for c in range(PAIRS):
                            last = nc.tensor.transpose(ps[:, c * P:(c + 1) * P], prob[:, g, t, c * P:(c + 1) * P], ident[:, :])
                        last.then_inc(full, 1)

                def output0(g):
                    ready(("p0T", g, 1))
                    ready(("fold_v", g, 0))
                    ps, full = open_(("o0", g, 0))
                    for t in TS:
                        for c in range(PAIRS):
                            last = mm(ps[:, t * D:(t + 1) * D], probT["1"][:, g, c, t * P:(t + 1) * P], fold_v[:, g, c, :],
                                      start=(c == 0), stop=(c == PAIRS - 1))
                    last.then_inc(full, 1)

                def stack_queries(l, i, g):
                    pe.wait_ge(q_rows_ready[l], i * G + g + 1)
                    ps, full = open_(("q%sT" % l, g, 0))
                    for s in range(STACKS):
                        for t in TS:
                            last = nc.tensor.transpose(ps[:, s * QL + t * P:s * QL + (t + 1) * P],
                                                       q_rows[l][:, g, t, s, :, :].rearrange("p a r -> p (a r)"), ident[:, :])
                    last.then_inc(full, 1)

                def scores(l, i, g):
                    ready(("q%sT" % l, g, 0))
                    pe.wait_ge(k_blocks_ready[l], i * G + g + 1)
                    for t in TS:
                        ps, full = open_(("s" + l, g, t))
                        fill = l == "1" and t == 0
                        for bank in range(2):
                            if fill:
                                mm(ps[:, bank * 512:(bank + 1) * 512], ident_bf[0:KL, :],
                                   causal[:, 0, :].unsqueeze(1).broadcast_to([KL, 8, KL]), start=True, stop=False,
                                   skip_group_check=True)
                            for s in (2 * bank, 2 * bank + 1):
                                last = mm(ps[:, s * QL:(s + 1) * QL], q_stack[l][:, g, s, t * P:(t + 1) * P],
                                          k_blocks[l][:, g, s, :, :], start=(s % 2 == 0 and not fill), stop=True,
                                          skip_group_check=True)
                        last.then_inc(full, 1)

                def scores_T(l, g, half):
                    if half == 0:
                        ready(("max" + l, g, 0))
                    ps, full = open_(("st" + l, g, half))
                    for c in range(4):
                        pair = 4 * half + c
                        s, a = pair // 2, pair % 2
                        o = ps[:, c * QL:(c + 1) * QL]
                        mm(o, k_blocks[l][:, g, s, 2 * a:2 * a + 2, :], q_stack[l][:, g, s, :], start=(c % 2 == 0), stop=False,
                           skip_group_check=True)
                        if l == "1":
                            mm(ps[:, c * QL:c * QL + KL], causal[:, :, :], ident_bf[0:KL, 0:KL], start=False, stop=False,
                               skip_group_check=True)
                        last = mm(o, spread[:, 2 * pair:2 * pair + 2, :], nmaxT[l][:, g, :], start=False, stop=True,
                                  skip_group_check=True)
                    last.then_inc(full, 1)

                def values(l, g):
                    ready(("st" + l, g, 0))
                    ready(("st" + l, g, 1))
                    ps, full = open_(("pv" + l, g, 0))
                    for half in range(2):
                        for c in range(4):
                            last = mm(ps[32 * c:32 * c + 32, half * QL:(half + 1) * QL], v_blocks[l][:, g, 4 * half + c, :],
                                      probT[l][:, g, 4 * half + c, :], start=True, stop=True)
                    last.then_inc(full, 1)

                def attention(l, g):
                    ready(("pv" + l, g, 0))
                    ps, full = open_(("at" + l, g, 0))
                    for t in TS:
                        for half in range(2):
                            last = nc.tensor.transpose(ps[:, (t * 2 + half) * P:(t * 2 + half + 1) * P],
                                                       attT[:, g, half, t * P:(t + 1) * P], ident[:, :])
                    last.then_inc(full, 1)

                def x_T(name, src, is_ready, i, g):
                    pe.wait_ge(is_ready, i * G + g + 1)
                    transpose_tiles((name, g, 0), lambda t: src[:, g, t, :])

                def y_T(l, i, g):
                    pe.wait_ge(z_ready[l], i + 1)
                    transpose_tiles(("y%sT" % l, g, 0), lambda t: z[l][:, g * TILES + t, :])

                def hidden(l, up, g):
                    ready(("y%sT" % l, g, 0))
                    ps, full = open_(("h" + l, g, 0))
                    for c in range(CHUNKS_FF):
                        last = mm(ps[:, c * QL:(c + 1) * QL], up(c), xT["3"][:, g, :], start=True, stop=True)
                    last.then_inc(full, 1)

                def down(l, w, g):
                    ready(("h" + l, g, 0))
                    ps, full = open_(("f" + l, g, 0))
                    for t in TS:
                        for c in range(CHUNKS_FF):
                            last = mm(ps[:, t * D:(t + 1) * D], hT[:, g, c, t * P:(t + 1) * P], w[:, c, :],
                                      start=(c == 0), stop=(c == CHUNKS_FF - 1))
                    last.then_inc(full, 1)

                def scores2(g):
                    ready(("x2T", g, 0))
                    ps, full = open_(("s2", g, 0))
                    for t in TS:
                        o = ps[:, t * KL:(t + 1) * KL]
                        mm(o, xT["3"][:, g, t * P:(t + 1) * P], fold2[:, g * KL:(g + 1) * KL], start=True, stop=False)
                        last = mm(o, ones_row[0:1, :], s2_row[0:1, g * KL:(g + 1) * KL], start=False, stop=True)
                    last.then_inc(full, 1)

                def prob2_T(g):
                    ready(("s2", g, 0))
                    ps, full = open_(("p2T", g, 0))
                    nc.tensor.transpose(ps[:, 0:P], prob2[:, g, :, :].rearrange("p t k -> p (t k)"), ident[:, :]).then_inc(full, 1)

                def output2(g):
                    ready(("p2T", g, 0))
                    ps, full = open_(("o2", g, 0))
                    for t in TS:
                        last = mm(ps[:, t * 512:t * 512 + D], prob2T[t * KL:(t + 1) * KL, g, :], v2[t * KL:(t + 1) * KL, g, :],
                                  start=True, stop=True)
                    last.then_inc(full, 1)

                def input_T(g):
                    pe.wait_ge(xn_ready, front * G + g + 1)
                    transpose_tiles(("xnT", g, 0), lambda t: xn[:, g, t, :])

                named = {"ctx3": context3, "stack_k3": lambda: stack_keys("3", front), "ctxT": context_T,
                         "fold_k_0": lambda: keys0(0), "fold_k_1": lambda: keys0(1), "ctx1": context1,
                         "stack_k1": lambda: stack_keys("1", front), **of_each("fold_v", values0), **of_each("xnT", input_T),
                         **of_each("s0", scores0), **of_each("max0", lambda g: transpose_maxima("0", "1", g, front)),
                         **of_each("sub0", less_max0), **of_each("p0T", probabilities_T), **of_each("o0", output0),
                         **of_each("x1T", lambda g: x_T("x1T", x1, x1_ready, front, g)),
                         **of_each("q1", lambda g: tiles_times("q1", "x1T", xT["1"], l1_wT[:, 0, :], g)),
                         **of_each("h1", lambda g: hidden("1", lambda c: w1T[:, c, :], g)), **of_each("f1", lambda g: down("1", w2T, g)),
                         **of_each("x2T", lambda g: x_T("x2T", x2, x2_ready, back, g)),
                         **of_each("s2", scores2), **of_each("p2T", prob2_T), **of_each("o2", output2),
                         **of_each("a3T", lambda g: x_T("a3T", att["3"], att_ready, back, g)),
                         **of_each("w3", lambda g: tiles_times("w3", "a3T", xT["3"], w_out[:, :], g)),
                         **of_each("h3", lambda g: hidden("3", lambda c: w_ff1[:, c * P:(c + 1) * P], g)),
                         **of_each("f3", lambda g: down("3", w_ff2, g))}
                for l, i in (("1", front), ("3", back)):
                    named.update(of_each("q%sT" % l, lambda g, l=l, i=i: stack_queries(l, i, g)))
                    named.update(of_each("s" + l, lambda g, l=l, i=i: scores(l, i, g)))
                    named.update(of_each("max" + l, lambda g, l=l, i=i: transpose_maxima(l, l, g, i)))
                    named.update(of_each("pv" + l, lambda g, l=l: values(l, g)))
                    named.update(of_each("at" + l, lambda g, l=l: attention(l, g)))
                    named.update(of_each("y%sT" % l, lambda g, l=l: y_T(l, back, g)))
                    for half in range(2):
                        for g in SEQS:
                            named["st%s_%d%d" % (l, g, half)] = lambda l=l, g=g, half=half: scores_T(l, g, half)
                return named

            sections(pe, "tensor", stages)


INPUTS = ["x", "ctx_1024", "mask_Bx1x1xS2_if1",
          "L0_xattn_wq", "L0_xattn_wk", "L0_xattn_wv", "L0_xattn_wo", "L0_xattn_norm_w",
          "L1_xattn_Wq", "L1_xattn_bq", "L1_xattn_Wk", "L1_xattn_bk", "L1_xattn_Wv", "L1_xattn_bv",
          "L1_xattn_W1", "L1_xattn_b1", "L1_xattn_W2", "L1_xattn_b2", "L1_xattn_ln_g", "L1_xattn_ln_b",
          "L2_xattn_Wq", "L2_xattn_bq", "L2_xattn_Wk", "L2_xattn_bk", "L2_xattn_Wv", "L2_xattn_bv",
          "L3_xattn_wv", "L3_xattn_wk", "L3_xattn_wq", "L3_xattn_w_out", "L3_xattn_b_out", "L3_xattn_g1",
          "L3_xattn_beta1", "L3_xattn_w_ff1", "L3_xattn_b_ff1", "L3_xattn_w_ff2", "L3_xattn_b_ff2",
          "L3_xattn_g2", "L3_xattn_beta2"]


def kernel(**inputs):
    import numpy as np
    import concourse.bacc as bacc
    from concourse.bass_utils import run_bass_kernel_spmd

    nc = bacc.Bacc("TRN2", target_bir_lowering=False, num_devices=1)
    arrays = {name: np.ascontiguousarray(inputs[name]) for name in INPUTS}
    aps = {name: nc.dram_tensor(name, a.shape, mybir.dt.from_np(a.dtype), kind="ExternalInput").ap()
           for name, a in arrays.items()}
    out = nc.dram_tensor("out", (BATCH, QL, D), mybir.dt.float32, kind="ExternalOutput").ap()
    build(nc, aps, out)
    r = run_bass_kernel_spmd(nc, [arrays], core_ids=[0])
    return r.results[0]["out"]
```

```python
import concourse.bass as bass
from concourse import mybir
from contextlib import ExitStack

BATCH, QL, D = 16, 256, 128
KL = 64
HEADS = 16
DKV = 64
DH = D // HEADS
FF = 512
P = 128
TILES = QL // P
G = 2
TURNS = BATCH // G
PAIRS = HEADS // 2
CHUNKS_FF = FF // P
STACKS = 4
RMS_EPS, LN_EPS = 1e-6, 1e-5
CAUSAL_FILL, MASK_FILL = -1e9, -1e20
SCALE1 = DH ** -0.5
SCALE3 = D ** -0.5

REGIONS_BIG, BIG = 3, 1024
REGIONS_SMALL, SMALL = 2, 512

ROWS = ["bq1", "bk1", "bv1", "ln_g", "ln_b", "bv2", "b_out", "g1", "beta1", "g2", "beta2"]
COLS = ["norm_w", "bk2", "bq2", "ln_gc", "ln_bc", "g1c", "beta1c"] + \
    ["b1_c%d" % c for c in range(CHUNKS_FF)] + ["bff1_c%d" % c for c in range(CHUNKS_FF)]
ROW_INPUT = {"bq1": "L1_xattn_bq", "bk1": "L1_xattn_bk", "bv1": "L1_xattn_bv", "b2_1": "L1_xattn_b2",
             "ln_g": "L1_xattn_ln_g", "ln_b": "L1_xattn_ln_b", "bv2": "L2_xattn_bv", "b_out": "L3_xattn_b_out",
             "g1": "L3_xattn_g1", "beta1": "L3_xattn_beta1", "b_ff2": "L3_xattn_b_ff2",
             "g2": "L3_xattn_g2", "beta2": "L3_xattn_beta2"}
COL_INPUT = {"norm_w": "L0_xattn_norm_w", "bk2": "L2_xattn_bk", "bq2": "L2_xattn_bq", "ln_gc": "L1_xattn_ln_g",
             "ln_bc": "L1_xattn_ln_b", "g1c": "L3_xattn_g1", "beta1c": "L3_xattn_beta1",
             "b1": "L1_xattn_b1", "bff1": "L3_xattn_b_ff1"}
VEC_STEPS, POOL_STEPS = 38, 3

PROLOGUE = [("wkT", 0, 0, "big"), ("wqT", 0, 0, "big"), ("wqk", 0, 0, "big"), ("wqk", 0, 1, "big")]

SEQS, TS = range(G), range(TILES)


def each(name, ring):
    return {"%s_%d" % (name, g): [(name, g, 0, ring)] for g in SEQS}


def each_tiles(name, ring):
    return {"%s_%d" % (name, g): [(name, g, t, ring) for t in TS] for g in SEQS}


def halves(name, ring):
    return {"%s_%d%d" % (name, g, h): [(name, g, h, ring)] for g in SEQS for h in range(2)}


FRONT = {
    "ctxT": [("ctxT", 0, 0, "small")], "fold_k_0": [("fold_k", 0, 0, "big")], "fold_k_1": [("fold_k", 0, 1, "big")],
    "ctx1": [("ctx_k1", 0, 0, "small"), ("ctx_v1", 0, 0, "small")],
    **each("xnT", "small"), **each("fold_v", "big"), "stack_k1": [("stack_k1", 0, 0, "small")],
    **each_tiles("s0", "big"), **each("max0", "small"), **each_tiles("sub0", "more s0"), **each_tiles("p0T", "big"),
    **each("o0", "small"), **each("x1T", "small"), **each("q1", "small"), **each("q1T", "big"), **each_tiles("s1", "big"),
    **each("max1", "small"), **halves("st1", "big"), **each("pv1", "small"), **each("at1", "small"),
    "ctx3": [("ctx_k3", 0, 0, "small"), ("ctx_v3", 0, 0, "small")], "stack_k3": [("stack_k3", 0, 0, "small")],
}
BACK = {
    **each("y1T", "small"), **each("h1", "big"), **each("f1", "small"), **each("x2T", "small"), **each("s2", "small"),
    **each("p2T", "small"), **each("o2", "big"), **each("q3T", "big"), **each_tiles("s3", "big"), **each("max3", "small"),
    **halves("st3", "big"), **each("pv3", "small"), **each("at3", "small"), **each("a3T", "small"), **each("w3", "small"),
    **each("y3T", "small"), **each("h3", "big"), **each("f3", "small"),
}
WEIGHTS = {
    "wvT": [("wvT", 0, 0, "big")], "wvo_0": [("wvo", 0, 0, "big")], "wvo_1": [("wvo", 0, 1, "big")],
    "l1_wT": [("l1_wT", 0, 0, "big")], "l12_w": [("l12_w", 0, 0, "big")], "l3_small_t": [("l3_small_t", 0, 0, "small")],
    "l3_b": [("l3_b", 0, 0, "small")], "l3_rep": [("l3_rep", 0, 0, "small")], "l3_full": [("l3_full", 0, 0, "small")],
}
ORDER = {
    "first": {
        "tensor": ("ctxT fold_k_0 l3_small_t l1_wT wvT fold_k_1 xnT_0 l3_b wvo_0 ctx1 s0_0 xnT_1 wvo_1 max0_0 sub0_0 l3_rep "
                   "s0_1 fold_v_0 max0_1 sub0_1 fold_v_1 p0T_0 stack_k1 l12_w o0_0 p0T_1 x1T_0 l3_full q1_0 o0_1 q1T_0 x1T_1 "
                   "q1_1 s1_0 q1T_1 ctx3 s1_1 max1_0 st1_00 max1_1 st1_01 st1_10 st1_11 stack_k3 pv1_0 pv1_1 at1_0 at1_1"),
        "vector": ("squares bias_sums fold_k_0 l3_small_t xn l1_wT l3_b xnT_0 fold_k_1 ctx1 s0_0 xnT_1 l3_rep s0_1 sums0_0 "
                   "sums0_1 l12_w o0_0 x1T_0 l3_full q1_0 o0_1 mask q1_1 s1_0 s1_1 max1_1 ctx3 at1_0 at1_1 stats1 norm1"),
        "scalar": ("ctxT squares fold_k_0 wvT fold_k_1 wvo_0 max0_0 sub0_0 wvo_1 max0_1 fold_v_0 sub0_1 fold_v_1 p0T_0 "
                   "stack_k1 p0T_1 x1T_1 q1T_0 q1T_1 max1_0 st1_00 st1_01 st1_10 st1_11 pv1_0 stack_k3 pv1_1"),
        "gpsimd": ("xn sums0_0 sums0_1 key_blocks1 key_blocks3 stats1 norm1"),
    },
    "loop": {
        "tensor": ("ctxT fold_v_0 fold_k_0 y1T_0 fold_k_1 y1T_1 h1_0 h1_1 ctx1 xnT_0 f1_0 s0_0 x2T_0 f1_1 max0_0 s2_0 xnT_1 "
                   "x2T_1 sub0_0 s2_1 s0_1 p2T_1 p2T_0 fold_v_1 max0_1 sub0_1 stack_k1 o2_0 o2_1 p0T_0 q3T_0 q3T_1 s3_0 o0_0 "
                   "p0T_1 x1T_0 s3_1 max3_0 o0_1 max3_1 st3_00 x1T_1 st3_01 q1_0 st3_10 q1_1 pv3_0 q1T_0 st3_11 at3_0 s1_0 "
                   "pv3_1 a3T_0 q1T_1 at3_1 w3_0 max1_0 s1_1 a3T_1 st1_00 w3_1 st1_01 max1_1 ctx3 st1_10 st1_11 stack_k3 "
                   "pv1_0 y3T_0 y3T_1 pv1_1 at1_0 h3_0 at1_1 h3_1 f3_0 f3_1"),
        "vector": ("squares y1T_0 fold_k_0 y1T_1 fold_k_1 xn xnT_0 ctx1 f1_0 s0_0 f1_1 s2_0 xnT_1 x2T_1 s2_1 rsum2 s0_1 "
                   "sums0_0 o2_0 o2_1 sums0_1 s3_0 o0_0 x1T_0 s3_1 max3_0 o0_1 q1_0 q1_1 at3_0 s1_0 at3_1 mask w3_0 s1_1 "
                   "w3_1 stats3 ctx3 norm3 y3T_0 y3T_1 at1_0 at1_1 stats1 f3_0 f3_1 stats4 norm1 norm4"),
        "scalar": ("ctxT squares fold_k_0 fold_v_0 fold_k_1 h1_0 h1_1 x2T_0 max0_0 s2_0 sub0_0 s2_1 p2T_1 p2T_0 max0_1 "
                   "fold_v_1 sub0_1 stack_k1 p0T_0 q3T_0 q3T_1 p0T_1 max3_1 st3_00 x1T_1 st3_01 st3_10 pv3_0 q1T_0 st3_11 "
                   "pv3_1 a3T_0 q1T_1 max1_0 a3T_1 max1_1 st1_01 st1_00 st1_10 st1_11 pv1_0 stack_k3 pv1_1 h3_0 h3_1"),
        "gpsimd": ("xn sums0_0 x3_bias sums0_1 key_blocks1 stats3 key_blocks3 norm3 stats1 stats4 norm1 norm4"),
    },
    "last": {
        "tensor": ("y1T_0 y1T_1 h1_0 h1_1 f1_0 f1_1 x2T_0 x2T_1 s2_0 s2_1 p2T_0 o2_0 p2T_1 o2_1 q3T_0 q3T_1 s3_0 s3_1 max3_0 "
                   "st3_00 st3_01 max3_1 st3_10 st3_11 pv3_0 pv3_1 at3_0 at3_1 a3T_0 a3T_1 w3_0 w3_1 y3T_0 y3T_1 h3_0 h3_1 "
                   "f3_0 f3_1"),
        "vector": ("y1T_0 y1T_1 f1_0 f1_1 x2T_0 s2_0 s2_1 rsum2 o2_0 o2_1 s3_0 s3_1 max3_1 at3_0 at3_1 a3T_0 w3_0 w3_1 "
                   "stats3 norm3 y3T_0 y3T_1 f3_0 f3_1 stats4 norm4"),
        "scalar": ("h1_0 h1_1 x2T_1 s2_0 p2T_0 s2_1 p2T_1 q3T_0 q3T_1 max3_0 st3_00 st3_01 st3_10 st3_11 pv3_0 pv3_1 a3T_1 "
                   "h3_0 h3_1"),
        "gpsimd": ("x3_bias stats3 norm3 stats4 norm4"),
    },
}
ROOMY = {
    "first": ("at1_1 l3_full max1_0 max1_1 pv1_0 pv1_1 q1_0 q1_1 x1T_1").split(),
    "loop": ("ctx1 ctxT f3_0 max1_0 max3_1 pv3_0 q1_1 s2_0 stack_k3 x1T_1 y3T_1").split(),
    "last": ("a3T_0 f1_1 f3_0 pv3_0 s2_0 s2_1 w3_1 x2T_0 y3T_0 y3T_1").split(),
}


def bursts(section):
    return [(name, g, part, "big" if s in ROOMY[section] and ring == "small" else ring)
            for s in ORDER[section]["tensor"].split() for name, g, part, ring in {**WEIGHTS, **FRONT, **BACK}[s]]


class Burst:

    def __init__(self, region, writes, drains):
        self.region, self.writes, self.drains = region, writes, drains
        self.per_turn = (0, 0)

    def is_written(self, j=0):
        return j * self.per_turn[0] + self.writes

    def is_free(self, j=0):
        return j * self.per_turn[1] + self.drains

    def is_drained(self, j=0):
        return self.is_free(j) + 1


def place(order, writes, drains, turns=1):
    at, first, used = {}, (dict(writes), dict(drains)), {"big": 0, "small": 0}
    for name, g, part, ring in order:
        if ring.startswith("more"):
            region = at[(ring.split()[1], g, part)].region
            before = at[(ring.split()[1], g, part)].drains
        else:
            count = REGIONS_BIG if ring == "big" else REGIONS_SMALL
            region = (ring, used[ring] % count)
            used[ring] += 1
            before = drains[region]
            drains[region] += 1
        writes[region] += 1
        at[(name, g, part)] = Burst(region, writes[region], before)
    for b in at.values():
        b.per_turn = (writes[b.region] - first[0][b.region], drains[b.region] - first[1][b.region])
    for r in writes:
        writes[r] += (turns - 1) * (writes[r] - first[0][r])
        drains[r] += (turns - 1) * (drains[r] - first[1][r])
    return at


def build(nc, I, out):
    f32, f32r, bf16, i32 = mybir.dt.float32, mybir.dt.float32r, mybir.dt.bfloat16, mybir.dt.int32
    ACT, ALU, AX = mybir.ActivationFunctionType, mybir.AluOpType, mybir.AxisListType
    ctx = ExitStack()
    with ctx:
        def sb(name, shape, dt=f32):
            return ctx.enter_context(nc.sbuf_tensor(name, shape, dt))

        def sem(name):
            return ctx.enter_context(nc.semaphore(name))

        regions = [("big", n) for n in range(REGIONS_BIG)] + [("small", n) for n in range(REGIONS_SMALL)]
        psum = {r: ctx.enter_context(nc.psum_tensor("ps_%s%d" % r, [P, BIG if r[0] == "big" else SMALL], f32))
                for r in regions}
        written = {r: sem("written_%s%d" % r) for r in regions}
        drained = {r: sem("drained_%s%d" % r) for r in regions}
        writes, drains = {r: 0 for r in regions}, {r: 0 for r in regions}
        pro = place(PROLOGUE, writes, drains)
        head = place(bursts("first"), writes, drains)
        body = place(bursts("loop"), writes, drains, TURNS - 1)
        tail = place(bursts("last"), writes, drains)

        def sections(eng, name, stages_of):
            stages = stages_of(head, 0, 0, None)
            for s in ORDER["first"][name].split():
                stages[s]()
            with eng.Fori(0, TURNS - 1) as j:
                stages = stages_of(body, j, j + 1, j)
                for s in ORDER["loop"][name].split():
                    stages[s]()
            stages = stages_of(tail, 0, None, TURNS - 1)
            for s in ORDER["last"][name].split():
                stages[s]()

        def of_each(name, stage):
            return {"%s_%d" % (name, g): (lambda g=g: stage(g)) for g in SEQS}

        early = sb("early", [P, 7 * HEADS * DKV])
        wq0, wk0, wv0 = (early[:, n * HEADS * DKV:(n + 1) * HEADS * DKV] for n in range(3))
        wo0, wkT, wqT, wvT = (early[:, n * HEADS * DKV:(n + 1) * HEADS * DKV].rearrange("p (c n) -> p c n", n=D)
                              for n in range(3, 7))
        probT = {l: sb("probT" + l, [P, G, PAIRS, QL]) for l in "13"}
        early2 = probT["3"][:, 1, :, :].rearrange("p c q -> p (c q)")
        hT = probT["3"][:, 0, :, :].rearrange("p (g c) q -> p g c q", g=G)
        wq1, wk1, wv1, wq2, wk2, wv2 = (early2[:, n * D:(n + 1) * D] for n in range(6))
        w2_1 = early2[:, 6 * D:6 * D + FF]
        w1_1 = early2[:, 10 * D:14 * D].rearrange("p (c n) -> p c n", n=D)
        w8, w8T = (probT["3"][0:DH, 0, 6, n * 3 * DH:(n + 1) * 3 * DH].rearrange("p (a n) -> p a n", n=DH)
                   for n in range(2))
        b8 = probT["3"][0:DH, 0, 6, 6 * DH:7 * DH]
        w_out, w_ff2 = sb("w_out", [P, D]), sb("w_ff2", [P, CHUNKS_FF, D])
        wqk = sb("wqk", [P, HEADS, D])
        wvo = sb("wvo", [P, 2, PAIRS, D])
        l1_wT = sb("l1_wT", [P, 3, D])
        up_hi, up_lo = ({l: sb(n + l, [P, CHUNKS_FF, P], f32r) for l in "13"} for n in ("up_hi", "up_lo"))
        w_ff1 = probT["3"][:, 0, 2:4, :].rearrange("p a q -> p (a q)").rearrange("p (c n) -> p c n", n=P)
        w2T = sb("w2T", [P, CHUNKS_FF, D])
        wv2T, wqk2 = sb("wv2T", [P, D]), sb("wqk2", [P, D])
        c2 = sb("c2", [P, 3])
        rep8 = probT["3"][0:DH, 0, 4, :].rearrange("p (a n) -> p a n", n=D)
        late_biases = probT["3"][:, 0, 5, :].rearrange("p (a n) -> p a n", n=D)
        l3_full = sb("l3_full", [P, 2, D])
        bc = sb("bc", [P, len(ROWS), D])
        cols = sb("cols", [P, len(COLS)])

        def row(name):
            return bc[:, ROWS.index(name), :]

        def col(name):
            n = COLS.index(name)
            return cols[:, n:n + 1]

        def per_tile(r):
            return r.unsqueeze(1).broadcast_to([P, G * TILES, D])

        ident = sb("ident", [P, P])
        ident_bf = sb("ident_bf", [P, P], bf16)
        ones_row = sb("ones_row", [1, P])
        rep_id = probT["3"][0:DH, 0, 7, 0:D].rearrange("p (h d) -> p h d", d=DH)
        head_of = sb("head_of", [P, HEADS])
        stack_head = sb("stack_head", [P, STACKS])
        stack_head3 = sb("stack_head3", [P, STACKS])
        spread = sb("spread", [2 * HEADS, HEADS, KL], f32r)
        causal = sb("causal", [KL, 2, KL], bf16)
        half_power = sb("half_power", [P, G * TILES])

        x_in = sb("x_in", [P, G, TILES, D])
        c_in = sb("c_in", [P, D])
        m_in = sb("m_in", [P, 1], i32)
        m01, pen = sb("m01", [P, 1]), sb("pen", [P, 1])
        ctxT = sb("ctxT", [P, G * KL])
        fold_k = sb("fold_k", [P, G, HEADS, KL], f32r)
        fold_v = sb("fold_v", [P, G, PAIRS, D])
        fold2 = sb("fold2", [P, G * KL])
        s2_row = sb("s2_row", [1, G * KL])
        v2 = sb("v2", [P, G, D])
        kf = sb("kf", [P, D])
        k_rows = {l: sb("k_rows" + l, [P, STACKS, 4, 32]) for l in "13"}
        k_stack = sb("k_stack", [P, STACKS, G * KL])
        k_blocks = {l: sb("k_blocks" + l, [P, G, STACKS, 4, KL], f32r) for l in "13"}
        v_blocks = {l: sb("v_blocks" + l, [P, G, PAIRS, 32]) for l in "13"}
        xT = {l: sb("xT" + l, [P, G, QL]) for l in "13"}
        xn_hi, xn_lo = (sb(n, [P, G, QL], f32r) for n in ("xn_hi", "xn_lo"))
        xn = sb("xn", [P, G, TILES, D])
        ss, ms, rs = sb("ss", [P, G * TILES]), sb("ms", [P, G * TILES]), sb("rs", [P, G * TILES])
        nmax = {l: sb("nmax" + l, [P, G, TILES, HEADS]) for l in "13"}
        nmax_hl = {l: sb("nmax_hl" + l, [P, G, TILES, 2, HEADS]) for l in "13"}
        nmaxT = {l: sb("nmaxT" + l, [2 * HEADS, G, QL], f32r) for l in "13"}
        prob = early[:, 0:4096].rearrange("p (g t n) -> p g t n", g=G, t=TILES)
        spread_f = probT["1"][0:2 * HEADS, 0, 0:4, :].rearrange("p c q -> p (c q)").rearrange("p (h k) -> p h k", k=KL)
        sums = sb("sums", [P, G, TILES, HEADS])
        rsum = {l: sb("rsum" + l, [P, G, TILES, HEADS]) for l in "13"}
        rsum["0"] = rsum["1"]
        x1, x2 = (sb(n, [P, G, TILES, D]) for n in ("x1", "x2"))
        x3 = x2
        q_rows = {"1": early[:, 4096:6144].rearrange("p (g t s a r) -> p g t s a r", g=G, t=TILES, s=STACKS, a=4),
                  "3": sb("q_rows3", [P, G, TILES, STACKS, 4, 32])}
        q_stack = {l: sb("q_stack" + l, [P, G, STACKS, QL], f32r) for l in "13"}
        fold_k_lo = q_stack["1"][:, :, :, :].rearrange("p g s (h k) -> p g (s h) k", k=KL)
        y_hi, y_lo = (q_stack["3"][:, :, n, :] for n in range(2))
        attT = early[:, 6144:7168].rearrange("p (g a q) -> p g a q", g=G, a=2)
        pre = {l: sb("pre" + l, [P, G, TILES, D]) for l in "134"}
        qf, att = pre["1"], pre
        stats, mv = ({l: sb(n + l, [P, G * TILES, w]) for l in "134"} for n, w in (("stats", 6), ("mv", 2)))
        var, rstd = ({l: sb(n + l, [P, G * TILES]) for l in "134"} for n in ("var", "rstd"))
        z = {l: pre[l][:, :, :, :].rearrange("p g t n -> p (g t) n") for l in "134"}
        y_bias = {l: sb("y_bias" + l, [P, G * TILES, D]) for l in "13"}
        x3_bias = xn[:, :, :, :].rearrange("p g t n -> p (g t) n")
        nmax2, sums2, rsum2 = sb("nmax2", [P, G, TILES]), sb("sums2", [P, G, TILES]), sb("rsum2", [P, G, TILES])
        prob2 = sb("prob2", [P, G, TILES, KL])
        prob2T = sb("prob2T", [P, G, P])

        keys_in, values_in, weights_in = sem("keys_in"), sem("values_in"), sem("weights_in")
        x_loaded, c_loaded = sem("x_loaded"), sem("c_loaded")
        stored = sem("stored")
        pool_consts = sem("pool_consts")
        vec_consts = sem("vec_consts")
        wq_scaled = sem("wq_scaled")
        mask_read, ctx_read = sem("mask_read"), sem("ctx_read")
        k_rows_ready = {l: sem("k_rows_ready" + l) for l in "13"}
        k_blocks_ready = {l: sem("k_blocks_ready" + l) for l in "13"}
        squares = sem("squares")
        ms_ready, rs_ready = sem("ms_ready"), sem("rs_ready")
        xn_ready = sem("xn_ready")
        fold_k_ready = sem("fold_k_ready")
        y_ready = {l: sem("y_ready" + l) for l in "13"}
        nmax_ready = {l: sem("nmax_ready" + l) for l in "013"}
        rsum_ready = sem("rsum_ready")
        norm_vec, norm_pool = sem("norm_vec"), sem("norm_pool")
        x1_ready, x2_ready, x3_ready = sem("x1_ready"), sem("x2_ready"), sem("x3_ready")
        x3_bias_ready = sem("x3_bias_ready")
        q_rows_ready = {l: sem("q_rows_ready" + l) for l in "13"}
        nmax2_ready = sem("nmax2_ready")
        att_ready = sem("att_ready")
        var_ready, rstd_ready, z_ready = ({l: sem(n + l) for l in "134"} for n in ("var_ready", "rstd_ready", "z_ready"))
        y_bias_ready = {l: sem("y_bias_ready" + l) for l in "13"}
        out_ready = sem("out_ready")
        stats_written = sem("stats_written")
        step = sem("step")
        pool_step = sem("pool_step")
        setup_step = sem("setup_step")

        block = ctx.enter_context(nc.Block())

        N_WEIGHTS = len(ROWS) + 2 + 8 + 3 + 11

        @block.sync
        def _(sp):
            def load_context(i):
                sp.dma_start(c_in[:, :], I["ctx_1024"].rearrange("(i g) k d -> i (g k) d", g=G)[i, :, :]).then_inc(c_loaded, 16)
                sp.dma_start(m_in[:, :], I["mask_Bx1x1xS2_if1"].rearrange("(i g) a b k -> i (g k) (a b)", g=G)[i, :, :]).then_inc(c_loaded, 16)

            def load_x(i):
                sp.dma_start(x_in[:, :, :, :], I["x"].rearrange("(i g) (t p) d -> i p g t d", g=G, p=P)[i, :, :, :, :]).then_inc(x_loaded, 16)

            def store(i):
                sp.wait_ge(out_ready, i + 1)
                sp.dma_start(out.rearrange("(i g) (t p) d -> i p (g t) d", g=G, p=P)[i, :, :, :], z["4"]).then_inc(stored, 16)

            sp.sem_inc(stored, 16)
            n = [0]

            def weight(dst, src):
                sp.dma_start(dst, src, allow_slow_non_contiguous=True).then_inc(weights_in, 16)
                n[0] += 1

            sp.dma_start(wk0, I["L0_xattn_wk"]).then_inc(keys_in, 16)
            sp.dma_start(wq0, I["L0_xattn_wq"]).then_inc(keys_in, 16)
            sp.dma_start(col("norm_w"), I[COL_INPUT["norm_w"]].rearrange("(n a) -> n a", a=1)).then_inc(keys_in, 16)
            sp.dma_start(wv0, I["L0_xattn_wv"]).then_inc(values_in, 16)
            sp.dma_start(wo0, I["L0_xattn_wo"].rearrange("(c p) n -> p c n", p=P)).then_inc(values_in, 16)
            load_context(0)
            load_x(0)
            for dst, name in ((wq1, "L1_xattn_Wq"), (wk1, "L1_xattn_Wk"), (wv1, "L1_xattn_Wv"), (w2_1, "L1_xattn_W2"),
                              (wq2, "L2_xattn_Wq"), (wk2, "L2_xattn_Wk"), (wv2, "L2_xattn_Wv")):
                weight(dst, I[name])
            weight(w1_1, I["L1_xattn_W1"].rearrange("(c p) n -> p c n", p=P))
            for k, name in enumerate(("L3_xattn_wk", "L3_xattn_wq", "L3_xattn_wv")):
                weight(w8[:, k, :], I[name])
            for r, name in enumerate(ROWS):
                weight(row(name), I[ROW_INPUT[name]].rearrange("(a n) -> a n", a=1).broadcast_to([P, D]))
            for r, name in enumerate(("b2_1", "b_ff2")):
                weight(late_biases[:, r, :], I[ROW_INPUT[name]].rearrange("(a n) -> a n", a=1).broadcast_to([P, D]))
            for c, name in enumerate(COLS[1:], 1):
                if name.endswith("_c0"):
                    weight(cols[:, c:c + CHUNKS_FF], I[COL_INPUT[name[:-3]]].rearrange("(c n) -> n c", n=P))
                elif "_c" not in name:
                    weight(cols[:, c:c + 1], I[COL_INPUT[name]].rearrange("(n a) -> n a", a=1))
            for dst, name in ((w_out[:, :], "L3_xattn_w_out"), (w_ff1.rearrange("p c n -> p (c n)"), "L3_xattn_w_ff1")):
                weight(dst, I[name])
            weight(w_ff2[:, :, :], I["L3_xattn_w_ff2"].rearrange("(c p) n -> p c n", p=P))
            assert n[0] == N_WEIGHTS, n[0]

            def load_after(j):
                sp.wait_ge(ctx_read, j + 1)
                sp.wait_ge(mask_read, j + 1)
                load_context(j + 1)
                sp.wait_ge(x1_ready, (j + 1) * G)
                load_x(j + 1)

            load_after(0)
            with sp.Fori(0, TURNS - 2) as j:
                load_after(j + 1)
                store(j)
            store(TURNS - 2)
            store(TURNS - 1)
            sp.wait_ge(stored, 16 * TURNS + 16)

        @block.gpsimd
        def _(pool):
            pool.memset(ident[:, :], 0.0).then_inc(pool_consts, 1)
            pool.wait_ge(pool_consts, 1)
            pool.affine_select(out=ident[:, :], in_=ident[:, :], compare_op=ALU.not_equal, fill=1.0, base=0,
                               pattern=[[-1, P]], channel_multiplier=1).then_inc(pool_consts, 1)
            pool.memset(ident_bf[:, :], 0.0)
            pool.memset(spread_f, 0.0)
            for t in (rep_id, causal):
                pool.memset(t[:, :, :], 0.0)
            pool.memset(half_power[:, :], -0.5)
            for l in "13":
                pool.memset(v_blocks[l][:, :, :, :].rearrange("p b c d -> p (b c d)"), 0.0)
                pool.memset(k_rows[l][:, :, :, :].rearrange("p b c d -> p (b c d)"), 0.0)
            pool.memset(q_rows["3"][:, :, :, :, :, :].rearrange("p a b c d e -> p (a b c d e)"), 0.0)
            pool.memset(ones_row[:, :], 1.0).then_inc(pool_consts, 1)
            pool.wait_ge(pool_consts, 3)
            pool.affine_select(out=ident_bf[:, :], in_=ident_bf[:, :], compare_op=ALU.not_equal, fill=1.0, base=0,
                               pattern=[[-1, P]], channel_multiplier=1)
            pool.affine_select(out=rep_id[:, :, :], in_=rep_id[:, :, :], compare_op=ALU.not_equal, fill=1.0, base=0,
                               pattern=[[0, HEADS], [-1, DH]], channel_multiplier=1)
            pool.affine_select(out=causal[:, :, :], in_=causal[:, :, :], compare_op=ALU.is_ge, fill=CAUSAL_FILL, base=0,
                               pattern=[[0, 2], [-1, KL]], channel_multiplier=1)
            pool.affine_select(out=spread_f, in_=spread_f, compare_op=ALU.not_equal, fill=1.0, base=0,
                               pattern=[[-1, HEADS], [0, KL]], channel_multiplier=1).then_inc(pool_consts, 1)
            pool.wait_ge(pool_consts, 4)
            pool.affine_select(out=spread_f, in_=spread_f, compare_op=ALU.not_equal, fill=1.0,
                               base=-HEADS, pattern=[[-1, HEADS], [0, KL]], channel_multiplier=1)
            pool.memset(q_rows["3"][:, :, :, :, 3, 0:2].rearrange("p g t s d -> p (g t s) d"), 1.0).then_inc(pool_consts, 1)
            pool.wait_ge(vec_consts, 1)

            taken = [0]

            def stages(at, j, front, back):
                looped = front is not None and back is not None
                base, own = taken[0], [0]
                if looped:
                    taken[0] += POOL_STEPS * (TURNS - 1)

                def link(ins):
                    own[0] += 1
                    ins.then_inc(pool_step, 1)
                    if looped:
                        pool.wait_ge(pool_step, base + j * POOL_STEPS + own[0])
                    else:
                        taken[0] += 1
                        pool.wait_ge(pool_step, taken[0])

                def key_blocks(l):
                    b = at[("stack_k" + l, 0, 0)]
                    heads_of = stack_head if l == "1" else stack_head3
                    pool.wait_ge(drained[b.region], b.is_drained(j))
                    for g in SEQS:
                        for s in range(STACKS):
                            last = pool.tensor_tensor(
                                out=k_blocks[l][:, g, s, :, :],
                                in0=k_stack[:, s, g * KL:(g + 1) * KL].unsqueeze(1).broadcast_to([P, 4, KL]),
                                in1=heads_of[:, :].unsqueeze(2).broadcast_to([P, 4, KL]), op=ALU.mult)
                        last.then_inc(k_blocks_ready[l], 1)

                def input_norm():
                    pool.wait_ge(ms_ready, front + 1)
                    pool.tensor_tensor(out=rs[:, :], in0=ms[:, :], in1=half_power[:, :], op=ALU.pow).then_inc(rs_ready, 1)

                def normalise(g):
                    pool.wait_ge(rsum_ready, (front * G + g) * TILES + 2)
                    pool.tensor_tensor(out=prob[:, g, 1, :].rearrange("p (h k) -> p h k", k=KL),
                                       in0=prob[:, g, 1, :].rearrange("p (h k) -> p h k", k=KL),
                                       in1=rsum["0"][:, g, 1, :].unsqueeze(2).broadcast_to([P, HEADS, KL]),
                                       op=ALU.mult).then_inc(norm_pool, 1)

                def power(l, i):
                    pool.wait_ge(var_ready[l], i + 1)
                    pool.tensor_tensor(out=rstd[l][:, :], in0=var[l][:, :], in1=half_power[:, :],
                                       op=ALU.pow).then_inc(rstd_ready[l], 1)

                def gain(l, i, gamma, beta, dst, done):
                    if back is None:
                        pool.wait_ge(vec_consts, 2)
                    pool.wait_ge(z_ready[l], i + 1)
                    src = z[l]
                    link(pool.tensor_tensor(out=dst, in0=src, in1=per_tile(row(gamma)), op=ALU.mult))
                    pool.tensor_tensor(out=dst, in0=dst, in1=per_tile(row(beta)), op=ALU.add).then_inc(done, 1)

                def x3_and_bias():
                    pool.wait_ge(x3_ready, (back + 1) * G)
                    pool.tensor_tensor(out=x3_bias[:, :, :], in0=x3[:, :, :, :].rearrange("p g t n -> p (g t) n"),
                                       in1=per_tile(row("b_out")), op=ALU.add).then_inc(x3_bias_ready, 1)

                return {"xn": input_norm, "key_blocks3": lambda: key_blocks("3"), "key_blocks1": lambda: key_blocks("1"),
                        **of_each("sums0", normalise), "x3_bias": x3_and_bias,
                        "stats1": lambda: power("1", front), "stats3": lambda: power("3", back), "stats4": lambda: power("4", back),
                        "norm1": lambda: gain("1", front, "ln_g", "ln_b", y_bias["1"][:, :, :], y_bias_ready["1"]),
                        "norm3": lambda: gain("3", back, "g1", "beta1", y_bias["3"][:, :, :], y_bias_ready["3"]),
                        "norm4": lambda: gain("4", back, "g2", "beta2", z["4"], out_ready)}

            sections(pool, "gpsimd", stages)

        @block.scalar
        def _(act):
            for name, part, dst in (("wkT", 0, wkT),
                                    ("wqk", 0, wqk[:, 0:8, :].rearrange("p (c a) n -> p a c n", a=2)),
                                    ("wqk", 1, wqk[:, 8:16, :].rearrange("p (c a) n -> p a c n", a=2))):
                b = pro[(name, 0, part)]
                act.wait_ge(written[b.region], b.is_written())
                src = psum[b.region][:, :].rearrange("p (c n) -> p c n", n=P)
                if name == "wqk":
                    src = psum[b.region][:, :].rearrange("p (a c n) -> p a c n", a=2, n=P)
                act.activation(dst, src, ACT.Copy).then_inc(drained[b.region], 1)

            def stages(at, j, front, back):
                def drain(key, dst, src):
                    b = at[key]
                    act.wait_ge(written[b.region], b.is_written(j))
                    act.activation(dst, src(psum[b.region]), ACT.Copy).then_inc(drained[b.region], 1)

                def input_squares():
                    act.wait_ge(x_loaded, 16 * (front + 1))
                    for n in range(G * TILES):
                        last = act.activation(xn[:, n // TILES, n % TILES, :], x_in[:, n // TILES, n % TILES, :], ACT.Square,
                                              accum_out=ss[:, n:n + 1])
                    last.then_inc(squares, 1)

                def keys0(half):
                    b = at[("fold_k", 0, half)]
                    act.wait_ge(written[b.region], b.is_written(j))
                    act.activation(fold_k[:, :, 8 * half:8 * half + 8, :],
                                   psum[b.region][:, :].rearrange("p (h g k) -> p g h k", g=G, k=KL), ACT.Copy).then_inc(fold_k_ready, 1)

                def stack(l):
                    if l == "3":
                        act.wait_ge(k_blocks_ready["1"], (front + 1) * G)
                    elif back is not None:
                        act.wait_ge(k_blocks_ready["3"], (back + 1) * G)
                    drain(("stack_k" + l, 0, 0), k_stack[:, :, :], lambda ps: ps[:, 0:SMALL].rearrange("p (s k) -> p s k", s=STACKS))

                def values0(g):
                    drain(("fold_v", g, 0), fold_v[:, g, :, :], lambda ps: ps[:, :].rearrange("p (c n) -> p c n", n=D))

                def exps0(g):
                    for t in TS:
                        b = at[("sub0", g, t)]
                        act.wait_ge(written[b.region], b.is_written(j))
                        act.activation(prob[:, g, t, :], psum[b.region][:, :], ACT.Exp).then_inc(drained[b.region], 1)

                def probabilities_T(g):
                    for t in TS:
                        drain(("p0T", g, t), probT["1"][:, g, :, t * P:(t + 1) * P], lambda ps: ps[:, :].rearrange("p (c q) -> p c q", q=P))

                def queries(l, g):
                    drain(("q%sT" % l, g, 0), q_stack[l][:, g, :, :], lambda ps: ps[:, :].rearrange("p (s q) -> p s q", q=QL))

                def exps_T(l, scale, g, half):
                    b = at[("st" + l, g, half)]
                    act.wait_ge(written[b.region], b.is_written(j))
                    act.activation(probT[l][:, g, 4 * half:4 * half + 4, :],
                                   psum[b.region][:, :].rearrange("p (c q) -> p c q", q=QL), ACT.Exp,
                                   scale=scale).then_inc(drained[b.region], 1)

                def outputs_T(l, g):
                    drain(("pv" + l, g, 0), attT[:, g, :, :], lambda ps: ps[:, 0:SMALL].rearrange("p (a q) -> p a q", q=QL))

                def hidden(l, g):
                    b = at[("h" + l, g, 0)]
                    act.wait_ge(written[b.region], b.is_written(j))
                    for c in range(CHUNKS_FF):
                        last = act.activation(hT[:, g, c, :], psum[b.region][:, c * QL:(c + 1) * QL],
                                              ACT.Gelu if l == "1" else ACT.Relu,
                                              bias=col(("b1_c%d" if l == "1" else "bff1_c%d") % c))
                    last.then_inc(drained[b.region], 1)

                def exps2(g):
                    act.wait_ge(nmax2_ready, back * G + g + 1)
                    b = at[("s2", g, 0)]
                    for t in TS:
                        last = act.activation(prob2[:, g, t, :], psum[b.region][:, t * KL:(t + 1) * KL], ACT.Exp,
                                              bias=nmax2[:, g, t:t + 1], accum_out=sums2[:, g, t:t + 1])
                    last.then_inc(drained[b.region], 1)

                def prob2_T(g):
                    drain(("p2T", g, 0), prob2T[:, g, :], lambda ps: ps[:, 0:P])

                named = {"ctxT": lambda: drain(("ctxT", 0, 0), ctxT[:, :], lambda ps: ps[:, 0:P]), "squares": input_squares, "fold_k_0": lambda: keys0(0), "fold_k_1": lambda: keys0(1),
                         **of_each("fold_v", values0), "stack_k1": lambda: stack("1"), "stack_k3": lambda: stack("3"),
                         **of_each("sub0", exps0), **of_each("p0T", probabilities_T), **of_each("s2", exps2), **of_each("p2T", prob2_T)}
                for name, dst in (("x1T", xT["1"]), ("x2T", xT["3"]), ("a3T", xT["3"])):
                    named.update(of_each(name, lambda g, name=name, dst=dst: drain((name, g, 0), dst[:, g, :], lambda ps: ps[:, 0:QL])))
                for l, buf in (("0", "1"), ("1", "1"), ("3", "3")):
                    named.update(of_each("max" + l, lambda g, l=l, buf=buf: drain(
                        ("max" + l, g, 0), nmaxT[buf][:, g, :], lambda ps: ps[0:2 * HEADS, 0:QL])))
                for name, key, dst in (("wvT", ("wvT", 0, 0), wvT), ("wvo_0", ("wvo", 0, 0), wvo[:, 0, :, :]),
                                       ("wvo_1", ("wvo", 0, 1), wvo[:, 1, :, :])):
                    named[name] = lambda key=key, dst=dst: drain(key, dst, lambda ps: ps[:, :].rearrange("p (c n) -> p c n", n=P))
                for l, scale in (("1", SCALE1), ("3", SCALE3)):
                    named.update(of_each("q%sT" % l, lambda g, l=l: queries(l, g)))
                    named.update(of_each("pv" + l, lambda g, l=l: outputs_T(l, g)))
                    named.update(of_each("h" + l, lambda g, l=l: hidden(l, g)))
                    for half in range(2):
                        for g in SEQS:
                            named["st%s_%d%d" % (l, g, half)] = lambda l=l, s=scale, g=g, half=half: exps_T(l, s, g, half)
                return named

            sections(act, "scalar", stages)

        @block.vector
        def _(dve):
            made = [0]

            def setup(ins):
                made[0] += 1
                ins.then_inc(setup_step, 1)
                dve.wait_ge(setup_step, made[0])

            def take(key, dst, src):
                b = pro[key]
                dve.wait_ge(written[b.region], b.is_written())
                dve.tensor_copy(dst, src(psum[b.region])).then_inc(drained[b.region], 1)

            dve.wait_ge(keys_in, 3 * 16)
            dve.tensor_scalar(wq0, wq0, col("norm_w"), None, ALU.mult).then_inc(wq_scaled, 1)
            dve.wait_ge(pool_consts, 5)
            setup(dve.tensor_copy(spread[:, :, :], spread_f))
            for half in range(2):
                for l in "13":
                    dve.memset(v_blocks[l][half * KL:(half + 1) * KL, :, :, 16 + half:17 + half], 1.0)
            setup(dve.reduce_sum(head_of[:, :], ident[:, :].rearrange("p (h r) -> p h r", r=DH), axis=AX.X))
            setup(dve.reduce_sum(stack_head[:, :], head_of[:, :].rearrange("p (a h) -> p h a", h=4), axis=AX.X))
            setup(dve.tensor_copy(stack_head3[:, :], stack_head[:, :]))
            dve.memset(stack_head3[96:128, :], 1.0).then_inc(vec_consts, 1)
            take(("wqT", 0, 0), wqT, lambda ps: ps[:, :].rearrange("p (c n) -> p c n", n=P))
            taken = [0]

            def stages(at, j, front, back):
                looped = front is not None and back is not None
                base, own = taken[0], [0]
                if looped:
                    taken[0] += VEC_STEPS * (TURNS - 1)
                vec_counts.append(own)

                def link(ins):
                    own[0] += 1
                    ins.then_inc(step, 1)
                    if looped:
                        dve.wait_ge(step, base + j * VEC_STEPS + own[0])
                    else:
                        taken[0] += 1
                        dve.wait_ge(step, taken[0])

                def opened(key):
                    b = at[key]
                    dve.wait_ge(written[b.region], b.is_written(j))
                    return psum[b.region], drained[b.region], b

                def drain(key, dst, src):
                    ps, free, _ = opened(key)
                    dve.tensor_copy(dst, src(ps)).then_inc(free, 1)

                def drain_T(name, dst):
                    return of_each(name, lambda g: drain((name, g, 0), dst[:, g, :], lambda ps: ps[:, 0:QL]))

                def tiles_of(ps):
                    return ps[:, 0:QL].rearrange("p (t n) -> p t n", n=D)

                def key_rows(l):
                    kv = kf[:, :].rearrange("p (s r) -> p s r", r=32)
                    for part in (0, 2):
                        last = dve.tensor_copy(k_rows[l][:, :, part, :].bitcast(f32r), kv)
                    if l == "3":
                        last = dve.tensor_copy(k_rows[l][:, :, 3, 0:1].bitcast(f32r), pen[:, :].unsqueeze(1).broadcast_to([P, STACKS, 1]))
                    link(last)
                    for part in ((1, 3) if l == "1" else (1,)):
                        last = dve.tensor_tensor(out=k_rows[l][:, :, part, :].bitcast(f32r), in0=kv,
                                                 in1=k_rows[l][:, :, 0, :], op=ALU.subtract)
                    if l == "3":
                        last = dve.tensor_tensor(out=k_rows[l][:, :, 3, 1:2].bitcast(f32r), in0=pen[:, :].unsqueeze(1).broadcast_to([P, STACKS, 1]),
                                                 in1=k_rows[l][:, :, 3, 0:1], op=ALU.subtract)
                    last.then_inc(k_rows_ready[l], 1)

                def value_blocks(l, ps):
                    for half in range(2):
                        rows_of, cols_of = slice(half * KL, (half + 1) * KL), slice(half * DH, (half + 1) * DH)
                        dst = v_blocks[l][rows_of, :, :, cols_of]
                        src = ps[rows_of, 0:P].rearrange("p (g c d) -> p g c d", g=G, d=DH)
                        if l == "1":
                            for g in SEQS:
                                last = dve.tensor_tensor(out=dst[:, g, :, :], in0=src[:, g, :, :],
                                                         in1=row("bv1")[rows_of, :].rearrange("p (c a d) -> p c a d", a=2, d=DH)[:, :, half, :],
                                                         op=ALU.add)
                        else:
                            last = dve.tensor_copy(dst, src)
                    return last

                def context3():
                    ps, free, b = opened(("ctx_k3", 0, 0))
                    dve.tensor_scalar(kf[:, :], ps[:, 0:D], m01[:, 0:1], None, ALU.mult)
                    dve.tensor_scalar(fold2[:, :], ps[:, D:2 * D], c2[:, 0:1], None, ALU.add)
                    dve.tensor_scalar(s2_row[:, :], ps[0:1, 2 * D:3 * D], c2[0:1, 2:3], None, ALU.add).then_inc(free, 1)
                    dve.wait_ge(free, b.is_drained(j))
                    key_rows("3")
                    ps, free, b = opened(("ctx_v3", 0, 0))
                    value_blocks("3", ps)
                    dve.tensor_tensor(out=v2[:, :, :], in0=ps[:, P:P + G * D].rearrange("p (g n) -> p g n", n=D),
                                      in1=row("bv2").unsqueeze(1).broadcast_to([P, G, D]), op=ALU.add).then_inc(free, 1)

                def mask():
                    if back is not None:
                        dve.wait_ge(k_rows_ready["3"], back + 1)
                    dve.wait_ge(c_loaded, 32 * (front + 1))
                    dve.tensor_scalar(m01[:, :], m_in[:, :], 0.0, None, ALU.not_equal)
                    link(dve.tensor_scalar(pen[:, :], m_in[:, :], 0.0, MASK_FILL, ALU.is_equal, ALU.mult))
                    dve.sem_inc(mask_read, 1)

                def keys0_lo(half):
                    dve.wait_ge(fold_k_ready, front * 2 + half + 1)
                    ps, free, _ = opened(("fold_k", 0, half))
                    dst = slice(8 * half, 8 * half + 8)
                    for g in SEQS:
                        last = dve.tensor_tensor(out=fold_k_lo[:, g, dst, :],
                                                 in0=ps[:, :].rearrange("p (h g k) -> p g h k", g=G, k=KL)[:, g, :, :],
                                                 in1=fold_k[:, g, dst, :].bitcast(f32), op=ALU.subtract)
                    last.then_inc(free, 1)

                def input_T(g):
                    ps, free, _ = opened(("xnT", g, 0))
                    link(dve.tensor_copy(xn_hi[:, g, :], ps[:, 0:QL]))
                    dve.tensor_tensor(out=xn_lo[:, g, :], in0=ps[:, 0:QL], in1=xn_hi[:, g, :].bitcast(f32),
                                      op=ALU.subtract).then_inc(free, 1)

                def mean_squares():
                    dve.wait_ge(squares, front + 1)
                    dve.tensor_scalar(ms[:, :], ss[:, :], 1.0 / D, RMS_EPS, ALU.mult, ALU.add).then_inc(ms_ready, 1)

                def context1():
                    ps, free, b = opened(("ctx_k1", 0, 0))
                    dve.tensor_tensor(out=kf[:, :], in0=ps[:, 0:D], in1=row("bk1"), op=ALU.add).then_inc(free, 1)
                    dve.wait_ge(free, b.is_drained(j))
                    key_rows("1")
                    ps, free, b = opened(("ctx_v1", 0, 0))
                    value_blocks("1", ps).then_inc(free, 1)

                def input_over_rms():
                    dve.wait_ge(rs_ready, front + 1)
                    for g in SEQS:
                        for t in TS:
                            last = dve.tensor_scalar(xn[:, g, t, :], x_in[:, g, t, :], rs[:, g * TILES + t:g * TILES + t + 1], None, ALU.mult)
                        last.then_inc(xn_ready, 1)

                def tile_max(key, l, g, t):
                    ps, free, _ = opened(key)
                    return dve.tensor_reduce(out=nmax[l][:, g, t, :], in_=ps[:, :].rearrange("p (h k) -> p h k", k=KL),
                                             op=ALU.max, axis=AX.X, negate=True), free

                def max_split(l, buf, g):
                    link(dve.tensor_copy(nmax_hl[buf][:, g, :, 0, :].bitcast(f32r), nmax[buf][:, g, :, :]))
                    dve.tensor_tensor(out=nmax_hl[buf][:, g, :, 1, :].bitcast(f32r), in0=nmax[buf][:, g, :, :],
                                      in1=nmax_hl[buf][:, g, :, 0, :], op=ALU.subtract).then_inc(nmax_ready[l], 1)

                def maxima0(g):
                    tile_max(("s0", g, 0), "1", g, 0)
                    link(tile_max(("s0", g, 1), "1", g, 1)[0])
                    max_split("0", "1", g)

                def maxima(l, g):
                    for t in TS:
                        ins, free = tile_max(("s" + l, g, t), l, g, t)
                        ins.then_inc(free, 1)
                    b = at[("s" + l, g, 1)]
                    dve.wait_ge(drained[b.region], b.is_drained(j))
                    max_split(l, l, g)

                def drain_maxT(l, buf, g):
                    drain(("max" + l, g, 0), nmaxT[buf][:, g, :], lambda ps: ps[0:2 * HEADS, 0:QL])

                def sums0(g):
                    for t in TS:
                        b = at[("s0", g, t)]
                        dve.wait_ge(drained[b.region], b.is_drained(j))
                        pv = prob[:, g, t, :].rearrange("p (h k) -> p h k", k=KL)
                        link(dve.reduce_sum(sums[:, g, t, :], pv, axis=AX.X))
                        dve.reciprocal(rsum["0"][:, g, t, :], sums[:, g, t, :]).then_inc(rsum_ready, 1)
                    dve.tensor_tensor(out=prob[:, g, 0, :].rearrange("p (h k) -> p h k", k=KL),
                                      in0=prob[:, g, 0, :].rearrange("p (h k) -> p h k", k=KL),
                                      in1=rsum["0"][:, g, 0, :].unsqueeze(2).broadcast_to([P, HEADS, KL]),
                                      op=ALU.mult).then_inc(norm_vec, 1)

                def output0(g):
                    ps, free, b = opened(("o0", g, 0))
                    dve.tensor_tensor(out=x1[:, g, :, :], in0=tiles_of(ps), in1=x_in[:, g, :, :], op=ALU.add).then_inc(free, 1)
                    dve.wait_ge(free, b.is_drained(j))
                    dve.sem_inc(x1_ready, 1)

                def query_rows(l, src, g):
                    qv = src[:, g, :, :].rearrange("p t (s r) -> p (t s) r", r=32)
                    dst = q_rows[l][:, g, :, :, :, :].rearrange("p t s a r -> p (t s) a r")
                    lo = 4 if l == "1" else 3
                    link(dve.tensor_copy(dst[:, :, 0:2, :].bitcast(f32r), qv.unsqueeze(2).broadcast_to([P, 8, 2, 32])))
                    dve.tensor_tensor(out=dst[:, :, 2:lo, :].bitcast(f32r), in0=qv.unsqueeze(2).broadcast_to([P, 8, lo - 2, 32]),
                                      in1=dst[:, :, 0:lo - 2, :], op=ALU.subtract).then_inc(q_rows_ready[l], 1)

                def queries1(g):
                    ps, free, b = opened(("q1", g, 0))
                    dve.tensor_tensor(out=qf[:, g, :, :], in0=tiles_of(ps),
                                      in1=row("bq1").unsqueeze(1).broadcast_to([P, TILES, D]), op=ALU.add).then_inc(free, 1)
                    dve.wait_ge(free, b.is_drained(j))
                    query_rows("1", qf, g)

                def statistics(l):
                    for n in range(G * TILES):
                        last = dve.bn_stats(stats[l][:, n, :], pre[l][:, n // TILES, n % TILES, :])
                    link(last)
                    dve.sem_inc(stats_written, 1)
                    for n in range(G * TILES):
                        last = dve.bn_aggr(mv[l][:, n, :], stats[l][:, n, :])
                    link(last)
                    dve.tensor_scalar(var[l][:, :], mv[l][:, :, 1], LN_EPS, None, ALU.add).then_inc(var_ready[l], 1)

                def norm(l, i):
                    dve.wait_ge(rstd_ready[l], i + 1)
                    for n in range(G * TILES):
                        src = pre[l][:, n // TILES, n % TILES, :]
                        last = dve.tensor_scalar(src, src, mv[l][:, n, 0:1], rstd[l][:, n:n + 1],
                                                 ALU.subtract, ALU.mult)
                    last.then_inc(z_ready[l], 1)

                def attention(l, g):
                    ps, free, b = opened(("at" + l, g, 0))
                    pv = ps[:, 0:SMALL].rearrange("p (n m) -> p n m", m=32)
                    link(dve.reciprocal(rsum[l][:, g, :, :].rearrange("p t (c a) -> p (t c) a", a=2), pv[:, :, 16:18]))
                    dve.tensor_tensor(out=att[l][:, g, :, :].rearrange("p t (c a d) -> p (t c) a d", a=2, d=DH),
                                      in0=pv[:, :, 0:16].rearrange("p n (a d) -> p n a d", d=DH),
                                      in1=rsum[l][:, g, :, :].rearrange("p t (c a) -> p (t c) a", a=2).unsqueeze(3).broadcast_to([P, 16, 2, DH]),
                                      op=ALU.mult).then_inc(free, 1)
                    dve.wait_ge(free, b.is_drained(j))
                    if l == "3":
                        dve.sem_inc(att_ready, 1)
                    else:
                        link(dve.tensor_tensor(out=pre[l][:, g, :, :], in0=att[l][:, g, :, :], in1=x1[:, g, :, :], op=ALU.add))

                def drain_yT(l, gamma, beta, g):
                    ps, free, b = opened(("y%sT" % l, g, 0))
                    y = xT["3"][:, g, :]
                    dve.tensor_scalar(y, ps[:, 0:QL], col(gamma), col(beta), ALU.mult, ALU.add).then_inc(free, 1)
                    dve.wait_ge(free, b.is_drained(j))
                    link(dve.tensor_copy(y_hi[:, g, :], y))
                    dve.tensor_tensor(out=y_lo[:, g, :], in0=y, in1=y_hi[:, g, :].bitcast(f32), op=ALU.subtract).then_inc(y_ready[l], 1)

                def feed_forward_out(l, g):
                    dve.wait_ge(y_bias_ready[l], back + 1)
                    ps, free, b = opened(("f" + l, g, 0))
                    dst = x2 if l == "1" else pre["4"]
                    if l == "3":
                        dve.wait_ge(stored, 16 * back + 16)
                    dve.tensor_tensor(out=dst[:, g, :, :], in0=tiles_of(ps), in1=y_bias[l][:, g * TILES:(g + 1) * TILES, :],
                                      op=ALU.add).then_inc(free, 1)
                    dve.wait_ge(free, b.is_drained(j))
                    if l == "1":
                        dve.sem_inc(x2_ready, 1)

                def maxima2(g):
                    ps, _, b = opened(("s2", g, 0))
                    dve.tensor_reduce(out=nmax2[:, g, :], in_=ps[:, 0:TILES * KL].rearrange("p (t k) -> p t k", k=KL),
                                      op=ALU.max, axis=AX.X, negate=True).then_inc(nmax2_ready, 1)

                def inverse_sums2():
                    for g in SEQS:
                        b = at[("s2", g, 0)]
                        dve.wait_ge(drained[b.region], b.is_drained(j))
                        last = dve.reciprocal(rsum2[:, g, :], sums2[:, g, :])
                    link(last)

                def output2(g):
                    ps, free, b = opened(("o2", g, 0))
                    for t in TS:
                        last = dve.scalar_tensor_tensor(out=x3[:, g, t, :], in0=ps[:, t * 512:t * 512 + D],
                                                        scalar=rsum2[:, g, t:t + 1], in1=x2[:, g, t, :],
                                                        op0=ALU.mult, op1=ALU.add)
                    last.then_inc(free, 1)
                    dve.wait_ge(free, b.is_drained(j))
                    dve.sem_inc(x3_ready, 1)
                    query_rows("3", x3, g)

                def out3(g):
                    dve.wait_ge(x3_bias_ready, back + 1)
                    ps, free, b = opened(("w3", g, 0))
                    dve.tensor_tensor(out=pre["3"][:, g, :, :], in0=tiles_of(ps), in1=x3_bias[:, g * TILES:(g + 1) * TILES, :],
                                      op=ALU.add).then_inc(free, 1)
                    dve.wait_ge(free, b.is_drained(j))

                def l1_weights():
                    ps, free, _ = opened(("l1_wT", 0, 0))
                    dve.tensor_copy(l1_wT[:, :, :], ps[:, 0:3 * P].rearrange("p (a n) -> p a n", n=P))
                    w1T = ps[:, 3 * P:7 * P].rearrange("p (a n) -> p a n", n=P)
                    link(dve.tensor_copy(up_hi["1"][:, :, :], w1T))
                    dve.tensor_tensor(out=up_lo["1"][:, :, :], in0=w1T, in1=up_hi["1"][:, :, :].bitcast(f32), op=ALU.subtract).then_inc(free, 1)

                def l12_weights():
                    ps, free, b = opened(("l12_w", 0, 0))
                    dve.tensor_copy(w2T[:, :, :], ps[:, 0:FF].rearrange("p (a n) -> p a n", n=P))
                    dve.tensor_copy(wv2T[:, :], ps[:, FF:FF + D])
                    dve.tensor_copy(wqk2[:, :], ps[:, FF + D:FF + 2 * D])
                    dve.tensor_copy(c2[:, 0:2], ps[:, FF + 2 * D:FF + 2 * D + 2])
                    dve.tensor_copy(c2[0:1, 2:3], ps[0:1, FF + 2 * D + 2:FF + 2 * D + 3]).then_inc(free, 1)
                    dve.wait_ge(free, b.is_drained(j))

                def l3_weights():
                    ps, free, b = opened(("l3_full", 0, 0))
                    for a in range(2):
                        last = dve.tensor_tensor(out=l3_full[:, a, :].rearrange("p (h d) -> p h d", d=DH),
                                                 in0=ps[:, a * D:(a + 1) * D].rearrange("p (h d) -> p h d", d=DH),
                                                 in1=head_of[:, :].unsqueeze(2).broadcast_to([P, HEADS, DH]), op=ALU.mult)
                    last.then_inc(free, 1)

                def bias_sums():
                    dve.wait_ge(weights_in, 16 * N_WEIGHTS)
                    link(dve.tensor_copy(up_hi["3"][:, :, :], w_ff1))
                    dve.tensor_tensor(out=up_lo["3"][:, :, :], in0=w_ff1, in1=up_hi["3"][:, :, :].bitcast(f32), op=ALU.subtract)
                    dve.tensor_tensor(out=row("ln_b"), in0=row("ln_b"), in1=late_biases[:, 0, :], op=ALU.add)
                    dve.tensor_tensor(out=row("beta1"), in0=row("beta1"), in1=late_biases[:, 1, :], op=ALU.add).then_inc(vec_consts, 1)

                named = {"l1_wT": l1_weights, "l12_w": l12_weights, "l3_full": l3_weights, "bias_sums": bias_sums,
                         "l3_small_t": lambda: drain(("l3_small_t", 0, 0), w8T[:, :, :],
                                                     lambda ps: ps[0:DH, 0:3 * DH].rearrange("p (a n) -> p a n", n=DH)),
                         "l3_b": lambda: drain(("l3_b", 0, 0), b8[:, :], lambda ps: ps[0:DH, 0:DH]),
                         "l3_rep": lambda: drain(("l3_rep", 0, 0), rep8[:, :, :],
                                                 lambda ps: ps[0:DH, 0:2 * D].rearrange("p (a n) -> p a n", n=D)),
                         "ctx3": context3, "mask": mask, "squares": mean_squares, "ctx1": context1, "xn": input_over_rms,
                         **of_each("xnT", input_T), "fold_k_0": lambda: keys0_lo(0), "fold_k_1": lambda: keys0_lo(1), **drain_T("x1T", xT["1"]), **drain_T("x2T", xT["3"]), **drain_T("a3T", xT["3"]),
                         **of_each("y1T", lambda g: drain_yT("1", "ln_gc", "ln_bc", g)),
                         **of_each("y3T", lambda g: drain_yT("3", "g1c", "beta1c", g)),
                         **of_each("s0", maxima0), **of_each("max0", lambda g: drain_maxT("0", "1", g)), **of_each("sums0", sums0),
                         **of_each("o0", output0), **of_each("q1", queries1), **of_each("s2", maxima2), "rsum2": inverse_sums2,
                         **of_each("o2", output2), **of_each("w3", out3),
                         "norm1": lambda: norm("1", front), "norm3": lambda: norm("3", back), "norm4": lambda: norm("4", back),
                         "stats1": lambda: statistics("1"), "stats3": lambda: statistics("3"), "stats4": lambda: statistics("4")}
                for l in "13":
                    named.update(of_each("s" + l, lambda g, l=l: maxima(l, g)))
                    named.update(of_each("max" + l, lambda g, l=l: drain_maxT(l, l, g)))
                    named.update(of_each("at" + l, lambda g, l=l: attention(l, g)))
                    named.update(of_each("f" + l, lambda g, l=l: feed_forward_out(l, g)))
                return named

            vec_counts = []
            sections(dve, "vector", stages)
            assert vec_counts[1][0] == VEC_STEPS, vec_counts

        @block.tensor
        def _(pe):
            mm = nc.tensor.matmul

            def open_pro(key):
                b = pro[key]
                if b.drains:
                    pe.wait_ge(drained[b.region], b.is_free())
                return psum[b.region], written[b.region]

            def pro_ready(key):
                b = pro[key]
                pe.wait_ge(drained[b.region], b.is_drained())

            pe.wait_ge(pool_consts, 2)
            pe.wait_ge(keys_in, 3 * 16)

            def transposes(key, src):
                ps, full = open_pro(key)
                for c, s in enumerate(src):
                    last = nc.tensor.transpose(ps[:, c * P:(c + 1) * P], s, ident[:, :])
                last.then_inc(full, 1)

            transposes(("wkT", 0, 0), [wk0[:, c * P:(c + 1) * P] for c in range(PAIRS)])
            pe.wait_ge(wq_scaled, 1)
            transposes(("wqT", 0, 0), [wq0[:, c * P:(c + 1) * P] for c in range(PAIRS)])
            pro_ready(("wkT", 0, 0))
            pro_ready(("wqT", 0, 0))
            for part in range(2):
                ps, full = open_pro(("wqk", 0, part))
                for n in range(8):
                    h = 8 * part + n
                    r = slice((h % 2) * DKV, (h % 2 + 1) * DKV)
                    at = (h % 2) * 4 + n // 2
                    last = mm(ps[:, at * P:(at + 1) * P], wkT[r, h // 2, :], wqT[r, h // 2, :], start=True, stop=True)
                last.then_inc(full, 1)
            pe.wait_ge(pool_consts, 5)
            pe.wait_ge(vec_consts, 1)
            pro_ready(("wqk", 0, 1))

            def stages(at, j, front, back):
                def open_(key):
                    b = at[key]
                    pe.wait_ge(drained[b.region], b.is_free(j))
                    return psum[b.region], written[b.region]

                def ready(key):
                    b = at[key]
                    pe.wait_ge(drained[b.region], b.is_drained(j))

                def transpose_tiles(key, src):
                    ps, full = open_(key)
                    for t in TS:
                        last = nc.tensor.transpose(ps[:, t * P:(t + 1) * P], src(t), ident[:, :])
                    last.then_inc(full, 1)

                def tiles_times(name, after, lhs, rhs, g):
                    ready((after, g, 0))
                    ps, full = open_((name, g, 0))
                    for t in TS:
                        last = mm(ps[:, t * D:(t + 1) * D], lhs[:, g, t * P:(t + 1) * P], rhs, start=True, stop=True)
                    last.then_inc(full, 1)

                def transposes_of(key, src):
                    ps, full = open_(key)
                    for c, w in enumerate(src):
                        last = nc.tensor.transpose(ps[:, c * P:(c + 1) * P], w, ident[:, :])
                    last.then_inc(full, 1)

                def values_weights_T():
                    pe.wait_ge(values_in, 2 * 16)
                    transposes_of(("wvT", 0, 0), [wv0[:, c * P:(c + 1) * P] for c in range(PAIRS)])

                def fold_values_weights(part):
                    ready(("wvT", 0, 0))
                    ps, full = open_(("wvo", 0, part))
                    r = slice(part * DKV, (part + 1) * DKV)
                    for c in range(PAIRS):
                        last = mm(ps[:, c * D:(c + 1) * D], wvT[r, c, :], wo0[r, c, :], start=True, stop=True)
                    last.then_inc(full, 1)

                def l1_weights_T():
                    pe.wait_ge(weights_in, 16 * N_WEIGHTS)
                    transposes_of(("l1_wT", 0, 0), [wq1, wk1, wv1] + [w1_1[:, c, :] for c in range(CHUNKS_FF)])

                def l12_weights():
                    ps, full = open_(("l12_w", 0, 0))
                    for c in range(CHUNKS_FF):
                        nc.tensor.transpose(ps[:, c * P:(c + 1) * P], w2_1[:, c * P:(c + 1) * P], ident[:, :])
                    nc.tensor.transpose(ps[:, FF:FF + D], wv2, ident[:, :])
                    mm(ps[:, FF + D:FF + 2 * D], wk2, wq2, start=True, stop=True)
                    mm(ps[:, FF + 2 * D:FF + 2 * D + 1], wq2, col("bk2"), start=True, stop=True)
                    mm(ps[:, FF + 2 * D + 1:FF + 2 * D + 2], wk2, col("bq2"), start=True, stop=True)
                    mm(ps[0:1, FF + 2 * D + 2:FF + 2 * D + 3], col("bq2"), col("bk2"), start=True, stop=True).then_inc(full, 1)

                def l3_small_T():
                    pe.wait_ge(weights_in, 16 * N_WEIGHTS)
                    ps, full = open_(("l3_small_t", 0, 0))
                    for a in range(3):
                        last = mm(ps[0:DH, a * DH:(a + 1) * DH], w8[:, a, :], ident[0:DH, 0:DH], start=True, stop=True)
                    last.then_inc(full, 1)

                def l3_wq_wk():
                    ready(("l3_small_t", 0, 0))
                    ps, full = open_(("l3_b", 0, 0))
                    mm(ps[0:DH, 0:DH], w8T[:, 1, :], w8T[:, 0, :], start=True, stop=True).then_inc(full, 1)

                def l3_repeat_columns():
                    ready(("l3_b", 0, 0))
                    ps, full = open_(("l3_rep", 0, 0))
                    mm(ps[0:DH, 0:D], b8[:, :], rep_id[:, :, :], start=True, stop=True)
                    mm(ps[0:DH, D:2 * D], w8T[:, 2, :], rep_id[:, :, :], start=True, stop=True).then_inc(full, 1)

                def l3_repeat_rows():
                    ready(("l3_rep", 0, 0))
                    ps, full = open_(("l3_full", 0, 0))
                    mm(ps[:, 0:2 * D], rep_id[:, :, :].rearrange("p h d -> p (h d)"), rep8[:, :, :], start=True, stop=True).then_inc(full, 1)

                def values_of_context(l, w, ps):
                    for g in SEQS:
                        for half in range(2):
                            last = mm(ps[half * KL:(half + 1) * KL, g * KL:(g + 1) * KL], ctxT[:, g * KL:(g + 1) * KL],
                                      w.rearrange("p (c a d) -> p c a d", a=2, d=DH)[:, :, half, :], start=True, stop=True)
                    return last

                def stack_keys(l, i):
                    pe.wait_ge(k_rows_ready[l], i + 1)
                    ps, full = open_(("stack_k" + l, 0, 0))
                    for s in range(STACKS):
                        last = nc.tensor.transpose(ps[:, s * P:(s + 1) * P], k_rows[l][:, s, :, :].rearrange("p a r -> p (a r)"), ident[:, :])
                    last.then_inc(full, 1)

                def context3():
                    if back is None:
                        ready(("l12_w", 0, 0))
                        ready(("l3_full", 0, 0))
                    ps, full = open_(("ctx_k3", 0, 0))
                    mm(ps[:, 0:D], ctxT[:, :], l3_full[:, 0, :], start=True, stop=True)
                    mm(ps[:, D:2 * D], wqk2[:, :], ctxT[:, :], start=True, stop=True)
                    mm(ps[0:1, 2 * D:3 * D], c2[:, 1:2], ctxT[:, :], start=True, stop=True).then_inc(full, 1)
                    ps, full = open_(("ctx_v3", 0, 0))
                    values_of_context("3", l3_full[:, 1, :], ps)
                    for g in SEQS:
                        for half in range(2):
                            last = mm(ps[half * KL:(half + 1) * KL, P + g * D:P + (g + 1) * D], ctxT[:, g * KL:(g + 1) * KL],
                                      wv2T[:, :], start=True, stop=True)
                    last.then_inc(full, 1)

                def context_T():
                    pe.wait_ge(c_loaded, 32 * (front + 1))
                    b = at[("ctxT", 0, 0)]
                    ps, full = open_(("ctxT", 0, 0))
                    nc.tensor.transpose(ps[:, 0:P], c_in[:, :], ident[:, :]).then_inc(full, 1)
                    pe.wait_ge(full, b.is_written(j))
                    pe.sem_inc(ctx_read, 1)
                    ready(("ctxT", 0, 0))

                def keys0(half):
                    ps, full = open_(("fold_k", 0, half))
                    for n in range(8):
                        last = mm(ps[:, n * P:(n + 1) * P], wqk[:, 8 * half + n, :], ctxT[:, :], start=True, stop=True)
                    last.then_inc(full, 1)

                def context1():
                    if back is None:
                        ready(("l1_wT", 0, 0))
                    ps, full = open_(("ctx_k1", 0, 0))
                    mm(ps[:, 0:D], ctxT[:, :], l1_wT[:, 1, :], start=True, stop=True).then_inc(full, 1)
                    ps, full = open_(("ctx_v1", 0, 0))
                    values_of_context("1", l1_wT[:, 2, :], ps).then_inc(full, 1)

                def values0(g):
                    if back is None:
                        ready(("wvo", 0, 1))
                    ps, full = open_(("fold_v", g, 0))
                    for c in range(0, PAIRS, 4):
                        for half in range(2):
                            last = mm(ps[half * KL:(half + 1) * KL, c * D:(c + 4) * D], ctxT[:, g * KL:(g + 1) * KL],
                                      wvo[:, half, c:c + 4, :], start=True, stop=True)
                    last.then_inc(full, 1)

                def transpose_maxima(l, buf, g, i):
                    pe.wait_ge(nmax_ready[l], i * G + g + 1)
                    ps, full = open_(("max" + l, g, 0))
                    for t in TS:
                        last = nc.tensor.transpose(ps[0:2 * HEADS, t * P:(t + 1) * P],
                                                   nmax_hl[buf][:, g, t, :, :].rearrange("p a h -> p (a h)"), ident[:, :])
                    last.then_inc(full, 1)

                def three_products(out, lhs, rhs):
                    for n, (a, b) in enumerate(((0, 0), (0, 1), (1, 0))):
                        last = mm(out, lhs[a], rhs[b], start=(n == 0), stop=(n == 2))
                    return last

                def scores0(g):
                    ready(("fold_k", 0, 1))
                    ready(("xnT", g, 0))
                    for t in TS:
                        ps, full = open_(("s0", g, t))
                        for c in range(0, HEADS, 8):
                            rows_of = slice(t * P, (t + 1) * P)
                            last = three_products(ps[:, c * KL:(c + 8) * KL],
                                                  (xn_hi[:, g, rows_of], xn_lo[:, g, rows_of]),
                                                  (fold_k[:, g, c:c + 8, :], fold_k_lo[:, g, c:c + 8, :]))
                        last.then_inc(full, 1)

                def less_max0(g):
                    ready(("max0", g, 0))
                    for t in TS:
                        b = at[("sub0", g, t)]
                        for c in range(0, HEADS, 8):
                            last = mm(psum[b.region][:, c * KL:(c + 8) * KL], nmaxT["1"][:, g, t * P:(t + 1) * P], spread[:, c:c + 8, :],
                                      start=False, stop=True, skip_group_check=True)
                        last.then_inc(written[b.region], 1)

                def probabilities_T(g):
                    for t in TS:
                        if t == 0:
                            pe.wait_ge(norm_vec, front * G + g + 1)
                        else:
                            pe.wait_ge(norm_pool, front * G + g + 1)
                        ps, full = open_(("p0T", g, t))
                        for c in range(PAIRS):
                            last = nc.tensor.transpose(ps[:, c * P:(c + 1) * P], prob[:, g, t, c * P:(c + 1) * P], ident[:, :])
                        last.then_inc(full, 1)

                def output0(g):
                    ready(("p0T", g, 1))
                    ready(("fold_v", g, 0))
                    ps, full = open_(("o0", g, 0))
                    for t in TS:
                        for c in range(PAIRS):
                            last = mm(ps[:, t * D:(t + 1) * D], probT["1"][:, g, c, t * P:(t + 1) * P], fold_v[:, g, c, :],
                                      start=(c == 0), stop=(c == PAIRS - 1))
                    last.then_inc(full, 1)

                def stack_queries(l, i, g):
                    pe.wait_ge(q_rows_ready[l], i * G + g + 1)
                    ps, full = open_(("q%sT" % l, g, 0))
                    for s in range(STACKS):
                        for t in TS:
                            last = nc.tensor.transpose(ps[:, s * QL + t * P:s * QL + (t + 1) * P],
                                                       q_rows[l][:, g, t, s, :, :].rearrange("p a r -> p (a r)"), ident[:, :])
                    last.then_inc(full, 1)

                def scores(l, i, g):
                    ready(("q%sT" % l, g, 0))
                    pe.wait_ge(k_blocks_ready[l], i * G + g + 1)
                    for t in TS:
                        ps, full = open_(("s" + l, g, t))
                        fill = l == "1" and t == 0
                        for bank in range(2):
                            if fill:
                                mm(ps[:, bank * 512:(bank + 1) * 512], ident_bf[0:KL, :],
                                   causal[:, 0, :].unsqueeze(1).broadcast_to([KL, 8, KL]), start=True, stop=False,
                                   skip_group_check=True)
                            for s in (2 * bank, 2 * bank + 1):
                                last = mm(ps[:, s * QL:(s + 1) * QL], q_stack[l][:, g, s, t * P:(t + 1) * P],
                                          k_blocks[l][:, g, s, :, :], start=(s % 2 == 0 and not fill), stop=True,
                                          skip_group_check=True)
                        last.then_inc(full, 1)

                def scores_T(l, g, half):
                    if half == 0:
                        ready(("max" + l, g, 0))
                    ps, full = open_(("st" + l, g, half))
                    banks = ps[:, :].rearrange("p (b c q) -> p b c q", b=2, q=QL)
                    for c in range(4):
                        pair = 4 * half + c
                        s, a = pair // 2, pair % 2
                        o = ps[:, c * QL:(c + 1) * QL]
                        mm(o, k_blocks[l][:, g, s, 2 * a:2 * a + 2, :], q_stack[l][:, g, s, :], start=(c % 2 == 0), stop=False,
                           skip_group_check=True)
                        if l == "1" and c % 2 == 0:
                            mm(banks[:, c // 2, :, 0:KL], causal[:, :, :],
                               ident_bf[0:KL, 0:KL].unsqueeze(1).broadcast_to([KL, 2, KL]), start=False, stop=False,
                               skip_group_check=True)
                        last = mm(o, spread[:, 2 * pair:2 * pair + 2, :], nmaxT[l][:, g, :], start=False, stop=True,
                                  skip_group_check=True)
                    last.then_inc(full, 1)

                def values(l, g):
                    ready(("st" + l, g, 0))
                    ready(("st" + l, g, 1))
                    ps, full = open_(("pv" + l, g, 0))
                    for half in range(2):
                        for c in range(4):
                            last = mm(ps[32 * c:32 * c + 32, half * QL:(half + 1) * QL], v_blocks[l][:, g, 4 * half + c, :],
                                      probT[l][:, g, 4 * half + c, :], start=True, stop=True)
                    last.then_inc(full, 1)

                def attention(l, g):
                    ready(("pv" + l, g, 0))
                    ps, full = open_(("at" + l, g, 0))
                    for t in TS:
                        for half in range(2):
                            last = nc.tensor.transpose(ps[:, (t * 2 + half) * P:(t * 2 + half + 1) * P],
                                                       attT[:, g, half, t * P:(t + 1) * P], ident[:, :])
                    last.then_inc(full, 1)

                def x_T(name, src, is_ready, i, g):
                    pe.wait_ge(is_ready, i * G + g + 1)
                    transpose_tiles((name, g, 0), lambda t: src[:, g, t, :])

                def y_T(l, i, g):
                    pe.wait_ge(z_ready[l], i + 1)
                    transpose_tiles(("y%sT" % l, g, 0), lambda t: z[l][:, g * TILES + t, :])

                def hidden(l, g):
                    pe.wait_ge(y_ready[l], back * G + g + 1)
                    ps, full = open_(("h" + l, g, 0))
                    for c in range(CHUNKS_FF):
                        last = three_products(ps[:, c * QL:(c + 1) * QL], (up_hi[l][:, c, :], up_lo[l][:, c, :]),
                                              (y_hi[:, g, :], y_lo[:, g, :]))
                    last.then_inc(full, 1)

                def down(l, w, g):
                    ready(("h" + l, g, 0))
                    ps, full = open_(("f" + l, g, 0))
                    for t in TS:
                        for c in range(CHUNKS_FF):
                            last = mm(ps[:, t * D:(t + 1) * D], hT[:, g, c, t * P:(t + 1) * P], w[:, c, :],
                                      start=(c == 0), stop=(c == CHUNKS_FF - 1))
                    last.then_inc(full, 1)

                def scores2(g):
                    ready(("x2T", g, 0))
                    ps, full = open_(("s2", g, 0))
                    mm(ps[:, 0:TILES * KL], ones_row[0:1, :],
                       s2_row[0:1, g * KL:(g + 1) * KL].unsqueeze(1).broadcast_to([1, TILES, KL]), start=True, stop=False,
                       skip_group_check=True)
                    for t in TS:
                        last = mm(ps[:, t * KL:(t + 1) * KL], xT["3"][:, g, t * P:(t + 1) * P], fold2[:, g * KL:(g + 1) * KL],
                                  start=False, stop=True, skip_group_check=True)
                    last.then_inc(full, 1)

                def prob2_T(g):
                    ready(("s2", g, 0))
                    ps, full = open_(("p2T", g, 0))
                    nc.tensor.transpose(ps[:, 0:P], prob2[:, g, :, :].rearrange("p t k -> p (t k)"), ident[:, :]).then_inc(full, 1)

                def output2(g):
                    ready(("p2T", g, 0))
                    ps, full = open_(("o2", g, 0))
                    for t in TS:
                        last = mm(ps[:, t * 512:t * 512 + D], prob2T[t * KL:(t + 1) * KL, g, :], v2[t * KL:(t + 1) * KL, g, :],
                                  start=True, stop=True)
                    last.then_inc(full, 1)

                def input_T(g):
                    pe.wait_ge(xn_ready, front * G + g + 1)
                    transpose_tiles(("xnT", g, 0), lambda t: xn[:, g, t, :])

                named = {"wvT": values_weights_T, "wvo_0": lambda: fold_values_weights(0), "wvo_1": lambda: fold_values_weights(1),
                         "l1_wT": l1_weights_T, "l12_w": l12_weights, "l3_small_t": l3_small_T, "l3_b": l3_wq_wk,
                         "l3_rep": l3_repeat_columns, "l3_full": l3_repeat_rows,
                         "ctx3": context3, "stack_k3": lambda: stack_keys("3", front), "ctxT": context_T,
                         "fold_k_0": lambda: keys0(0), "fold_k_1": lambda: keys0(1), "ctx1": context1,
                         "stack_k1": lambda: stack_keys("1", front), **of_each("fold_v", values0), **of_each("xnT", input_T),
                         **of_each("s0", scores0), **of_each("max0", lambda g: transpose_maxima("0", "1", g, front)),
                         **of_each("sub0", less_max0), **of_each("p0T", probabilities_T), **of_each("o0", output0),
                         **of_each("x1T", lambda g: x_T("x1T", x1, x1_ready, front, g)),
                         **of_each("q1", lambda g: tiles_times("q1", "x1T", xT["1"], l1_wT[:, 0, :], g)),
                         **of_each("h1", lambda g: hidden("1", g)), **of_each("f1", lambda g: down("1", w2T, g)),
                         **of_each("x2T", lambda g: x_T("x2T", x2, x2_ready, back, g)),
                         **of_each("s2", scores2), **of_each("p2T", prob2_T), **of_each("o2", output2),
                         **of_each("a3T", lambda g: x_T("a3T", att["3"], att_ready, back, g)),
                         **of_each("w3", lambda g: tiles_times("w3", "a3T", xT["3"], w_out[:, :], g)),
                         **of_each("h3", lambda g: hidden("3", g)),
                         **of_each("f3", lambda g: down("3", w_ff2, g))}
                for l, i in (("1", front), ("3", back)):
                    named.update(of_each("q%sT" % l, lambda g, l=l, i=i: stack_queries(l, i, g)))
                    named.update(of_each("s" + l, lambda g, l=l, i=i: scores(l, i, g)))
                    named.update(of_each("max" + l, lambda g, l=l, i=i: transpose_maxima(l, l, g, i)))
                    named.update(of_each("pv" + l, lambda g, l=l: values(l, g)))
                    named.update(of_each("at" + l, lambda g, l=l: attention(l, g)))
                    named.update(of_each("y%sT" % l, lambda g, l=l: y_T(l, back, g)))
                    for half in range(2):
                        for g in SEQS:
                            named["st%s_%d%d" % (l, g, half)] = lambda l=l, g=g, half=half: scores_T(l, g, half)
                return named

            sections(pe, "tensor", stages)


INPUTS = ["x", "ctx_1024", "mask_Bx1x1xS2_if1",
          "L0_xattn_wq", "L0_xattn_wk", "L0_xattn_wv", "L0_xattn_wo", "L0_xattn_norm_w",
          "L1_xattn_Wq", "L1_xattn_bq", "L1_xattn_Wk", "L1_xattn_bk", "L1_xattn_Wv", "L1_xattn_bv",
          "L1_xattn_W1", "L1_xattn_b1", "L1_xattn_W2", "L1_xattn_b2", "L1_xattn_ln_g", "L1_xattn_ln_b",
          "L2_xattn_Wq", "L2_xattn_bq", "L2_xattn_Wk", "L2_xattn_bk", "L2_xattn_Wv", "L2_xattn_bv",
          "L3_xattn_wv", "L3_xattn_wk", "L3_xattn_wq", "L3_xattn_w_out", "L3_xattn_b_out", "L3_xattn_g1",
          "L3_xattn_beta1", "L3_xattn_w_ff1", "L3_xattn_b_ff1", "L3_xattn_w_ff2", "L3_xattn_b_ff2",
          "L3_xattn_g2", "L3_xattn_beta2"]


def kernel(**inputs):
    import numpy as np
    import concourse.bacc as bacc
    from concourse.bass_utils import run_bass_kernel_spmd

    nc = bacc.Bacc("TRN2", target_bir_lowering=False, num_devices=1)
    arrays = {name: np.ascontiguousarray(inputs[name]) for name in INPUTS}
    aps = {name: nc.dram_tensor(name, a.shape, mybir.dt.from_np(a.dtype), kind="ExternalInput").ap()
           for name, a in arrays.items()}
    out = nc.dram_tensor("out", (BATCH, QL, D), mybir.dt.float32, kind="ExternalOutput").ap()
    build(nc, aps, out)
    r = run_bass_kernel_spmd(nc, [arrays], core_ids=[0])
    return r.results[0]["out"]
```
